# Optimizing a Trainium2 kernel written in Bass

```python
import numpy as np
import jax
import jax.numpy as jnp

def _softmax(x, axis=-1):
    return jax.nn.softmax(x, axis=axis)

def _gelu(x):
    return jax.nn.gelu(x, approximate=True)

def _silu(x):
    return jax.nn.silu(x)

def _sigmoid(x):
    return jax.nn.sigmoid(x)

def _layernorm(x, axis=-1, eps=1e-05):
    m = jnp.mean(x, axis=axis, keepdims=True)
    v = jnp.var(x, axis=axis, keepdims=True)
    return (x - m) / jnp.sqrt(v + eps)

def _scatter_add(tgt, idx, src, axis=0):
    return tgt.at[idx].add(src)

def _segment_sum(src, seg, n):
    return jax.ops.segment_sum(src, seg, n)
kernel_name = 'mk_prb_d1_jaxref_r4_d9e15b'

def setup_inputs(seed: int=0):
    np.random.seed(seed)
    _w = jnp.asarray

    def _L0_attn_setup():
        import jax, jax.numpy as jnp
        import numpy as np
        MODEL_DIM = 256
        HEADS = 16
        HEAD_DIM = MODEL_DIM // HEADS
        B, T = (2, 512)
        TB_LEN = 125
        key = jax.random.key(seed)
        ks = jax.random.split(key, 12)
        s = 0.02
        d = MODEL_DIM
        return {'x': jax.random.normal(ks[0], (B, T, d), dtype=jnp.float32), 'Wq': jax.random.normal(ks[1], (d, d), dtype=jnp.float32) * s, 'bq': jnp.zeros((d,), jnp.float32), 'Wk': jax.random.normal(ks[2], (d, d), dtype=jnp.float32) * s, 'bk': jnp.zeros((d,), jnp.float32), 'Wv': jax.random.normal(ks[3], (d, d), dtype=jnp.float32) * s, 'bv': jnp.zeros((d,), jnp.float32), 'Wo': jax.random.normal(ks[4], (d, d), dtype=jnp.float32) * s, 'bo': jnp.zeros((d,), jnp.float32), 'et_gate': jax.random.normal(ks[5], (1, 1, 1), dtype=jnp.float32), 'is_gate': jax.random.normal(ks[6], (1, 1, 1), dtype=jnp.float32), 'time_bias': jnp.linspace(-1.0, 1.0, TB_LEN, dtype=jnp.float32).reshape(1, 1, TB_LEN)}
    _L0_attn_in = _L0_attn_setup()

    def _L0_ffn_setup():
        import jax, jax.numpy as jnp
        import numpy as np
        TOP_K = 2
        key = jax.random.key(seed)
        k0, k1, k2, k3, k4 = jax.random.split(key, 5)
        B, S, H, I, E = (4, 512, 256, 704, 8)
        s_h = 1.0 / np.sqrt(H)
        s_i = 1.0 / np.sqrt(I)
        return {'x': jax.random.normal(k0, (B, S, H), jnp.float32), 'w_router': jax.random.normal(k1, (E, H), jnp.float32) * s_h, 'w_gate': jax.random.normal(k2, (E, I, H), jnp.float32) * s_h, 'w_up': jax.random.normal(k3, (E, I, H), jnp.float32) * s_h, 'w_down': jax.random.normal(k4, (E, H, I), jnp.float32) * s_i}
    _L0_ffn_in = _L0_ffn_setup()
    _d = {'L0_attn_x': _L0_attn_in['x'], 'L0_attn_Wq': _L0_attn_in['Wq'], 'L0_attn_bq': _L0_attn_in['bq'], 'L0_attn_Wk': _L0_attn_in['Wk'], 'L0_attn_bk': _L0_attn_in['bk'], 'L0_attn_Wv': _L0_attn_in['Wv'], 'L0_attn_bv': _L0_attn_in['bv'], 'L0_attn_Wo': _L0_attn_in['Wo'], 'L0_attn_bo': _L0_attn_in['bo'], 'L0_attn_et_gate': _L0_attn_in['et_gate'], 'L0_attn_is_gate': _L0_attn_in['is_gate'], 'L0_attn_time_bias': _L0_attn_in['time_bias'], 'L0_ffn_w_router': _L0_ffn_in['w_router'], 'L0_ffn_w_gate': _L0_ffn_in['w_gate'], 'L0_ffn_w_up': _L0_ffn_in['w_up'], 'L0_ffn_w_down': _L0_ffn_in['w_down']}
    _x0 = _d['L0_attn_x']
    _d['L0_attn_x'] = jax.random.normal(jax.random.fold_in(jax.random.key(seed), 1), (4, 1024, 256), dtype=_x0.dtype)
    del _x0
    return _d

def reference(L0_attn_x, L0_attn_Wq, L0_attn_bq, L0_attn_Wk, L0_attn_bk, L0_attn_Wv, L0_attn_bv, L0_attn_Wo, L0_attn_bo, L0_attn_et_gate, L0_attn_is_gate, L0_attn_time_bias, L0_ffn_w_router, L0_ffn_w_gate, L0_ffn_w_up, L0_ffn_w_down):

    def _L0_attn_ref(x, Wq, bq, Wk, bk, Wv, bv, Wo, bo, et_gate, is_gate, time_bias):
        import jax, jax.numpy as jnp
        import numpy as np
        MODEL_DIM = 256
        HEADS = 16
        HEAD_DIM = MODEL_DIM // HEADS
        B, T = (2, 512)
        TB_LEN = 125
        Bb, Tt, D = x.shape
        H, hd = (HEADS, HEAD_DIM)
        Q = (x @ Wq.T + bq).reshape(Bb, Tt, H, hd).transpose(0, 2, 1, 3)
        K = (x @ Wk.T + bk).reshape(Bb, Tt, H, hd).transpose(0, 2, 1, 3)
        V = (x @ Wv.T + bv).reshape(Bb, Tt, H, hd).transpose(0, 2, 1, 3)
        scores = jnp.einsum('bhqd,bhkd->bhqk', Q, K) / jnp.sqrt(jnp.float32(hd))
        pos = jnp.arange(Tt)[None, :] - jnp.arange(Tt)[:, None]
        idx = jnp.clip(pos + TB_LEN // 2, 0, TB_LEN - 1)
        tp = time_bias[:, :, idx]
        tp = jnp.squeeze(tp, axis=1)[None, None]
        scores = scores + jax.nn.sigmoid(et_gate) * tp + is_gate
        attn = jax.nn.softmax(scores, axis=-1)
        context = jnp.matmul(attn, V)
        context = context.transpose(0, 2, 1, 3, 4).reshape(Bb, Tt, D)
        return context @ Wo.T + bo

    def _L0_ffn_ref(x, w_router, w_gate, w_up, w_down):
        import jax, jax.numpy as jnp
        import numpy as np
        TOP_K = 2
        B, S, H = x.shape
        E = w_router.shape[0]
        xf = x.reshape(-1, H)
        logits = jnp.einsum('th,eh->te', xf, w_router)
        probs = jax.nn.softmax(logits, axis=-1)
        topw, topi = jax.lax.top_k(probs, TOP_K)
        topw = topw / jnp.sum(topw, axis=-1, keepdims=True)
        onehot = (topi[..., None] == jnp.arange(E)).astype(x.dtype)
        combine = jnp.einsum('tk,tke->te', topw, onehot)
        gate = jax.nn.silu(jnp.einsum('th,eih->eti', xf, w_gate))
        up = jnp.einsum('th,eih->eti', xf, w_up)
        down = jnp.einsum('eti,ehi->eth', gate * up, w_down)
        out = jnp.einsum('eth,te->th', down, combine)
        return out.reshape(B, S, H)
    x = L0_attn_x
    xn = _layernorm(x, axis=-1)
    x = x + _L0_attn_ref(xn, L0_attn_Wq, L0_attn_bq, L0_attn_Wk, L0_attn_bk, L0_attn_Wv, L0_attn_bv, L0_attn_Wo, L0_attn_bo, L0_attn_et_gate, L0_attn_is_gate, L0_attn_time_bias) + _L0_ffn_ref(xn, L0_ffn_w_router, L0_ffn_w_gate, L0_ffn_w_up, L0_ffn_w_down)
    return x

_drawn_inputs = setup_inputs


def setup_inputs(seed=0):
    import zlib

    import numpy as np

    out = dict(_drawn_inputs(seed))
    spreads = {'L0_attn_bq': (0.0, 0.8),
     'L0_attn_bk': (0.0, 0.8),
     'L0_attn_bv': (0.0, 0.289),
     'L0_attn_bo': (0.0, 0.1)}
    factors = {'L0_attn_Wq': 8.0, 'L0_attn_Wk': 8.0, 'L0_attn_Wv': 8.0, 'L0_attn_time_bias': 8.0}
    for name, (base, spread) in spreads.items():
        noise = np.random.default_rng([zlib.crc32(name.encode()), seed]).standard_normal(out[name].shape)
        drawn = base * np.exp(spread * noise) if base else spread * noise
        out[name] = jnp.asarray(drawn.astype(out[name].dtype))
    for name, factor in factors.items():
        out[name] = (out[name] * factor).astype(out[name].dtype)
    return out
```

```python
from contextlib import ExitStack

import numpy as np
import concourse.bass as bass
import concourse.mybir as mybir

FP32 = mybir.dt.float32
FP32R = mybir.dt.float32r
BF16 = mybir.dt.bfloat16
I32 = mybir.dt.int32
U32 = mybir.dt.uint32
ALU = mybir.AluOpType
ACT = mybir.ActivationFunctionType
AX = mybir.AxisListType

P = 128
B, T, D = 4, 1024, 256
H, HD = 16, 16
NTOK = B * T
NT = NTOK // P
E, I, TOPK = 8, 704, 2
TB = 125
REACH = TB // 2
KT = D // P
EPS = 1e-5

HU = 4
GU = H // HU
NU = B * GU
QT = T // P
HALF = 512
VW = 32
NPAIR = 6
QPART = [0, 0, 0, 1, 1, 2]
KPART = [0, 1, 2, 0, 1, 0]
ROW_FAR = NPAIR * HD
ROW_MAX = ROW_FAR + 3 * QT
ROWS = ROW_MAX + 3
NBUF = 3
MAXIMA = HU * QT * 2
STEPS = 2 * QT
SCALE_INV = 4.0

NTILE = 72
NPOS = NTILE * P
IC = 352
NI = (I + P - 1) // P
GUW = 2 * I
TBLEN = 384


def linker(engine, done, base=0):
    count = [0]

    def link(ins):
        count[0] += 1
        ins.then_inc(done, 1)
        engine.wait_ge(done, base + count[0])

    return link, count


def phase_project(nc, io, mem, sem):
    with ExitStack() as ctx:
        sb = lambda n, s, d: ctx.enter_context(nc.sbuf_tensor(n, s, d))
        ps = lambda n, s, d=FP32: ctx.enter_context(nc.psum_tensor(n, s, d))
        xbuf = sb("xbuf", [P, 2, 4, D], FP32)
        xns = sb("xns", [P, 2, 4, D], FP32)
        stats = sb("stats", [P, 2, 4, 6], FP32)
        both = sb("both_stats", [P, 2, 4, 2], FP32)
        diff = sb("diff", [P, 2, 4], FP32)
        diff2 = sb("diff2", [P, 2, 4], FP32)
        mean = sb("mean", [P, 2, 4], FP32)
        var = sb("var", [P, 2, 4], FP32)
        vareps = sb("vareps", [P, 2, 4], FP32)
        std = sb("std", [P, 2, 4], FP32)
        rstd = sb("rstd", [P, 2, 4], FP32)
        xhi = sb("xhi", [P, 2, KT, HALF], FP32R)
        xlo = sb("xlo", [P, 2, KT, HALF], FP32R)
        wqk = sb("wqk", [P, KT, 2 * D], FP32)
        wqk_hi = sb("wqk_hi", [P, KT, 2 * D], FP32R)
        wqk_lo = sb("wqk_lo", [P, KT, 2 * D], FP32R)
        wvr = sb("wvr", [P, KT, D + E], FP32)
        wvr_hi = sb("wvr_hi", [P, KT, D + E], FP32R)
        wvr_lo = sb("wvr_lo", [P, KT, D + E], FP32R)
        bqk = sb("bqk", [P, 4], FP32)
        bv = sb("bv", [P, D], FP32)
        q32 = sb("q32", [P, 4, HALF], FP32)
        rest = sb("rest", [P, 4, HALF], FP32)
        parts = sb("parts", [P, 4, 3, HALF], BF16)
        vpad = sb("vpad", [P, 2, 4, H, VW], FP32)
        tr = ps("tr", [P, KT, HALF])
        qk = ps("qk", [P, 2, HALF])
        vr = ps("vr", [P, 2, HALF])
        block = ctx.enter_context(nc.Block())
        NC = NTOK // HALF

        @block.sync
        def _(sp):
            sp.dma_start(wqk[:], io["w_qk"]).then_inc(sem["weights"], 16)
            sp.dma_start(wvr[:], io["w_vr"]).then_inc(sem["weights"], 16)
            sp.dma_start(bqk[:], io["b_qk"]).then_inc(sem["weights"], 16)
            sp.dma_start(bv[:], io["b_v"].partition_broadcast(P)).then_inc(sem["weights"], 16)
            sp.dma_start(mem["ident"][:], io["ident"]).then_inc(sem["weights"], 16)
            x4 = io["x"].rearrange("(c a p) d -> c p a d", a=4, p=P)

            def load(c, s):
                sp.dma_start(xbuf[:, s], x4[bass.ds(c, 1)].rearrange("c p a d -> (c p) a d"))\
                    .then_inc(sem["x_loaded"][s], 16)

            def store(it, s, more):
                c = it * 2 + s
                sp.wait_ge(sem["xn_ready"], c + (2 + 1))
                if more:
                    load(it * 2 + (2 + s), s)
                sp.dma_start(mem["xn"][:, bass.ds(c * 4, 4), :], xns[:, s]).then_inc(sem["xn_stored"][s], 16)
                for m in range(4):
                    sp.wait_ge(sem["lo_ready"], it * 8 + (4 + 4 * s + m + 1))
                    for g in range(2):
                        sp.dma_start(mem["qk_dram"][bass.ds(it * GU + (2 * (m % 2) + g), 1), m // 2, :, :,
                                                    HALF * s:HALF * s + HALF]
                                     .rearrange("u c r t -> (u r) c t"),
                                     parts[64 * g:64 * g + 64, m]).then_inc(sem["parts_stored"][m], 16)
                sp.wait_ge(sem["vr_used"], it * 8 + (2 + 4 * s + 4))
                for g in range(GU):
                    sp.dma_start(mem["v_dram"][bass.ds(it * GU + g, 1), :, 4 * s:4 * s + 4, :]
                                 .rearrange("u p a w -> (u p) a w"),
                                 vpad[:, s, :, HU * g:HU * g + HU, :].rearrange("p a h w -> p a (h w)"))\
                        .then_inc(sem["v_stored"][s], 16)

            for s in range(2):
                load(s, s)
            with sp.Fori(0, NC // 2 - 1) as it:
                for s in range(2):
                    store(it, s, True)
            for s in range(2):
                store(NC // 2 - 1, s, False)
            for s in range(2):
                sp.wait_ge(sem["xn_stored"][s], 16 + 16 * NC // 2)
                sp.wait_ge(sem["v_stored"][s], 64 + 64 * NC // 2)
            for m in range(4):
                sp.wait_ge(sem["parts_stored"][m], 32 + 32 * NC)

        @block.gpsimd
        def _(pool):
            with pool.Fori(0, NC // 2) as it:
                for s in range(2):
                    for m in range(4):
                        n = it * 8 + (4 * s + m)
                        pool.wait_ge(sem["mid_ready"], n + 1)
                        nc.gpsimd.tensor_tensor(parts[:, m, 2, :], rest[:, m, :], parts[:, m, 1, :],
                                                ALU.subtract).then_inc(sem["lo_ready"], 1)

        @block.scalar
        def _(act):
            act.wait_ge(sem["weights"], 80)
            nc.scalar.activation(wqk_hi[:], wqk[:], ACT.Copy).then_inc(sem["w_hi"], 1)
            nc.scalar.activation(wvr_hi[:], wvr[:], ACT.Copy).then_inc(sem["w_hi"], 1)

            def root(c, s):
                act.wait_ge(sem["var_ready"], c + 1)
                nc.scalar.activation(std[:, s], vareps[:, s], ACT.Sqrt).then_inc(sem["std_ready"], 1)

            def x_hi(c, s):
                act.wait_ge(sem["tr_ready"], c + 1)
                nc.scalar.activation(xhi[:, s], tr[:], ACT.Copy).then_inc(sem["xhi_ready"], 1)

            def chunk(it, s, next1=True, next2=True):
                c = it * 2 + s

                def middle(m):
                    act.wait_ge(sem["rest_ready"], it * 8 + (4 + 4 * s + m + 1))
                    nc.scalar.activation(parts[:, m, 1, :], rest[:, m, :], ACT.Copy)\
                        .then_inc(sem["mid_ready"], 1)

                for m in range(4):
                    n = it * 8 + (4 * s + m)
                    act.wait_ge(sem["qk_ready"], n + 1)
                    act.wait_ge(sem["rest_ready"], n + (4 - 3))
                    act.wait_ge(sem["parts_stored"][m], it * 64 + (32 + 32 * s))
                    nc.scalar.activation(q32[:, m, :], qk[:, m % 2, :], ACT.Identity,
                                         bias=bqk[:, m:m + 1]).then_inc(sem["q32_ready"], 1)
                    act.wait_ge(sem["q32_ready"], n + (2 + 1))
                    nc.scalar.activation(parts[:, m, 0, :], q32[:, m, :], ACT.Copy)\
                        .then_inc(sem["hi_ready"], 1)
                    if m:
                        middle(m - 1)
                    if m == 1 and next1:
                        x_hi(c + 1, 1 - s)
                middle(3)
                if next2:
                    root(c + 2, s)

            root(0, 0)
            root(1, 1)
            x_hi(0, 0)
            with act.Fori(0, NC // 2 - 1) as it:
                for s in range(2):
                    chunk(it, s)
            chunk(NC // 2 - 1, 0, next2=False)
            chunk(NC // 2 - 1, 1, next1=False, next2=False)

        @block.vector
        def _(dve):
            nc.vector.memset(vpad[:], 1.0).then_inc(sem["ones_ready"], 1)
            dve.wait_ge(sem["ones_ready"], 1)
            dve.wait_ge(sem["w_hi"], 2)
            nc.vector.tensor_tensor(wqk_lo[:], wqk[:], wqk_hi[:], ALU.subtract).then_inc(sem["w_lo"], 1)
            nc.vector.tensor_tensor(wvr_lo[:], wvr[:], wvr_hi[:], ALU.subtract).then_inc(sem["w_lo"], 1)

            LINKS = 3

            def statistics(c, s, loaded):
                link, _ = linker(dve, sem["stats_chain"], c * LINKS)
                dve.wait_ge(sem["x_loaded"][s], loaded)
                for a in range(4):
                    last = nc.vector.bn_stats(stats[:, s, a], xbuf[:, s, a])
                link(last)
                even, odd = stats[:, s, :, 1:3], stats[:, s, :, 4:6]
                nc.vector.tensor_tensor(both[:, s], even, odd, ALU.add)
                link(nc.vector.tensor_tensor(diff[:, s], even[:, :, 0], odd[:, :, 0], ALU.subtract))
                nc.vector.tensor_scalar(mean[:, s], both[:, s, :, 0], 0.5, None, ALU.mult)
                nc.vector.tensor_scalar(var[:, s], both[:, s, :, 1], 1.0 / D, EPS, ALU.mult, ALU.add)
                link(nc.vector.scalar_tensor_tensor(out=diff2[:, s], in0=diff[:, s], scalar=0.25,
                                                    in1=diff[:, s], op0=ALU.mult, op1=ALU.mult))
                nc.vector.tensor_tensor(vareps[:, s], var[:, s], diff2[:, s], ALU.add)\
                    .then_inc(sem["var_ready"], 1)

            def normalise(c, s, stored):
                link, _ = linker(dve, sem["root_chain"], c)
                dve.wait_ge(sem["std_ready"], c + 1)
                link(nc.vector.reciprocal(rstd[:, s], std[:, s]))
                dve.wait_ge(sem["xn_stored"][s], stored)
                for a in range(4):
                    last = nc.vector.tensor_scalar(xns[:, s, a], xbuf[:, s, a], mean[:, s, a:a + 1],
                                                   rstd[:, s, a:a + 1], ALU.subtract, ALU.mult)
                last.then_inc(sem["xn_ready"], 1)

            def x_lo(c, s):
                dve.wait_ge(sem["xhi_ready"], c + 1)
                nc.vector.tensor_tensor(xlo[:, s], tr[:], xhi[:, s], ALU.subtract)\
                    .then_inc(sem["xlo_ready"], 1)

            def take_rest(it, s, m):
                n = it * 8 + (4 * s + m)
                dve.wait_ge(sem["hi_ready"], n + 1)
                dve.wait_ge(sem["lo_ready"], n + (4 - 3))
                nc.vector.tensor_tensor(rest[:, m, :], q32[:, m, :], parts[:, m, 0, :],
                                        ALU.subtract).then_inc(sem["rest_ready"], 1)

            def values(it, s, a):
                n = it * 8 + (4 * s + a)
                dve.wait_ge(sem["vr_ready"], n + 1)
                if a == 0:
                    dve.wait_ge(sem["v_stored"][s], it * 64 + 64)
                nc.vector.tensor_tensor(vpad[:, s, a, :, 0:HD],
                                        vr[:, a % 2, 0:D].rearrange("p (h d) -> p h d", h=H),
                                        bv[:].rearrange("p (h d) -> p h d", h=H), ALU.add)
                nc.vector.tensor_scalar(mem["logits"][:, bass.ds(it * 8 + (4 * s + a), 1), :],
                                        vr[:, a % 2:a % 2 + 1, D:D + E], 1.0, None, ALU.mult)\
                    .then_inc(sem["vr_used"], 1)

            def chunk(it, s, next1=True, next2=True):
                c = it * 2 + s
                if next1:
                    normalise(c + 1, 1 - s, it * 16 + 16 * (s + 1))
                take_rest(it, s, 0)
                take_rest(it, s, 1)
                if next1:
                    x_lo(c + 1, 1 - s)
                take_rest(it, s, 2)
                values(it, s, 0)
                take_rest(it, s, 3)
                for a in range(1, 4):
                    values(it, s, a)
                if next2:
                    statistics(c + 2, s, it * 16 + 32)

            statistics(0, 0, 16)
            statistics(1, 1, 16)
            normalise(0, 0, 16)
            x_lo(0, 0)
            with dve.Fori(0, NC // 2 - 1) as it:
                for s in range(2):
                    chunk(it, s)
            chunk(NC // 2 - 1, 0, next2=False)
            chunk(NC // 2 - 1, 1, next1=False, next2=False)

        @block.tensor
        def _(pe):
            for s in range(2):
                pe.sem_inc(sem["xn_stored"][s], 16)
                pe.sem_inc(sem["v_stored"][s], 64)
            pe.sem_inc(sem["xn_ready"], 2)
            for m in range(4):
                pe.sem_inc(sem["parts_stored"][m], 32)
            pe.sem_inc(sem["rest_ready"], 4)
            pe.sem_inc(sem["lo_ready"], 4)
            pe.sem_inc(sem["q32_ready"], 2)
            pe.sem_inc(sem["vr_used"], 2)
            pe.wait_ge(sem["weights"], 80)
            pe.wait_ge(sem["w_lo"], 2)

            def x_T(c, s):
                pe.wait_ge(sem["xn_ready"], c + (2 + 1))
                for a in range(4):
                    for k in range(KT):
                        last = nc.tensor.transpose(tr[:, k, P * a:P * a + P],
                                                   xns[:, s, a, P * k:P * k + P], mem["ident"][:])
                last.then_inc(sem["tr_ready"], 1)

            def chunk(it, s, ahead):
                c = it * 2 + s
                pe.wait_ge(sem["xlo_ready"], c + 1)
                for m in range(4):
                    pe.wait_ge(sem["q32_ready"], it * 8 + (4 * s + m) + (2 - 1))
                    i = 0
                    for k in range(KT):
                        for w, x in ((wqk_hi, xhi), (wqk_hi, xlo), (wqk_lo, xhi)):
                            last = nc.tensor.matmul(qk[:, m % 2, :], w[:, k, P * m:P * m + P], x[:, s, k, :],
                                                    start=(i == 0), stop=(i == 3 * KT - 1))
                            i += 1
                    last.then_inc(sem["qk_ready"], 1)
                    if m == 1 and ahead:
                        x_T(c + 1, 1 - s)
                for a in range(4):
                    pe.wait_ge(sem["vr_used"], it * 8 + (4 * s + a) + (2 - 1))
                    i = 0
                    for k in range(KT):
                        for w, x in ((wvr_hi, xhi), (wvr_hi, xlo), (wvr_lo, xhi)):
                            last = nc.tensor.matmul(vr[:, a % 2, 0:D + E], x[:, s, k, P * a:P * a + P],
                                                    w[:, k, :], start=(i == 0), stop=(i == 3 * KT - 1))
                            i += 1
                    last.then_inc(sem["vr_ready"], 1)

            x_T(0, 0)
            with pe.Fori(0, NC // 2 - 1) as it:
                for s in range(2):
                    chunk(it, s, True)
            chunk(NC // 2 - 1, 0, True)
            chunk(NC // 2 - 1, 1, False)


def split3(nc, link, src, hi, mid, lo, rest):
    link(nc.vector.tensor_copy(hi, src))
    link(nc.vector.tensor_tensor(rest, src, hi, ALU.subtract))
    link(nc.vector.tensor_copy(mid, rest))
    link(nc.vector.tensor_tensor(lo, rest, mid, ALU.subtract))


def phase_route(nc, io, mem, sem):
    with ExitStack() as ctx:
        sb = lambda n, s, d: ctx.enter_context(nc.sbuf_tensor(n, s, d))
        ps = lambda n, s, d=FP32: ctx.enter_context(nc.psum_tensor(n, s, d))
        NPAT = 8
        R3 = 96
        tb = sb("tb", [R3, NPAT, 256], FP32)
        tbmask = sb("tbmask", [R3, NPAT, 256], FP32)
        tbr = sb("tbr", [R3, NPAT, 256], FP32)
        tb_hi = sb("tb_hi", [R3, NPAT, 256], BF16)
        tb_mid = sb("tb_mid", [R3, NPAT, 256], BF16)
        tb_lo = sb("tb_lo", [R3, NPAT, 256], BF16)
        gates = sb("gates", [P, 2], FP32)
        sig = sb("sig", [P, 4], FP32)
        ends = sb("ends", [P, 2], FP32)
        endr = sb("endr", [P, 2], FP32)
        ends_p = sb("ends_p", [P, 3, 2], BF16)
        endsel = sb("endsel", [P, 2], FP32)
        part_of = sb("part_of", [P, 3], FP32)
        sides = sb("sides", [P, 2, T], BF16)
        far = sb("far", [P, T], FP32)
        krows = sb("krows", [P, T], BF16)
        far_bf = sb("far_bf", [P, T], BF16)
        lmax = sb("lmax", [P, NT], FP32)
        ex = sb("ex", [P, NT, E], FP32)
        ex2 = sb("ex2", [P, NT, E], FP32)
        ssum = sb("ssum", [P, NT], FP32)
        best = sb("best", [P, NT, 8], FP32)
        besti = sb("besti", [P, NT, 8], U32)
        bestf = sb("bestf", [P, NT, 2], FP32)
        wsum = sb("wsum", [P, NT], FP32)
        oh = sb("oh", [P, 2, NT, E], FP32)
        both = sb("both", [P, NT, E], BF16)
        tri = sb("tri", [P, P], BF16)
        ones = sb("ones", [P, P], BF16)
        iota8 = sb("iota8", [P, E], FP32)
        steps = sb("steps", [P, NT + 1], FP32)
        tot = sb("tot", [P, 2, NT, E], FP32)
        excl = sb("excl", [P, NT, E], FP32)
        count = sb("count", [P, E], FP32)
        ge = sb("ge", [P, E, NT], FP32)
        ntile = sb("ntile", [P, 2, E], FP32)
        tile0 = sb("tile0", [P, E], FP32)
        pos_e = sb("pos_e", [P, NT, E], FP32)
        posf = sb("posf", [P, 2, NT], FP32)
        zero = mem["w_gu"][:, NT * D:(NT + 4) * D].rearrange("p (a d) -> p a d", d=D)
        titer = sb("titer", [1, NTILE], FP32)
        tge = sb("tge", [1, NTILE, E], FP32)
        texp = sb("texp", [1, NTILE], FP32)
        psum_ex = ps("psum_ex", [P, 512])
        psum_tot = ps("psum_tot", [P, 512])
        block = ctx.enter_context(nc.Block())
        hi_rows = slice(ROW_FAR, ROW_MAX)
        NTABLES = 13 + 3 * NPAT

        @block.sync
        def _(sp):
            loads = [(part_of[hi_rows], io["part_of"]),
                     (sides[hi_rows], io["sides"]), (tbmask[:], io["tb_mask"]),
                     (tri[:], io["tri"]), (iota8[:], io["iota8"]), (steps[:], io["steps"]),
                     (titer[:], io["tile_index"]), (mem["anti"][:], io["anti"]),
                     (mem["ident_bf"][:], io["ident_bf"]),
                     (gates[:, 0:1], io["et_gate"].partition_broadcast(P)),
                     (gates[:, 1:2], io["is_gate"].partition_broadcast(P)),
                     (ends[:, 0:1], io["tb_rise"][0:1, TBLEN - 1:TBLEN].partition_broadcast(P)),
                     (ends[:, 1:2], io["tb_rise"][0:1, 0:1].partition_broadcast(P))]
            for g in range(3):
                for n in range(NPAT):
                    src = io["tb_rise"] if n < 4 else io["tb_fall"]
                    off = (129 - (P if n < 2 else 0) - 32 * n + 31) if n < 4 else 96 - 32 * (n - 4)
                    loads.append((tb[32 * g:32 * g + 32, n, :],
                                  bass.AP(src.tensor, src.offset + off, [[1, 32], [1, 256]])))
            for dst, src in loads:
                sp.dma_start(dst, src).then_inc(sem["tables"], 16)
            assert len(loads) == NTABLES
            n = 0
            for b in range(NBUF):
                for h in range(HU):
                    sp.dma_start(mem["kst"][ROW_FAR:ROWS, b, h, :], io["key_rows"]).then_inc(sem["rows_set"], 16)
                    n += 1
            sp.wait_ge(sem["far_ready"], 1)
            for b in range(NBUF):
                for h in range(HU):
                    sp.dma_start(mem["qst"][ROW_FAR:ROW_MAX, b, h, :], far_bf[hi_rows, :]).then_inc(sem["rows_set"], 16)
                    n += 1
            sp.wait_ge(sem["rows_set"], 16 * n)

        @block.scalar
        def _(act):
            act.wait_ge(sem["zero_ready"], 1)
            xs = mem["xs_dram"].rearrange("(c a p) d -> c p a d", a=4, p=P)
            for c in range(NTILE // 4):
                act.dma_start(xs[c], zero).then_inc(sem["zeroed"], 16)
            act.wait_ge(sem["tables"], 16 * NTABLES)
            nc.scalar.activation(sig[:, 0:1], gates[:, 0:1], ACT.Exp, scale=-1.0).then_inc(sem["sig_ready"], 1)
            act.wait_ge(sem["ex_ready"], 1)
            nc.scalar.activation(ex2[:], ex[:], ACT.Exp).then_inc(sem["exp_ready"], 1)
            act.wait_ge(sem["zeroed"], 16 * NTILE // 4)

        @block.tensor
        def _(pe):
            pe.wait_ge(sem["onehot_ready"], 1)
            fb = both[:].rearrange("p t e -> p (t e)")
            nc.tensor.matmul(psum_ex[:, 0:NT * E], tri[:], fb, start=True, stop=True)
            nc.tensor.matmul(psum_tot[:, 0:NT * E], ones[:], fb, start=True, stop=True)\
                .then_inc(sem["counts_ready"], 1)

        @block.vector
        def _(dve):
            link, _ = linker(dve, sem["route_chain"])
            nc.vector.memset(zero, 0.0).then_inc(sem["zero_ready"], 1)
            link(nc.vector.memset(ones[:], 1.0))
            dve.wait_ge(sem["tables"], 16 * NTABLES)
            dve.wait_ge(sem["sig_ready"], 1)
            link(nc.vector.tensor_scalar(sig[:, 1:2], sig[:, 0:1], 1.0, None, ALU.add))
            link(nc.vector.reciprocal(sig[:, 2:3], sig[:, 1:2]))
            link(nc.vector.tensor_scalar(ends[:], ends[:], sig[:, 2:3], gates[:, 1:2], ALU.mult, ALU.add))
            link(nc.vector.tensor_scalar(ends[:], ends[:], SCALE_INV, None, ALU.mult))
            split3(nc, link, ends[:], ends_p[:, 0], ends_p[:, 1], ends_p[:, 2], endr[:])
            link(nc.vector.tensor_scalar(endsel[hi_rows], ends_p[hi_rows, 0], part_of[hi_rows, 0:1], None, ALU.mult))
            for j in (1, 2):
                link(nc.vector.scalar_tensor_tensor(out=endsel[hi_rows], in0=ends_p[hi_rows, j],
                                                    scalar=part_of[hi_rows, j:j + 1], in1=endsel[hi_rows],
                                                    op0=ALU.mult, op1=ALU.add))
            link(nc.vector.tensor_scalar(far[hi_rows], sides[hi_rows, 0], endsel[hi_rows, 0:1], None, ALU.mult))
            nc.vector.scalar_tensor_tensor(out=far_bf[hi_rows], in0=sides[hi_rows, 1],
                                           scalar=endsel[hi_rows, 1:2], in1=far[hi_rows],
                                           op0=ALU.mult, op1=ALU.add).then_inc(sem["far_ready"], 1)
            link(nc.vector.tensor_scalar(tb[:], tb[:], sig[0:R3, 2:3], gates[0:R3, 1:2], ALU.mult, ALU.add))
            link(nc.vector.scalar_tensor_tensor(out=tb[:], in0=tb[:], scalar=SCALE_INV, in1=tbmask[:],
                                                op0=ALU.mult, op1=ALU.mult))
            split3(nc, link, tb[:], tb_hi[:], tb_mid[:], tb_lo[:], tbr[:])
            for j, part in enumerate((tb_hi, tb_mid, tb_lo)):
                link(nc.vector.tensor_copy(mem["near"][32 * j:32 * j + 32], part[32 * j:32 * j + 32]))

            lg = mem["logits"]
            link(nc.vector.tensor_reduce(lmax[:], lg[:], AX.X, ALU.max))
            nc.vector.tensor_tensor(ex[:], lg[:], lmax[:].unsqueeze(2).to_broadcast([P, NT, E]), ALU.subtract)\
                .then_inc(sem["ex_ready"], 1)
            dve.wait_ge(sem["exp_ready"], 1)
            link(nc.vector.tensor_reduce(ssum[:], ex2[:], AX.X, ALU.add))
            link(nc.vector.reciprocal(wsum[:], ssum[:]))
            link(nc.vector.tensor_tensor(ex[:], ex2[:], wsum[:].unsqueeze(2).to_broadcast([P, NT, E]), ALU.mult))
            for t in range(NT):
                last = nc.vector.max(best[:, t], ex[:, t])
            link(last)
            for t in range(NT):
                last = nc.vector.max_index(besti[:, t], best[:, t], ex[:, t])
            link(last)
            link(nc.vector.tensor_tensor(ssum[:], best[:, :, 0], best[:, :, 1], ALU.add))
            link(nc.vector.reciprocal(wsum[:], ssum[:]))
            link(nc.vector.tensor_copy(bestf[:], besti[:, :, 0:2]))
            for k in range(TOPK):
                link(nc.vector.tensor_tensor(mem["gate_w"][:, k, :], best[:, :, k], wsum[:], ALU.mult))
                link(nc.vector.tensor_tensor(oh[:, k], bestf[:, :, k:k + 1].to_broadcast([P, NT, E]),
                                             iota8[:].unsqueeze(1).to_broadcast([P, NT, E]), ALU.is_equal))
            nc.vector.tensor_tensor(both[:], oh[:, 0], oh[:, 1], ALU.add).then_inc(sem["onehot_ready"], 1)
            dve.wait_ge(sem["counts_ready"], 1)
            link(nc.vector.tensor_copy(tot[:, 0], psum_tot[:, 0:NT * E].rearrange("p (t e) -> p t e", e=E)))
            a = 0
            d = 1
            while d < NT:
                link(nc.vector.tensor_copy(tot[:, 1 - a, 0:d], tot[:, a, 0:d]))
                link(nc.vector.tensor_tensor(tot[:, 1 - a, d:NT], tot[:, a, d:NT], tot[:, a, 0:NT - d], ALU.add))
                a, d = 1 - a, 2 * d
            link(nc.vector.tensor_copy(count[:], tot[:, a, NT - 1]))
            link(nc.vector.tensor_tensor(excl[:], tot[:, a],
                                         psum_tot[:, 0:NT * E].rearrange("p (t e) -> p t e", e=E), ALU.subtract))
            link(nc.vector.tensor_tensor(ge[:], count[:].unsqueeze(2).to_broadcast([P, E, NT]),
                                         steps[:, 0:NT].unsqueeze(1).to_broadcast([P, E, NT]), ALU.is_gt))
            link(nc.vector.tensor_reduce(ntile[:, 0], ge[:], AX.X, ALU.add))
            link(nc.vector.tensor_copy(count[:], ntile[:, 0]))
            a, d = 0, 1
            while d < E:
                link(nc.vector.tensor_copy(ntile[:, 1 - a, 0:d], ntile[:, a, 0:d]))
                link(nc.vector.tensor_tensor(ntile[:, 1 - a, d:E], ntile[:, a, d:E], ntile[:, a, 0:E - d], ALU.add))
                a, d = 1 - a, 2 * d
            link(nc.vector.tensor_tensor(tile0[:], ntile[:, a], count[:], ALU.subtract))
            link(nc.vector.tensor_tensor(pos_e[:], excl[:],
                                         psum_ex[:, 0:NT * E].rearrange("p (t e) -> p t e", e=E), ALU.add))
            link(nc.vector.scalar_tensor_tensor(out=pos_e[:], in0=tile0[:].unsqueeze(1).to_broadcast([P, NT, E]),
                                                scalar=float(P), in1=pos_e[:], op0=ALU.mult, op1=ALU.add))
            for k in range(TOPK):
                link(nc.vector.tensor_tensor(oh[:, k], oh[:, k], pos_e[:], ALU.mult))
                link(nc.vector.tensor_reduce(posf[:, k], oh[:, k], AX.X, ALU.add))
                link(nc.vector.tensor_copy(mem["pos"][:, k, :], posf[:, k]))
            link(nc.vector.tensor_tensor(tge[:], titer[:].unsqueeze(2).to_broadcast([1, NTILE, E]),
                                         ntile[0:1, a, :].unsqueeze(1).to_broadcast([1, NTILE, E]), ALU.is_ge))
            link(nc.vector.tensor_reduce(texp[:], tge[:], AX.X, ALU.add))
            link(nc.vector.tensor_scalar(texp[:], texp[:], float(E - 1), None, ALU.min))
            nc.vector.tensor_copy(mem["tile_expert"][:], texp[:]).then_inc(sem["routed"], 1)


def near_queries(i, half):
    lo, hi = max(P * i - REACH, HALF * half), min(P * i + P + REACH, HALF * half + HALF)
    return lo - HALF * half, hi - lo, lo - (P * i - REACH)


def near_keys(j, half, group):
    start = P * (j - 1) if group < 2 else P * j
    lo, hi = max(start, HALF * half), min(start + 2 * P, HALF * half + HALF)
    return lo - HALF * half, hi - lo, lo - start


def phase_attention(nc, io, mem, sem):
    with ExitStack() as ctx:
        sb = lambda n, s, d: ctx.enter_context(nc.sbuf_tensor(n, s, d))
        ps = lambda n, s, d=FP32: ctx.enter_context(nc.psum_tensor(n, s, d))
        qst, kst, near, anti = mem["qst"], mem["kst"], mem["near"], mem["anti"]
        vst = sb("vst", [P, NBUF, QT, P], FP32)
        probs = sb("probs", [P, 2, HU, HALF], FP32)
        rowmax = sb("rowmax", [P, 1, HU, QT, 2], FP32)
        negmax = sb("negmax", [P, HU, QT], FP32)
        maxrest = sb("maxrest", [P, HU, QT], FP32)
        maxparts = sb("maxparts", [P, 3, HU, QT], BF16)
        maxT = sb("maxT", [3 * HU * QT, P], BF16)
        ctxu = sb("ctxu", [P, 2, HALF], FP32)
        recip = sb("recip", [P, 2, 4, HU], FP32)
        ctxn = sb("ctxn", [P, 2, 4, HU, HD], FP32)
        sc = ps("sc", [P, 4, HALF])
        sm = ps("sm", [P, 2, HALF])
        pv = ps("pv", [P, HALF])
        misc = ps("misc", [P, HALF])
        miscbf = misc[:].bitcast(BF16)
        block = ctx.enter_context(nc.Block())
        LOADS = 2 * NPAIR + 1

        @block.sync
        def _(sp):
            def load_unit(u, buf):
                unit = mem["qk_dram"][bass.ds(u, 1)]
                for stack, which, order in ((qst, 0, QPART), (kst, 1, KPART)):
                    for g, part in enumerate(order):
                        sp.dma_start(stack[HD * g:HD * g + HD, buf],
                                     unit[:, which, part].rearrange("u (h d) t -> (u d) h t", d=HD))\
                            .then_inc(sem["stack_loaded"][buf], 16)
                sp.dma_start(vst[:, buf], mem["v_dram"][bass.ds(u, 1)].rearrange("u p a w -> (u p) a w"))\
                    .then_inc(sem["stack_loaded"][buf], 16)

            def max_rows(count, buf):
                sp.wait_ge(sem["maxT_ready"], count)
                for j in range(3):
                    sp.dma_start(qst[ROW_MAX + j:ROW_MAX + j + 1, buf].rearrange("p h (j q) -> p (h j) q", q=P),
                                 maxT[HU * QT * j:HU * QT * j + HU * QT, :]).then_inc(sem["max_rows"][buf], 16)

            def store_ctx(u, half):
                sp.wait_ge(sem["ctxn_ready"], u * 2 + (1 + half + 1))
                for h in range(HU):
                    sp.dma_start(mem["ctx_dram"][bass.ds(u, 1), h, HALF * half:HALF * half + HALF, :]
                                 .rearrange("u (a p) d -> (u p) a d", p=P),
                                 ctxn[:, half, :, h, :]).then_inc(sem["ctx_stored"][half], 16)

            load_unit(0, 0)
            load_unit(1, 1)
            max_rows(1, 0)

            def unit(u, r, more):
                sp.wait_ge(sem["ctxT_ready"], u * 2 + 2)
                if more:
                    load_unit(u + 2, (r + 2) % NBUF)
                store_ctx(u, 0)
                max_rows(u + 2, (r + 1) % NBUF)
                store_ctx(u, 1)

            rounds = (NU - 1) // NBUF
            with sp.Fori(0, rounds - 1) as it:
                for r in range(NBUF):
                    unit(it * NBUF + r, r, True)
            for r in range(NBUF):
                u = (rounds - 1) * NBUF + r
                unit(u, r, u + 2 < NU)
            store_ctx(NU - 1, 0)
            store_ctx(NU - 1, 1)
            for half in range(2):
                sp.wait_ge(sem["ctx_stored"][half], 64 + 64 * NU)

        @block.gpsimd
        def _(pool):
            for k in range(TOPK):
                for t in range(NT):
                    pool.indirect_dma_start(mem["xs_dram"], bass.IndirectOffsetOnAxis(
                        ap=mem["pos"][:, k, t:t + 1], axis=0), mem["xn"][:, t, :], None)\
                        .then_inc(sem["scattered"], 16)
            pool.wait_ge(sem["scattered"], 16 * TOPK * NT)
            pool.dma_start(mem["w_gu"][:], io["w_gu"]).then_inc(sem["gu_loaded"], 16)
            pool.wait_ge(sem["gu_loaded"], 16)

        def pe_max(pe, base, n, buf, first=False):
            if not (first and n < 2):
                pe.wait_ge(sem["max_taken"], base + (n - 1))
            h, j, half = n // (2 * QT), n // 2 % QT, n % 2
            parts = [(g, *near_keys(j, half, g)) for g in range(4)]
            parts = [x for x in parts if x[2] > 0]
            last = nc.tensor.matmul(sm[:, n % 2, :], qst[0:ROW_MAX, buf, h, P * j:P * j + P],
                                    kst[0:ROW_MAX, buf, h, HALF * half:HALF * half + HALF],
                                    start=True, stop=not parts, skip_group_check=True)
            for g, at, width, col in parts:
                last = nc.tensor.matmul(sm[32 * g:32 * g + 32, n % 2, at:at + width], anti[0:96, :],
                                        near[0:96, g, col:col + width], start=False, stop=True,
                                        skip_group_check=True)
            last.then_inc(sem["max_scores"], 1)

        def pe_maxT(pe, count):
            pe.wait_ge(sem["maxparts_ready"], count)
            nc.tensor.transpose(miscbf[0:3 * HU * QT, 0:P], maxparts[:].rearrange("p c h j -> p (c h j)"),
                                mem["ident_bf"][:]).then_inc(sem["maxT_done"], 1)

        def pe_scores(pe, base, step, buf, h):
            half, i = step // QT, step % QT
            at, width, col = near_queries(i, half)
            if h % 2 == 0:
                pe.wait_ge(sem["probs_ready"], base + (2 + 2 * step + h // 2 - 1))
            last = nc.tensor.matmul(sc[:, h, :], kst[0:ROWS, buf, h, P * i:P * i + P],
                                    qst[0:ROWS, buf, h, HALF * half:HALF * half + HALF],
                                    start=True, stop=width <= 0, skip_group_check=True)
            if width > 0:
                for g in range(4):
                    last = nc.tensor.matmul(sc[32 * g:32 * g + 32, h, at:at + width], anti[0:96, :],
                                            near[0:96, 4 + g, col:col + width], start=False, stop=True,
                                            skip_group_check=True)
            if h % 2:
                last.then_inc(sem["scores_ready"], 1)

        def pe_values(pe, base, u, step, buf):
            half, i = step // QT, step % QT
            pe.wait_ge(sem["probs_ready"], base + (2 + 2 * step + 2))
            if i == 0:
                pe.wait_ge(sem["ctxu_ready"], u * 2 + (1 + half))
            for h in range(HU):
                last = nc.tensor.matmul(pv[32 * h:32 * h + 32, :], vst[:, buf, i, 32 * h:32 * h + 32],
                                        probs[:, step % 2, h, :], start=(i == 0), stop=(i == QT - 1),
                                        skip_group_check=True)
            last.then_inc(sem["values_added"], 1)

        def pe_ctxT(pe, u, half):
            pe.wait_ge(sem["ctxu_ready"], u * 2 + (1 + half + 1))
            if half == 0:
                pe.wait_ge(sem["ctxn_ready"], u * 2 + 1)
            else:
                pe.wait_ge(sem["ctxn_ready"], u * 2 + (1 + 1))
            for a in range(4):
                last = nc.tensor.transpose(misc[:, P * a:P * a + P], ctxu[:, half, P * a:P * a + P], mem["ident"][:])
            last.then_inc(sem["ctxT_ready"], 1)

        @block.tensor
        def _(pe):
            pe.sem_inc(sem["probs_ready"], 2)
            pe.sem_inc(sem["values_added"], 2)
            pe.sem_inc(sem["ctxT_ready"], 2)
            pe.sem_inc(sem["ctxu_ready"], 1)
            pe.sem_inc(sem["ctxn_ready"], 1)
            for half in range(2):
                pe.sem_inc(sem["ctx_stored"][half], 64)

            def unit(it, r, ahead):
                u = it * NBUF + r
                base = u * (2 * STEPS)
                nxt = (r + 1) % NBUF
                n = 0
                pe.wait_ge(sem["max_rows"][r], it * 48 + 48)
                if ahead:
                    pe.wait_ge(sem["stack_loaded"][nxt], (it + (1 if r == NBUF - 1 else 0)) * (16 * LOADS) + 16 * LOADS)
                for step in range(STEPS):
                    for h in range(HU):
                        pe_scores(pe, base, step, r, h)
                        if ahead and n < MAXIMA:
                            pe_max(pe, u * MAXIMA + MAXIMA, n, nxt)
                            n += 1
                    if step:
                        pe_values(pe, base, u, step - 1, r)
                    if ahead and n < MAXIMA:
                        pe_max(pe, u * MAXIMA + MAXIMA, n, nxt)
                        n += 1
                    if step == 11:
                        pe_ctxT(pe, u, 0)
                    if ahead and step == STEPS - 1:
                        pe_maxT(pe, u + 2)
                pe_values(pe, base, u, STEPS - 1, r)
                if ahead:
                    pe.wait_ge(sem["maxT_ready"], u + 2)
                pe_ctxT(pe, u, 1)

            pe.wait_ge(sem["stack_loaded"][0], 16 * LOADS)
            for n in range(MAXIMA):
                pe_max(pe, 0, n, 0, first=True)
            pe_maxT(pe, 1)
            with pe.Fori(0, (NU - 1) // NBUF) as it:
                for r in range(NBUF):
                    unit(it, r, True)
            unit((NU - 1) // NBUF, 0, False)

        @block.scalar
        def _(act):
            def copy_maxT(count):
                act.wait_ge(sem["maxT_done"], count)
                nc.scalar.activation(maxT[:], miscbf[0:3 * HU * QT, 0:P], ACT.Copy).then_inc(sem["maxT_ready"], 1)

            def copy_ctx(u, half):
                act.wait_ge(sem["values_added"], u * STEPS + (2 + QT * (half + 1)))
                nc.scalar.activation(ctxu[:, half, :], pv[:], ACT.Copy).then_inc(sem["ctxu_ready"], 1)

            def unit(it, r, ahead):
                u = it * NBUF + r
                for step in range(STEPS):
                    for pair in range(2):
                        c = 2 * step + pair
                        act.wait_ge(sem["scores_ready"], u * (2 * STEPS) + (c + 1))
                        if pair == 0:
                            act.wait_ge(sem["values_added"], u * STEPS + (2 + step - 1))
                        nc.scalar.activation(probs[:, step % 2, 2 * pair:2 * pair + 2, :],
                                             sc[:, 2 * pair:2 * pair + 2, :], ACT.Exp, scale=1.0 / SCALE_INV)\
                            .then_inc(sem["probs_ready"], 1)
                    if step == QT:
                        copy_ctx(u, 0)
                if ahead:
                    copy_maxT(u + 2)
                copy_ctx(u, 1)

            copy_maxT(1)
            with act.Fori(0, (NU - 1) // NBUF) as it:
                for r in range(NBUF):
                    unit(it, r, True)
            unit((NU - 1) // NBUF, 0, False)

        @block.vector
        def _(dve):
            def take_max(base, n, slot):
                h, j, half = n // (2 * QT), n // 2 % QT, n % 2
                dve.wait_ge(sem["max_scores"], base + (n + 1))
                nc.vector.tensor_reduce(rowmax[:, slot, h, j, half:half + 1], sm[:, n % 2, :], AX.X, ALU.max)\
                    .then_inc(sem["max_taken"], 1)

            def split_max(base, links, slot, count):
                dve.wait_ge(sem["max_taken"], base + MAXIMA)
                link, made = linker(dve, sem["max_chain"], links)
                link(nc.vector.tensor_reduce(negmax[:], rowmax[:, slot], AX.X, ALU.max, negate=True))
                split3_last(link)
                return made[0]

            def split3_last(link):
                hi, mid, lo = (maxparts[:, j] for j in range(3))
                link(nc.vector.tensor_copy(hi, negmax[:]))
                link(nc.vector.tensor_tensor(maxrest[:], negmax[:], hi, ALU.subtract))
                link(nc.vector.tensor_copy(mid, maxrest[:]))
                nc.vector.tensor_tensor(lo, maxrest[:], mid, ALU.subtract).then_inc(sem["maxparts_ready"], 1)

            def normalise(u, half):
                dve.wait_ge(sem["ctxT_ready"], u * 2 + (2 + half + 1))
                dve.wait_ge(sem["ctx_stored"][half], u * (16 * 4) + 64)
                m = misc[:].rearrange("p (a h w) -> p a h w", a=4, w=VW)
                nc.vector.reciprocal(recip[:, half], m[:, :, :, HD]).then_inc(sem["recip_ready"], 1)
                dve.wait_ge(sem["recip_ready"], u * 2 + (half + 1))
                nc.vector.tensor_tensor(ctxn[:, half], m[:, :, :, 0:HD],
                                        recip[:, half].unsqueeze(3).to_broadcast([P, 4, HU, HD]),
                                        ALU.mult).then_inc(sem["ctxn_ready"], 1)

            LINKS = 4

            def unit(it, r, ahead):
                u = it * NBUF + r
                if ahead:
                    for n in range(MAXIMA):
                        take_max(u * MAXIMA + MAXIMA, n, 0)
                        if n == 60:
                            normalise(u, 0)
                    made = split_max(u * MAXIMA + MAXIMA, u * LINKS + LINKS, 0, u + 2)
                    assert made == LINKS
                else:
                    normalise(u, 0)
                normalise(u, 1)

            for n in range(MAXIMA):
                take_max(0, n, 0)
            split_max(0, 0, 0, 1)
            with dve.Fori(0, (NU - 1) // NBUF) as it:
                for r in range(NBUF):
                    unit(it, r, True)
            unit((NU - 1) // NBUF, 0, False)


def phase_experts(nc, io, mem, sem):
    with ExitStack() as ctx:
        sb = lambda n, s, d: ctx.enter_context(nc.sbuf_tensor(n, s, d))
        ps = lambda n, s, d=FP32: ctx.enter_context(nc.psum_tensor(n, s, d))
        w_gu = mem["w_gu"]
        w_dn = sb("w_dn", [P, E * NI * D], FP32)
        xs = sb("xs", [P, 2, D], FP32)
        xsT = sb("xsT", [P, 2, KT, P], FP32)
        silu = sb("silu", [P, 2, IC], FP32)
        hid = sb("hid", [P, 2, I], FP32)
        hidT = sb("hidT", [P, NI, P], FP32)
        ys = sb("ys", [P, 2, D], FP32)
        gu = ps("gu", [P, 4, HALF])
        xt = ps("xt", [P, HALF])
        ht = ps("ht", [P, 8, P])
        yp = ps("yp", [P, HALF])
        block = ctx.enter_context(nc.Block())
        PAIRS = (NTILE - 2) // 2
        REM = I - (NI - 1) * P

        @block.sync
        def _(sp):
            dn = w_dn[:].rearrange("p (e i d) -> p e i d", e=E, i=NI)
            sp.dma_start(dn[0:REM, :, NI - 1, :], io["w_dn"][:, (NI - 1) * P:I, :].rearrange("e p d -> p e d"))\
                .then_inc(sem["dn_loaded"], 16)
            for i in range(NI - 1):
                sp.dma_start(dn[:, :, i, :], io["w_dn"][:, i * P:i * P + P, :].rearrange("e p d -> p e d"))\
                    .then_inc(sem["dn_loaded"], 16)

            def load(t, s):
                sp.dma_start(xs[:, s, :], mem["xs_dram"][bass.ds(t * P, P), :]).then_inc(sem["xs_loaded"][s], 16)

            def store(t, s):
                sp.wait_ge(sem["y_ready"], t + 1)
                sp.dma_start(mem["y_dram"][bass.ds(t * P, P), :], ys[:, s, :]).then_inc(sem["y_stored"][s], 16)

            load(0, 0)
            load(1, 1)
            sp.wait_ge(sem["xT_done"], 1)
            load(2, 0)
            with sp.Fori(0, PAIRS - 1) as it:
                for r in range(2):
                    t = it * 2 + (r + 1)
                    sp.wait_ge(sem["xT_done"], t + 1)
                    load(t + 2, (r + 1) % 2)
                    store(t - 1, r)
            for t in range(NTILE - 3, NTILE + 1):
                if t + 2 < NTILE:
                    sp.wait_ge(sem["xT_done"], t + 1)
                    load(t + 2, t % 2)
                store(t - 1, (t - 1) % 2)
            for s in range(2):
                sp.wait_ge(sem["y_stored"][s], 16 + 16 * NTILE // 2)

        @block.tensor
        def _(pe):
            def x_T(s, loaded):
                pe.wait_ge(sem["xs_loaded"][s], loaded)
                for k in range(KT):
                    last = nc.tensor.transpose(xt[:, P * k:P * k + P], xs[:, s, P * k:P * k + P], mem["ident"][:])
                last.then_inc(sem["xT_done"], 1)

            def expert(t):
                return pe.value_load(mem["tile_expert"][0:1, bass.ds(t, 1)], min_val=0, max_val=E - 1)

            def gate_up(t, s, e, first=False):
                pe.wait_ge(sem["xsT_ready"], t + 1)
                for j in range(2):
                    if not first:
                        pe.wait_ge(sem["hid_ready"], t * 2 + (j - 1))
                    for which in range(2):
                        for k in range(KT):
                            last = nc.tensor.matmul(
                                gu[:, 2 * j + which, 0:IC], xsT[:, s, k, :],
                                w_gu[:, bass.ds(e * (KT * GUW) + (k * GUW + which * I + j * IC), IC)],
                                start=(k == 0), stop=(k == KT - 1))
                    last.then_inc(sem["gate_up"], 1)

            def h_T(t, s):
                pe.wait_ge(sem["hid_ready"], t * 2 + 2)
                for i in range(NI):
                    w = min(P, I - P * i)
                    last = nc.tensor.transpose(ht[0:w, i, :], hid[:, s, P * i:P * i + w], mem["ident"][:])
                last.then_inc(sem["hT_done"], 1)

            def down(t, e, first=False):
                pe.wait_ge(sem["hidT_lo"], t + 1)
                pe.wait_ge(sem["hidT_hi"], t + 1)
                if not first:
                    pe.wait_ge(sem["y_ready"], t)
                for i in range(NI):
                    w = min(P, I - P * i)
                    last = nc.tensor.matmul(yp[:, 0:D], hidT[0:w, i, :],
                                            w_dn[0:w, bass.ds(e * (NI * D) + i * D, D)],
                                            start=(i == 0), stop=(i == NI - 1))
                last.then_inc(sem["y_done"], 1)

            for s in range(2):
                pe.sem_inc(sem["y_stored"][s], 16)
            x_T(0, 16)
            gate_up(0, 0, expert(0), first=True)
            x_T(1, 16)
            pe.wait_ge(sem["dn_loaded"], 16 * NI)
            with pe.Fori(0, PAIRS) as it:
                for r in range(2):
                    t = it * 2 + (r + 1)
                    s = (r + 1) % 2
                    h_T(t - 1, r)
                    gate_up(t, s, expert(t))
                    x_T(r, it * 16 + (32 if r == 0 else 32))
                    down(t - 1, expert(t - 1))
            t = NTILE - 1
            h_T(t - 1, 0)
            gate_up(t, 1, expert(t))
            down(t - 1, expert(t - 1))
            h_T(t, 1)
            down(t, expert(t))

        @block.scalar
        def _(act):
            def copy_xT(t, s):
                act.wait_ge(sem["xT_done"], t + 1)
                nc.scalar.activation(xsT[:, s], xt[:, 0:KT * P].rearrange("p (k t) -> p k t", k=KT), ACT.Copy)\
                    .then_inc(sem["xsT_ready"], 1)

            def gate(t, first=False):
                for j in range(2):
                    act.wait_ge(sem["gate_up"], t * 2 + (j + 1))
                    if not first:
                        act.wait_ge(sem["hid_ready"], t * 2 + (j - 1))
                    nc.scalar.activation(silu[:, j, :], gu[:, 2 * j, 0:IC], ACT.Silu).then_inc(sem["silu_ready"], 1)

            def copy_hT(t):
                act.wait_ge(sem["hT_done"], t + 1)
                nc.scalar.activation(hidT[:, 4, :], ht[:, 4, :], ACT.Copy)
                nc.scalar.activation(hidT[0:REM, 5, :], ht[0:REM, 5, :], ACT.Copy).then_inc(sem["hidT_hi"], 1)

            def copy_y(t, s, stored):
                act.wait_ge(sem["y_done"], t + 1)
                act.wait_ge(sem["y_stored"][s], stored)
                nc.scalar.activation(ys[:, s, :], yp[:, 0:D], ACT.Copy).then_inc(sem["y_ready"], 1)

            copy_xT(0, 0)
            gate(0, first=True)
            copy_xT(1, 1)
            with act.Fori(0, PAIRS) as it:
                for r in range(2):
                    t = it * 2 + (r + 1)
                    copy_hT(t - 1)
                    gate(t)
                    copy_xT(t + 1, r)
                    copy_y(t - 1, r, it * 16 + 16)
            t = NTILE - 1
            copy_hT(t - 1)
            gate(t)
            copy_y(t - 1, 0, 16 + 16 * (t - 1) // 2)
            copy_hT(t)
            copy_y(t, 1, 16 + 16 * (t - 1) // 2)

        @block.vector
        def _(dve):
            def copy_hT(t):
                dve.wait_ge(sem["hT_done"], t + 1)
                nc.vector.tensor_copy(hidT[:, 0:4, :], ht[:, 0:4, :]).then_inc(sem["hidT_lo"], 1)

            def hidden(t, s):
                for j in range(2):
                    dve.wait_ge(sem["silu_ready"], t * 2 + (j + 1))
                    nc.vector.tensor_tensor(hid[:, s, j * IC:j * IC + IC], silu[:, j, :], gu[:, 2 * j + 1, 0:IC],
                                            ALU.mult).then_inc(sem["hid_ready"], 1)

            hidden(0, 0)
            with dve.Fori(0, PAIRS) as it:
                for r in range(2):
                    t = it * 2 + (r + 1)
                    copy_hT(t - 1)
                    hidden(t, (r + 1) % 2)
            copy_hT(NTILE - 2)
            hidden(NTILE - 1, 1)
            copy_hT(NTILE - 1)


def phase_combine(nc, io, mem, sem, out):
    with ExitStack() as ctx:
        sb = lambda n, s, d: ctx.enter_context(nc.sbuf_tensor(n, s, d))
        ps = lambda n, s, d=FP32: ctx.enter_context(nc.psum_tensor(n, s, d))
        R = 4
        wo = sb("wo", [P, KT, D], FP32)
        wo_hi = sb("wo_hi", [P, KT, D], FP32R)
        wo_lo = sb("wo_lo", [P, KT, D], FP32R)
        bo = sb("bo", [P, D], FP32)
        xin = sb("xin", [P, R, D], FP32)
        cin = sb("cin", [P, R, D], FP32)
        yin = sb("yin", [P, R, TOPK, D], FP32)
        chi = sb("chi", [P, 2, KT, P], FP32R)
        clo = sb("clo", [P, 2, KT, P], FP32R)
        acc = sb("acc", [P, 2, 3, D], FP32)
        res = sb("res", [P, R, D], FP32)
        ct = ps("ct", [P, 2, HALF])
        op = ps("op", [P, 2, HALF])
        block = ctx.enter_context(nc.Block())

        @block.sync
        def _(sp):
            sp.dma_start(wo[:], io["w_o"]).then_inc(sem["wo_loaded"], 16)
            sp.dma_start(bo[:], io["b_o"].partition_broadcast(P)).then_inc(sem["wo_loaded"], 16)
            with sp.Fori(0, GU) as g:
                for tt in range(QT):
                    r = tt % R
                    t = g * QT + tt
                    sp.wait_ge(sem["res_ready"], t + (R - R + 1))
                    sp.dma_start(xin[:, r, :], io["x"][bass.ds(t * P, P), :]).then_inc(sem["in_loaded"][r], 16)
                    for b in range(2):
                        sp.dma_start(cin[64 * b:64 * b + 64, r, :],
                                     mem["ctx_dram"][bass.ds(g + (2 * (tt % 2) + b) * GU, 1), tt // 2]
                                     .rearrange("u (r q) d -> (u r) (q d)", q=HD)).then_inc(sem["in_loaded"][r], 16)

        @block.gpsimd
        def _(pool):
            for t in range(NT):
                if t >= R:
                    pool.wait_ge(sem["res_ready"], R + t - R + 1)
                for k in range(TOPK):
                    pool.indirect_dma_start(yin[:, t % R, k, :], None, mem["y_dram"], bass.IndirectOffsetOnAxis(
                        ap=mem["pos"][:, k, t:t + 1], axis=0)).then_inc(sem["y_gathered"][t % R], 16)

        @block.tensor
        def _(pe):
            pe.sem_inc(sem["res_ready"], R)
            pe.sem_inc(sem["proj_used"], 2)
            for r in range(R):
                pe.sem_inc(sem["out_stored"][r], 16)
            pe.wait_ge(sem["wo_split"], 2)
            with pe.Fori(0, GU) as g:
                for tt in range(QT):
                    r, s, t = tt % R, tt % 2, g * QT + tt
                    pe.wait_ge(sem["in_loaded"][r], g * (2 * 48) + (tt // R * 48 + 48))
                    pe.wait_ge(sem["proj_used"], t + 1)
                    for k in range(KT):
                        last = nc.tensor.transpose(ct[:, s, P * k:P * k + P], cin[:, r, P * k:P * k + P], mem["ident"][:])
                    last.then_inc(sem["ct_done"], 1)
                    pe.wait_ge(sem["clo_ready"], t + 1)
                    i = 0
                    for k in range(KT):
                        for c, w in ((chi, wo_hi), (clo, wo_hi), (chi, wo_lo)):
                            last = nc.tensor.matmul(op[:, s, 0:D], c[:, s, k, :], w[:, k, :],
                                                    start=(i == 0), stop=(i == 3 * KT - 1))
                            i += 1
                    last.then_inc(sem["proj_done"], 1)

        @block.scalar
        def _(act):
            act.wait_ge(sem["wo_loaded"], 32)
            nc.scalar.activation(wo_hi[:], wo[:], ACT.Copy).then_inc(sem["wo_split"], 1)

            def store(t, r):
                act.wait_ge(sem["res_ready"], t + (R + 1))
                act.dma_start(out[bass.ds(t * P, P), :], res[:, r, :]).then_inc(sem["out_stored"][r], 16)

            with act.Fori(0, GU) as g:
                for tt in range(QT):
                    s, t = tt % 2, g * QT + tt
                    act.wait_ge(sem["ct_done"], t + 1)
                    nc.scalar.activation(chi[:, s], ct[:, s, 0:KT * P].rearrange("p (k t) -> p k t", k=KT), ACT.Copy)\
                        .then_inc(sem["chi_ready"], 1)
                    store(t, tt % R)
            for r in range(R):
                act.wait_ge(sem["out_stored"][r], 16 + 16 * NT // R)

        @block.vector
        def _(dve):
            dve.wait_ge(sem["wo_split"], 1)
            nc.vector.tensor_tensor(wo_lo[:], wo[:], wo_hi[:], ALU.subtract).then_inc(sem["wo_split"], 1)
            with dve.Fori(0, GU) as g:
                for tt in range(QT):
                    r, s, t = tt % R, tt % 2, g * QT + tt
                    link, _ = linker(dve, sem["sum_chain"], g * (2 * QT) + 2 * tt)
                    dve.wait_ge(sem["chi_ready"], t + 1)
                    nc.vector.tensor_tensor(clo[:, s], ct[:, s, 0:KT * P].rearrange("p (k t) -> p k t", k=KT),
                                            chi[:, s], ALU.subtract).then_inc(sem["clo_ready"], 1)
                    dve.wait_ge(sem["in_loaded"][r], g * (2 * 48) + (tt // R * 48 + 48))
                    link(nc.vector.tensor_tensor(acc[:, s, 0], xin[:, r, :], bo[:], ALU.add))
                    dve.wait_ge(sem["proj_done"], t + 1)
                    nc.vector.tensor_tensor(acc[:, s, 1], acc[:, s, 0], op[:, s, 0:D], ALU.add)\
                        .then_inc(sem["proj_used"], 1)
                    dve.wait_ge(sem["proj_used"], t + (2 + 1))
                    dve.wait_ge(sem["y_gathered"][r], g * (2 * 32) + (tt // R * 32 + 32))
                    link(nc.vector.scalar_tensor_tensor(out=acc[:, s, 2], in0=yin[:, r, 0, :],
                                                        scalar=mem["gate_w"][:, 0, bass.ds(t, 1)],
                                                        in1=acc[:, s, 1], op0=ALU.mult, op1=ALU.add))
                    dve.wait_ge(sem["out_stored"][r], g * 32 + (16 + tt // R * 16))
                    nc.vector.scalar_tensor_tensor(out=res[:, r, :], in0=yin[:, r, 1, :],
                                                   scalar=mem["gate_w"][:, 1, bass.ds(t, 1)],
                                                   in1=acc[:, s, 2], op0=ALU.mult, op1=ALU.add)\
                        .then_inc(sem["res_ready"], 1)


SEMS = """weights w_hi w_lo ones_ready xn_ready rest_ready lo_ready q32_ready vr_used var_ready std_ready
tr_ready xhi_ready xlo_ready qk_ready hi_ready mid_ready vr_ready stats_chain root_chain
tables rows_set far_ready zero_ready zeroed sig_ready ex_ready exp_ready onehot_ready counts_ready route_chain routed
scattered gu_loaded max_scores max_taken maxparts_ready maxT_done maxT_ready scores_ready probs_ready values_added
ctxu_ready ctxT_ready ctxn_ready recip_ready max_chain
dn_loaded xT_done xsT_ready gate_up silu_ready hid_ready hT_done hidT_lo hidT_hi y_done y_ready
wo_loaded wo_split ct_done chi_ready clo_ready proj_done proj_used sum_chain res_ready""".split()
SEM_RINGS = {"x_loaded": 2, "xn_stored": 2, "parts_stored": 4, "v_stored": 2, "stack_loaded": NBUF, "max_rows": NBUF,
             "ctx_stored": 2, "xs_loaded": 2, "y_stored": 2, "in_loaded": 4, "y_gathered": 4, "out_stored": 4}


def build(nc, io, out):
    with ExitStack() as ctx:
        sb = lambda n, s, d: ctx.enter_context(nc.sbuf_tensor(n, s, d))
        dram = lambda n, s, d: nc.dram_tensor(n, s, d, kind="Internal").ap()
        sem = {n: ctx.enter_context(nc.semaphore(n)) for n in SEMS}
        for n, k in SEM_RINGS.items():
            sem[n] = [ctx.enter_context(nc.semaphore(f"{n}{i}")) for i in range(k)]
        mem = {
            "qk_dram": dram("qk_dram", (NU, 2, 3, HU * HD, T), BF16),
            "v_dram": dram("v_dram", (NU, P, QT, P), FP32),
            "ctx_dram": dram("ctx_dram", (NU, HU, T, HD), FP32),
            "xs_dram": dram("xs_dram", (NPOS, D), FP32),
            "y_dram": dram("y_dram", (NPOS, D), FP32),
            "ident": sb("ident", [P, P], FP32),
            "pos": sb("pos", [P, TOPK, NT], I32),
            "gate_w": sb("gate_w", [P, TOPK, NT], FP32),
            "tile_expert": sb("tile_expert", [1, NTILE], I32),
            "logits": sb("logits", [P, NT, E], FP32),
            "w_gu": sb("w_gu", [P, E * KT * GUW], FP32),
        }
        mem["xn"] = mem["w_gu"][:, 0:NT * D].rearrange("p (t d) -> p t d", d=D)
        phase_project(nc, io, mem, sem)
        with ExitStack() as stacks:
            for n, s in (("qst", [P, NBUF, HU, T]), ("kst", [P, NBUF, HU, T]), ("near", [96, 8, 256]),
                         ("anti", [96, 32]), ("ident_bf", [P, P])):
                mem[n] = stacks.enter_context(nc.sbuf_tensor(n, s, BF16))
            phase_route(nc, io, mem, sem)
            phase_attention(nc, io, mem, sem)
        phase_experts(nc, io, mem, sem)
        phase_combine(nc, io, mem, sem, out)


def constants():
    def bf16_bits(ones):
        return np.where(ones != 0, 0x3F80, 0).astype(np.uint16)

    c = {}
    c["ident"] = np.eye(P, dtype=np.float32)
    c["ident_bf"] = bf16_bits(np.eye(P))
    c["anti"] = bf16_bits(np.tile(np.eye(32)[::-1], (3, 1)))
    c["tri"] = bf16_bits(np.triu(np.ones((P, P)), 1))
    c["iota8"] = np.tile(np.arange(E, dtype=np.float32), (P, 1))
    c["steps"] = np.tile(np.arange(NT + 1, dtype=np.float32) * P, (P, 1))
    c["tile_index"] = np.arange(NTILE, dtype=np.float32)[None]
    t = np.arange(T)
    rows = np.zeros((ROWS - ROW_FAR, T), np.float32)
    sides = np.zeros((3 * QT, 2, T), np.float32)
    part_of = np.zeros((3 * QT, 3), np.float32)
    for p in range(3):
        for i in range(QT):
            rows[QT * p + i] = (t // P == i)
            sides[QT * p + i, 0] = t < P * i - REACH
            sides[QT * p + i, 1] = t >= P * i + P + REACH
            part_of[QT * p + i, p] = 1
    rows[3 * QT:] = 1
    c["key_rows"] = bf16_bits(rows)
    c["sides"] = bf16_bits(sides)
    c["part_of"] = part_of
    m = np.ones((3, 32, 8, 256), np.float32)
    m[:, 0:2, 1, 0:P] = 0
    m[:, 30:32, 2, P:] = 0
    c["tb_mask"] = m.reshape(96, 8, 256)
    return c


def kernel(L0_attn_x, L0_attn_Wq, L0_attn_bq, L0_attn_Wk, L0_attn_bk, L0_attn_Wv, L0_attn_bv, L0_attn_Wo,
           L0_attn_bo, L0_attn_et_gate, L0_attn_is_gate, L0_attn_time_bias, L0_ffn_w_router, L0_ffn_w_gate,
           L0_ffn_w_up, L0_ffn_w_down):
    import concourse.bacc as bacc
    from concourse.bass_utils import run_bass_kernel_spmd

    a = np.asarray
    tiles = lambda w: np.ascontiguousarray(w.reshape(KT, P, -1).transpose(1, 0, 2))
    tb = a(L0_attn_time_bias).reshape(TB)
    arrays = dict(constants())
    arrays["x"] = np.ascontiguousarray(a(L0_attn_x).reshape(NTOK, D))
    arrays["w_qk"] = tiles(np.concatenate([a(L0_attn_Wq).T, a(L0_attn_Wk).T], axis=1))
    arrays["w_vr"] = tiles(np.concatenate([a(L0_attn_Wv).T, a(L0_ffn_w_router).T], axis=1))
    arrays["w_o"] = tiles(a(L0_attn_Wo).T)
    arrays["b_qk"] = np.ascontiguousarray(np.concatenate([a(L0_attn_bq), a(L0_attn_bk)]).reshape(4, P).T)
    arrays["b_v"] = a(L0_attn_bv).reshape(1, D)
    arrays["b_o"] = a(L0_attn_bo).reshape(1, D)
    arrays["et_gate"] = a(L0_attn_et_gate).reshape(1, 1)
    arrays["is_gate"] = a(L0_attn_is_gate).reshape(1, 1)
    arrays["tb_rise"] = np.ascontiguousarray(np.pad(tb, (129, TBLEN - 129 - TB), mode="edge")[None])
    arrays["tb_fall"] = np.ascontiguousarray(np.pad(tb[::-1], (127, TBLEN - 127 - TB), mode="edge")[None])
    gu = np.concatenate([a(L0_ffn_w_gate), a(L0_ffn_w_up)], axis=1).transpose(0, 2, 1)
    arrays["w_gu"] = np.ascontiguousarray(gu.reshape(E, KT, P, GUW).transpose(2, 0, 1, 3).reshape(P, -1))
    arrays["w_dn"] = np.ascontiguousarray(a(L0_ffn_w_down).transpose(0, 2, 1))

    nc = bacc.Bacc("TRN2", target_bir_lowering=False, num_devices=1)
    io = {n: nc.dram_tensor(n + "_in", v.shape, mybir.dt.from_np(v.dtype), kind="ExternalInput").ap()
          for n, v in arrays.items()}
    for n, v in arrays.items():
        if v.dtype == np.uint16:
            io[n] = io[n].bitcast(BF16)
    out = nc.dram_tensor("out", (NTOK, D), FP32, kind="ExternalOutput").ap()
    build(nc, io, out)
    r = run_bass_kernel_spmd(nc, [{n + "_in": v for n, v in arrays.items()}], core_ids=[0])
    return r.results[0]["out"].reshape(B, T, D)
```

```python
from contextlib import ExitStack

import numpy as np
import concourse.bass as bass
import concourse.mybir as mybir

FP32 = mybir.dt.float32
FP32R = mybir.dt.float32r
BF16 = mybir.dt.bfloat16
I32 = mybir.dt.int32
U32 = mybir.dt.uint32
ALU = mybir.AluOpType
ACT = mybir.ActivationFunctionType
AX = mybir.AxisListType

P = 128
B, T, D = 4, 1024, 256
H, HD = 16, 16
NTOK = B * T
NT = NTOK // P
E, I, TOPK = 8, 704, 2
TB = 125
REACH = TB // 2
KT = D // P
EPS = 1e-5

HU = 4
GU = H // HU
NU = B * GU
QT = T // P
HALF = 512
VW = 32
NPAIR = 6
QPART = [0, 0, 0, 1, 1, 2]
KPART = [0, 1, 2, 0, 1, 0]
ROW_FAR = NPAIR * HD
ROW_MAX = ROW_FAR + 3 * QT
ROWS = ROW_MAX + 3
NBUF = 3
MAXIMA = HU * QT * 2
STEPS = 2 * QT
SCALE_INV = 4.0

NTILE = 72
NPOS = NTILE * P
IC = 352
NI = (I + P - 1) // P
GUW = 2 * I
TBLEN = 384
CONSTS = ["near_mask", "anti", "ident_bf", "tri", "iota8", "steps", "tile_after"]


def linker(engine, done, base=0):
    count = [0]

    def link(ins):
        count[0] += 1
        ins.then_inc(done, 1)
        engine.wait_ge(done, base + count[0])

    return link, count


def phase_project(nc, io, mem, sem):
    with ExitStack() as ctx:
        sb = lambda n, s, d: ctx.enter_context(nc.sbuf_tensor(n, s, d))
        ps = lambda n, s, d=FP32: ctx.enter_context(nc.psum_tensor(n, s, d))
        xbuf = sb("xbuf", [P, 2, 4, D], FP32)
        xns = sb("xns", [P, 2, 4, D], FP32)
        stats = sb("stats", [P, 2, 4, 6], FP32)
        both = sb("both_stats", [P, 2, 4, 2], FP32)
        diff = sb("diff", [P, 2, 4], FP32)
        diff2 = sb("diff2", [P, 2, 4], FP32)
        mean = sb("mean", [P, 2, 4], FP32)
        var = sb("var", [P, 2, 4], FP32)
        vareps = sb("vareps", [P, 2, 4], FP32)
        std = sb("std", [P, 2, 4], FP32)
        rstd = sb("rstd", [P, 2, 4], FP32)
        xhi = sb("xhi", [P, 2, KT, HALF], FP32R)
        xlo = sb("xlo", [P, 2, KT, HALF], FP32R)
        wqk = sb("wqk", [P, KT, 2 * D], FP32)
        wqk_hi = sb("wqk_hi", [P, KT, 2 * D], FP32R)
        wqk_lo = sb("wqk_lo", [P, KT, 2 * D], FP32R)
        wvr = sb("wvr", [P, KT, D + E], FP32)
        wvr_hi = sb("wvr_hi", [P, KT, D + E], FP32R)
        wvr_lo = sb("wvr_lo", [P, KT, D + E], FP32R)
        bqk = sb("bqk", [P, 4], FP32)
        bv = sb("bv", [P, D], FP32)
        q32 = sb("q32", [P, 4, HALF], FP32)
        rest = sb("rest", [P, 4, HALF], FP32)
        parts = sb("parts", [P, 4, 3, HALF], BF16)
        vpad = sb("vpad", [P, 2, 4, H, VW], FP32)
        bias = sb("bias", [2, TBLEN], FP32)
        bias_rest = sb("bias_rest", [2, TBLEN], FP32)
        bias_parts = sb("bias_parts", [2, 3, TBLEN], BF16)
        gates = sb("gates", [2, 2], FP32)
        sig = sb("sig", [2, 3], FP32)
        tr = ps("tr", [P, KT, HALF])
        qk = ps("qk", [P, 2, HALF])
        vr = ps("vr", [P, 2, HALF])
        block = ctx.enter_context(nc.Block())
        NC = NTOK // HALF

        @block.sync
        def _(sp):
            sp.dma_start(wqk[:], io["w_qk"]).then_inc(sem["weights"], 16)
            sp.dma_start(wvr[:], io["w_vr"]).then_inc(sem["weights"], 16)
            sp.dma_start(bqk[:], io["b_qk"]).then_inc(sem["weights"], 16)
            sp.dma_start(bv[:], io["b_v"].partition_broadcast(P)).then_inc(sem["weights"], 16)
            sp.dma_start(mem["ident"][:], io["ident"]).then_inc(sem["weights"], 16)
            x4 = io["x"].rearrange("(c a p) d -> c p a d", a=4, p=P)

            def load(c, s):
                sp.dma_start(xbuf[:, s], x4[bass.ds(c, 1)].rearrange("c p a d -> (c p) a d"))\
                    .then_inc(sem["x_loaded"][s], 16)

            def store(it, s, more):
                c = it * 2 + s
                sp.wait_ge(sem["xn_ready"], c + (2 + 1))
                if more:
                    load(it * 2 + (2 + s), s)
                sp.dma_start(mem["xn"][:, bass.ds(c * 4, 4), :], xns[:, s]).then_inc(sem["xn_stored"][s], 16)
                for m in range(4):
                    sp.wait_ge(sem["lo_ready"], it * 8 + (4 + 4 * s + m + 1))
                    for g in range(2):
                        sp.dma_start(mem["qk_dram"][bass.ds(it * GU + (2 * (m % 2) + g), 1), m // 2, :, :,
                                                    HALF * s:HALF * s + HALF]
                                     .rearrange("u c r t -> (u r) c t"),
                                     parts[64 * g:64 * g + 64, m]).then_inc(sem["parts_stored"][m], 16)
                sp.wait_ge(sem["vr_used"], it * 8 + (2 + 4 * s + 4))
                for g in range(GU):
                    sp.dma_start(mem["v_dram"][bass.ds(it * GU + g, 1), :, 4 * s:4 * s + 4, :]
                                 .rearrange("u p a w -> (u p) a w"),
                                 vpad[:, s, :, HU * g:HU * g + HU, :].rearrange("p a h w -> p a (h w)"))\
                        .then_inc(sem["v_stored"][s], 16)

            for s in range(2):
                load(s, s)
            with sp.Fori(0, NC // 2 - 1) as it:
                for s in range(2):
                    store(it, s, True)
            sp.wait_ge(sem["bias_stored"], 16)
            loads = bias_tables(mem) + [(mem[n][:], io[n]) for n in CONSTS]
            loads.append((mem["sides"][ROW_FAR:ROW_MAX], io["sides"]))
            for dst, src in loads:
                sp.dma_start(dst, src).then_inc(sem["tables"], 16)
            for s in range(2):
                store(NC // 2 - 1, s, False)
            sp.wait_ge(sem["tables"], 16 * len(loads))
            for s in range(2):
                sp.wait_ge(sem["xn_stored"][s], 16 + 16 * NC // 2)
                sp.wait_ge(sem["v_stored"][s], 64 + 64 * NC // 2)
            for m in range(4):
                sp.wait_ge(sem["parts_stored"][m], 32 + 32 * NC)

        @block.gpsimd
        def _(pool):
            pool.dma_start(gates[:, 0:1], io["et_gate"].partition_broadcast(2)).then_inc(sem["gates_loaded"], 16)
            pool.dma_start(gates[:, 1:2], io["is_gate"].partition_broadcast(2)).then_inc(sem["gates_loaded"], 16)
            pool.dma_start(bias[:], io["time_bias"]).then_inc(sem["bias_loaded"], 16)
            link, _ = linker(pool, sem["bias_chain"])
            pool.wait_ge(sem["bias_loaded"], 16)
            pool.wait_ge(sem["gates_loaded"], 32)
            pool.wait_ge(sem["sig_ready"], 3)
            link(nc.gpsimd.tensor_scalar(bias[:], bias[:], sig[:, 2:3], gates[:, 1:2], ALU.mult, ALU.add))
            link(nc.gpsimd.tensor_scalar(bias[:], bias[:], SCALE_INV, None, ALU.mult))
            link(nc.gpsimd.tensor_copy(bias_parts[:, 0], bias[:]))
            link(nc.gpsimd.tensor_tensor(bias_rest[:], bias[:], bias_parts[:, 0], ALU.subtract))
            link(nc.gpsimd.tensor_copy(bias_parts[:, 1], bias_rest[:]))
            link(nc.gpsimd.tensor_tensor(bias_parts[:, 2], bias_rest[:], bias_parts[:, 1], ALU.subtract))
            pool.dma_start(mem["bias_dram"].rearrange("c s t -> s c t"), bias_parts[:]).then_inc(sem["bias_stored"], 16)
            with pool.Fori(0, NC // 2) as it:
                for s in range(2):
                    for m in range(4):
                        n = it * 8 + (4 * s + m)
                        pool.wait_ge(sem["mid_ready"], n + 1)
                        nc.gpsimd.tensor_tensor(parts[:, m, 2, :], rest[:, m, :], parts[:, m, 1, :],
                                                ALU.subtract).then_inc(sem["lo_ready"], 1)

        @block.scalar
        def _(act):
            act.wait_ge(sem["gates_loaded"], 32)
            nc.scalar.activation(sig[:, 0:1], gates[:, 0:1], ACT.Exp, scale=-1.0).then_inc(sem["sig_ready"], 1)
            act.wait_ge(sem["weights"], 80)
            nc.scalar.activation(wqk_hi[:], wqk[:], ACT.Copy).then_inc(sem["w_hi"], 1)
            nc.scalar.activation(wvr_hi[:], wvr[:], ACT.Copy).then_inc(sem["w_hi"], 1)

            def root(c, s):
                act.wait_ge(sem["var_ready"], c + 1)
                nc.scalar.activation(std[:, s], vareps[:, s], ACT.Sqrt).then_inc(sem["std_ready"], 1)

            def x_hi(c, s):
                act.wait_ge(sem["tr_ready"], c + 1)
                nc.scalar.activation(xhi[:, s], tr[:], ACT.Copy).then_inc(sem["xhi_ready"], 1)

            def chunk(it, s, next1=True, next2=True):
                c = it * 2 + s

                def middle(m):
                    act.wait_ge(sem["rest_ready"], it * 8 + (4 + 4 * s + m + 1))
                    nc.scalar.activation(parts[:, m, 1, :], rest[:, m, :], ACT.Copy)\
                        .then_inc(sem["mid_ready"], 1)

                for m in range(4):
                    n = it * 8 + (4 * s + m)
                    act.wait_ge(sem["qk_ready"], n + 1)
                    act.wait_ge(sem["rest_ready"], n + (4 - 3))
                    act.wait_ge(sem["parts_stored"][m], it * 64 + (32 + 32 * s))
                    nc.scalar.activation(q32[:, m, :], qk[:, m % 2, :], ACT.Identity,
                                         bias=bqk[:, m:m + 1]).then_inc(sem["q32_ready"], 1)
                    act.wait_ge(sem["q32_ready"], n + (2 + 1))
                    nc.scalar.activation(parts[:, m, 0, :], q32[:, m, :], ACT.Copy)\
                        .then_inc(sem["hi_ready"], 1)
                    if m:
                        middle(m - 1)
                    if m == 1 and next1:
                        x_hi(c + 1, 1 - s)
                middle(3)
                if next2:
                    root(c + 2, s)

            root(0, 0)
            root(1, 1)
            x_hi(0, 0)
            with act.Fori(0, NC // 2 - 1) as it:
                for s in range(2):
                    chunk(it, s)
            chunk(NC // 2 - 1, 0, next2=False)
            chunk(NC // 2 - 1, 1, next1=False, next2=False)

        @block.vector
        def _(dve):
            nc.vector.memset(vpad[:], 1.0).then_inc(sem["ones_ready"], 1)
            dve.wait_ge(sem["ones_ready"], 1)
            dve.wait_ge(sem["w_hi"], 2)
            nc.vector.tensor_tensor(wqk_lo[:], wqk[:], wqk_hi[:], ALU.subtract).then_inc(sem["w_lo"], 1)
            nc.vector.tensor_tensor(wvr_lo[:], wvr[:], wvr_hi[:], ALU.subtract).then_inc(sem["w_lo"], 1)

            LINKS = 3

            def statistics(c, s, loaded):
                link, _ = linker(dve, sem["stats_chain"], c * LINKS)
                dve.wait_ge(sem["x_loaded"][s], loaded)
                for a in range(4):
                    last = nc.vector.bn_stats(stats[:, s, a], xbuf[:, s, a])
                link(last)
                even, odd = stats[:, s, :, 1:3], stats[:, s, :, 4:6]
                nc.vector.tensor_tensor(both[:, s], even, odd, ALU.add)
                link(nc.vector.tensor_tensor(diff[:, s], even[:, :, 0], odd[:, :, 0], ALU.subtract))
                nc.vector.tensor_scalar(mean[:, s], both[:, s, :, 0], 0.5, None, ALU.mult)
                nc.vector.tensor_scalar(var[:, s], both[:, s, :, 1], 1.0 / D, EPS, ALU.mult, ALU.add)
                link(nc.vector.scalar_tensor_tensor(out=diff2[:, s], in0=diff[:, s], scalar=0.25,
                                                    in1=diff[:, s], op0=ALU.mult, op1=ALU.mult))
                nc.vector.tensor_tensor(vareps[:, s], var[:, s], diff2[:, s], ALU.add)\
                    .then_inc(sem["var_ready"], 1)

            def normalise(c, s, stored):
                link, _ = linker(dve, sem["root_chain"], c)
                dve.wait_ge(sem["std_ready"], c + 1)
                link(nc.vector.reciprocal(rstd[:, s], std[:, s]))
                dve.wait_ge(sem["xn_stored"][s], stored)
                for a in range(4):
                    last = nc.vector.tensor_scalar(xns[:, s, a], xbuf[:, s, a], mean[:, s, a:a + 1],
                                                   rstd[:, s, a:a + 1], ALU.subtract, ALU.mult)
                last.then_inc(sem["xn_ready"], 1)

            def x_lo(c, s):
                dve.wait_ge(sem["xhi_ready"], c + 1)
                nc.vector.tensor_tensor(xlo[:, s], tr[:], xhi[:, s], ALU.subtract)\
                    .then_inc(sem["xlo_ready"], 1)

            def take_rest(it, s, m):
                n = it * 8 + (4 * s + m)
                dve.wait_ge(sem["hi_ready"], n + 1)
                dve.wait_ge(sem["lo_ready"], n + (4 - 3))
                nc.vector.tensor_tensor(rest[:, m, :], q32[:, m, :], parts[:, m, 0, :],
                                        ALU.subtract).then_inc(sem["rest_ready"], 1)

            def values(it, s, a):
                n = it * 8 + (4 * s + a)
                dve.wait_ge(sem["vr_ready"], n + 1)
                if a == 0:
                    dve.wait_ge(sem["v_stored"][s], it * 64 + 64)
                nc.vector.tensor_tensor(vpad[:, s, a, :, 0:HD],
                                        vr[:, a % 2, 0:D].rearrange("p (h d) -> p h d", h=H),
                                        bv[:].rearrange("p (h d) -> p h d", h=H), ALU.add)
                nc.vector.tensor_scalar(mem["logits"][:, bass.ds(it * 8 + (4 * s + a), 1), :],
                                        vr[:, a % 2:a % 2 + 1, D:D + E], 1.0, None, ALU.mult)\
                    .then_inc(sem["vr_used"], 1)

            def chunk(it, s, next1=True, next2=True):
                c = it * 2 + s
                if next1:
                    normalise(c + 1, 1 - s, it * 16 + 16 * (s + 1))
                take_rest(it, s, 0)
                take_rest(it, s, 1)
                if next1:
                    x_lo(c + 1, 1 - s)
                take_rest(it, s, 2)
                values(it, s, 0)
                take_rest(it, s, 3)
                for a in range(1, 4):
                    values(it, s, a)
                if next2:
                    statistics(c + 2, s, it * 16 + 32)

            statistics(0, 0, 16)
            statistics(1, 1, 16)
            normalise(0, 0, 16)
            dve.wait_ge(sem["sig_ready"], 1)
            nc.vector.tensor_scalar(sig[:, 1:2], sig[:, 0:1], 1.0, None, ALU.add).then_inc(sem["sig_ready"], 1)
            dve.wait_ge(sem["sig_ready"], 2)
            nc.vector.reciprocal(sig[:, 2:3], sig[:, 1:2]).then_inc(sem["sig_ready"], 1)
            x_lo(0, 0)
            with dve.Fori(0, NC // 2 - 1) as it:
                for s in range(2):
                    chunk(it, s)
            chunk(NC // 2 - 1, 0, next2=False)
            chunk(NC // 2 - 1, 1, next1=False, next2=False)

        @block.tensor
        def _(pe):
            for s in range(2):
                pe.sem_inc(sem["xn_stored"][s], 16)
                pe.sem_inc(sem["v_stored"][s], 64)
            pe.sem_inc(sem["xn_ready"], 2)
            for m in range(4):
                pe.sem_inc(sem["parts_stored"][m], 32)
            pe.sem_inc(sem["rest_ready"], 4)
            pe.sem_inc(sem["lo_ready"], 4)
            pe.sem_inc(sem["q32_ready"], 2)
            pe.sem_inc(sem["vr_used"], 2)
            pe.wait_ge(sem["weights"], 80)
            pe.wait_ge(sem["w_lo"], 2)

            def x_T(c, s):
                pe.wait_ge(sem["xn_ready"], c + (2 + 1))
                for a in range(4):
                    for k in range(KT):
                        last = nc.tensor.transpose(tr[:, k, P * a:P * a + P],
                                                   xns[:, s, a, P * k:P * k + P], mem["ident"][:])
                last.then_inc(sem["tr_ready"], 1)

            def chunk(it, s, ahead):
                c = it * 2 + s
                pe.wait_ge(sem["xlo_ready"], c + 1)
                for m in range(4):
                    pe.wait_ge(sem["q32_ready"], it * 8 + (4 * s + m) + (2 - 1))
                    i = 0
                    for k in range(KT):
                        for w, x in ((wqk_hi, xhi), (wqk_hi, xlo), (wqk_lo, xhi)):
                            last = nc.tensor.matmul(qk[:, m % 2, :], w[:, k, P * m:P * m + P], x[:, s, k, :],
                                                    start=(i == 0), stop=(i == 3 * KT - 1))
                            i += 1
                    last.then_inc(sem["qk_ready"], 1)
                    if m == 1 and ahead:
                        x_T(c + 1, 1 - s)
                for a in range(4):
                    pe.wait_ge(sem["vr_used"], it * 8 + (4 * s + a) + (2 - 1))
                    i = 0
                    for k in range(KT):
                        for w, x in ((wvr_hi, xhi), (wvr_hi, xlo), (wvr_lo, xhi)):
                            last = nc.tensor.matmul(vr[:, a % 2, 0:D + E], x[:, s, k, P * a:P * a + P],
                                                    w[:, k, :], start=(i == 0), stop=(i == 3 * KT - 1))
                            i += 1
                    last.then_inc(sem["vr_ready"], 1)

            x_T(0, 0)
            with pe.Fori(0, NC // 2 - 1) as it:
                for s in range(2):
                    chunk(it, s, True)
            chunk(NC // 2 - 1, 0, True)
            chunk(NC // 2 - 1, 1, False)


def bias_tables(mem):
    parts = mem["bias_dram"]
    loads = []
    for j in range(3):
        rows = slice(32 * j, 32 * j + 32)
        rise, fall = parts.offset + 2 * j * TBLEN, parts.offset + (2 * j + 1) * TBLEN
        for first, at in ((0, 32), (2, 96)):
            loads.append((mem["near"][rows, first:first + 2, :],
                          bass.AP(parts.tensor, rise + at, [[1, 32], [-32, 2], [1, 256]])))
        loads.append((mem["near"][rows, 4:8, :],
                      bass.AP(parts.tensor, fall + 96, [[1, 32], [-32, 4], [1, 256]])))
        for side, at in enumerate((TBLEN - 1, 0)):
            loads.append((mem["ends"][ROW_FAR + QT * j:ROW_FAR + QT * j + QT, side:side + 1],
                          bass.AP(parts.tensor, rise + at, [[0, QT], [1, 1]])))
    return loads


def load_stacks(nc, mem, sem, queue, u, buf):
    unit = mem["qk_dram"][bass.ds(u, 1)]
    for stack, which, order in ((mem["qst"], 0, QPART), (mem["kst"], 1, KPART)):
        for g, part in enumerate(order):
            queue.dma_start(stack[HD * g:HD * g + HD, buf],
                            unit[:, which, part].rearrange("u (h d) t -> (u d) h t", d=HD))\
                .then_inc(sem["stack_loaded"][buf], 16)
    queue.dma_start(mem["vst"][:, buf], mem["v_dram"][bass.ds(u, 1)].rearrange("u p a w -> (u p) a w"))\
        .then_inc(sem["stack_loaded"][buf], 16)


def phase_route(nc, io, mem, sem):
    with ExitStack() as ctx:
        sb = lambda n, s, d: ctx.enter_context(nc.sbuf_tensor(n, s, d))
        ps = lambda n, s, d=FP32: ctx.enter_context(nc.psum_tensor(n, s, d))
        ends32 = sb("ends32", [P, 2], FP32)
        far = sb("far", [P, 2, T], FP32)
        far_bf = sb("far_bf", [P, T], BF16)
        lmax = sb("lmax", [P, NT], FP32)
        ex = sb("ex", [P, NT, E], FP32)
        ex2 = sb("ex2", [P, NT, E], FP32)
        ssum = sb("ssum", [P, NT], FP32)
        wsum = sb("wsum", [P, NT], FP32)
        best = sb("best", [P, NT, 8], FP32)
        besti = sb("besti", [P, NT, 8], U32)
        bestf = sb("bestf", [P, NT, 2], FP32)
        both = sb("both", [P, NT, E], BF16)
        ones = sb("ones", [P, P], BF16)
        psum_ex = ps("psum_ex", [P, 512])
        psum_tot = ps("psum_tot", [P, 512])
        block = ctx.enter_context(nc.Block())
        far_rows = slice(ROW_FAR, ROW_MAX)
        onehot = mem["onehot"]

        @block.sync
        def _(sp):
            sp.dma_start(mem["kst"][ROW_FAR:ROWS].rearrange("p b h t -> p (b h) t"),
                         io["key_rows"].unsqueeze(1).to_broadcast([ROWS - ROW_FAR, NBUF * HU, T]))\
                .then_inc(sem["rows_set"], 16)
            sp.wait_ge(sem["far_ready"], 1)
            sp.dma_start(mem["qst"][far_rows].rearrange("p b h t -> p (b h) t"),
                         far_bf[far_rows].unsqueeze(1).to_broadcast([3 * QT, NBUF * HU, T]))\
                .then_inc(sem["rows_set"], 16)
            sp.wait_ge(sem["rows_set"], 32)

        @block.gpsimd
        def _(pool):
            pool.wait_ge(sem["far_begun"], 3)
            nc.gpsimd.tensor_tensor(far_bf[far_rows], far[far_rows, 0], far[far_rows, 1], ALU.add)\
                .then_inc(sem["far_ready"], 1)
            link, _ = linker(pool, sem["far_chain"])
            link(nc.gpsimd.tensor_tensor(mem["near"][:, 1:3], mem["near"][:, 1:3], mem["near_mask"][:], ALU.mult))
            link(nc.gpsimd.memset(mem["zero"], 0.0))

        @block.scalar
        def _(act):
            nc.scalar.activation(ends32[far_rows], mem["ends"][far_rows], ACT.Copy).then_inc(sem["far_begun"], 1)
            act.wait_ge(sem["far_begun"], 1)
            for side in range(2):
                nc.scalar.activation(far[far_rows, side], mem["sides"][far_rows, side], ACT.Copy,
                                     scale=ends32[far_rows, side:side + 1]).then_inc(sem["far_begun"], 1)
            act.wait_ge(sem["ex_ready"], 1)
            nc.scalar.activation(ex2[:], ex[:], ACT.Exp).then_inc(sem["exp_ready"], 1)
            load_stacks(nc, mem, sem, act, 0, 0)
            act.wait_ge(sem["counts_ready"], 1)
            nc.scalar.activation(mem["in_tile"][:].rearrange("p t e -> p (t e)"), psum_ex[:, 0:NT * E], ACT.Copy)
            nc.scalar.activation(mem["tile_sum"][:].rearrange("p t e -> p (t e)"), psum_tot[:, 0:NT * E], ACT.Copy)\
                .then_inc(sem["sums_copied"], 1)
            act.wait_ge(sem["sums_copied"], 1)

        @block.tensor
        def _(pe):
            pe.wait_ge(sem["onehot_ready"], 1)
            pairs = both[:].rearrange("p t e -> p (t e)")
            nc.tensor.matmul(psum_ex[:, 0:NT * E], mem["tri"][:], pairs, start=True, stop=True)
            nc.tensor.matmul(psum_tot[:, 0:NT * E], ones[:], pairs, start=True, stop=True)\
                .then_inc(sem["counts_ready"], 1)

        @block.vector
        def _(dve):
            link, _ = linker(dve, sem["route_chain"])
            logits = mem["logits"]
            link(nc.vector.tensor_reduce(lmax[:], logits[:], AX.X, ALU.max))
            nc.vector.tensor_tensor(ex[:], logits[:], lmax[:].unsqueeze(2).to_broadcast([P, NT, E]), ALU.subtract)\
                .then_inc(sem["ex_ready"], 1)
            link(nc.vector.memset(ones[:], 1.0))
            dve.wait_ge(sem["exp_ready"], 1)
            link(nc.vector.tensor_reduce(ssum[:], ex2[:], AX.X, ALU.add))
            link(nc.vector.reciprocal(wsum[:], ssum[:]))
            link(nc.vector.tensor_tensor(ex[:], ex2[:], wsum[:].unsqueeze(2).to_broadcast([P, NT, E]), ALU.mult))
            for t in range(NT):
                last = nc.vector.max(best[:, t], ex[:, t])
            link(last)
            for t in range(NT):
                last = nc.vector.max_index(besti[:, t], best[:, t], ex[:, t])
            link(last)
            link(nc.vector.tensor_copy(bestf[:], besti[:, :, 0:2]))
            for k in range(TOPK):
                link(nc.vector.tensor_tensor(onehot[:, k], bestf[:, :, k:k + 1].to_broadcast([P, NT, E]),
                                             mem["iota8"][:].unsqueeze(1).to_broadcast([P, NT, E]), ALU.is_equal))
            nc.vector.tensor_tensor(both[:], onehot[:, 0], onehot[:, 1], ALU.add).then_inc(sem["onehot_ready"], 1)
            link(nc.vector.tensor_tensor(ssum[:], best[:, :, 0], best[:, :, 1], ALU.add))
            link(nc.vector.reciprocal(wsum[:], ssum[:]))
            for k in range(TOPK):
                link(nc.vector.tensor_tensor(mem["gate_w"][:, k, :], best[:, :, k], wsum[:], ALU.mult))


def positions(nc, mem, pool, chain):
    link, _ = linker(pool, chain)
    eng = nc.gpsimd
    tot, excl, count, ge, ntile = (mem[n] for n in ("tot", "excl", "count", "ge", "ntile"))
    src, a, d = mem["tile_sum"], 0, 1
    while d < NT:
        dst = tot[:, a]
        link(eng.tensor_copy(dst[:, 0:d], src[:, 0:d]))
        link(eng.tensor_tensor(dst[:, d:NT], src[:, d:NT], src[:, 0:NT - d], ALU.add))
        src, a, d = dst, 1 - a, 2 * d
    link(eng.tensor_copy(count[:], src[:, NT - 1]))
    link(eng.tensor_tensor(excl[:], src, mem["tile_sum"][:], ALU.subtract))
    link(eng.tensor_tensor(ge[:], count[:].unsqueeze(2).to_broadcast([P, E, NT]),
                           mem["steps"][:].unsqueeze(1).to_broadcast([P, E, NT]), ALU.subtract))
    link(eng.tensor_scalar(ge[:], ge[:], 0.0, 1.0, ALU.max, ALU.min))
    w = NT
    while w > 1:
        w //= 2
        link(eng.tensor_tensor(ge[:, :, 0:w], ge[:, :, 0:w], ge[:, :, w:2 * w], ALU.add))
    link(eng.tensor_copy(ntile[:, 0], ge[:, :, 0]))
    a, d = 0, 1
    while d < E:
        link(eng.tensor_copy(ntile[:, 1 - a, 0:d], ntile[:, a, 0:d]))
        link(eng.tensor_tensor(ntile[:, 1 - a, d:E], ntile[:, a, d:E], ntile[:, a, 0:E - d], ALU.add))
        a, d = 1 - a, 2 * d
    tile0 = mem["tile0"]
    link(eng.tensor_tensor(tile0[:], ntile[:, a], ge[:, :, 0], ALU.subtract))
    link(eng.tensor_scalar(tile0[:], tile0[:], float(P), None, ALU.mult))
    link(eng.tensor_tensor(excl[:], excl[:], mem["in_tile"][:], ALU.add))
    link(eng.tensor_tensor(excl[:], excl[:], tile0[:].unsqueeze(1).to_broadcast([P, NT, E]), ALU.add))
    for k in range(TOPK):
        own = mem["onehot"][:, k]
        link(eng.tensor_tensor(own, own, excl[:], ALU.mult))
        w = E
        while w > 1:
            w //= 2
            link(eng.tensor_tensor(own[:, :, 0:w], own[:, :, 0:w], own[:, :, w:2 * w], ALU.add))
        link(eng.tensor_copy(mem["pos"][:, k, :], own[:, :, 0]))
    past = mem["past"]
    link(eng.tensor_tensor(past[:], mem["tile_after"][:].unsqueeze(2).to_broadcast([1, NTILE, E]),
                           ntile[0:1, a, :].unsqueeze(1).to_broadcast([1, NTILE, E]), ALU.subtract))
    link(eng.tensor_scalar(past[:], past[:], 0.0, 1.0, ALU.max, ALU.min))
    w = E
    while w > 1:
        w //= 2
        link(eng.tensor_tensor(past[:, :, 0:w], past[:, :, 0:w], past[:, :, w:2 * w], ALU.add))
    link(eng.tensor_scalar(past[:, :, 0], past[:, :, 0], float(E - 1), None, ALU.min))
    link(eng.tensor_copy(mem["tile_expert"][:], past[:, :, 0]))


def near_queries(i, half):
    lo, hi = max(P * i - REACH, HALF * half), min(P * i + P + REACH, HALF * half + HALF)
    return lo - HALF * half, hi - lo, lo - (P * i - REACH)


def near_keys(j, half, group):
    start = P * (j - 1) if group < 2 else P * j
    lo, hi = max(start, HALF * half), min(start + 2 * P, HALF * half + HALF)
    return lo - HALF * half, hi - lo, lo - start


def phase_attention(nc, io, mem, sem):
    with ExitStack() as ctx:
        sb = lambda n, s, d: ctx.enter_context(nc.sbuf_tensor(n, s, d))
        ps = lambda n, s, d=FP32: ctx.enter_context(nc.psum_tensor(n, s, d))
        qst, kst, vst, near, anti = (mem[n] for n in ("qst", "kst", "vst", "near", "anti"))
        probs = sb("probs", [P, 2, HU, HALF], FP32)
        rowmax = sb("rowmax", [P, 1, HU, QT, 2], FP32)
        negmax = sb("negmax", [P, HU, QT], FP32)
        maxrest = sb("maxrest", [P, HU, QT], FP32)
        maxparts = sb("maxparts", [P, 3, HU, QT], BF16)
        maxT = sb("maxT", [3 * HU * QT, P], BF16)
        ctxu = sb("ctxu", [P, 2, HALF], FP32)
        recip = sb("recip", [P, 2, 4, HU], FP32)
        ctxn = sb("ctxn", [P, 2, 4, HU, HD], FP32)
        sc = ps("sc", [P, 4, HALF])
        sm = ps("sm", [P, 2, HALF])
        pv = ps("pv", [P, HALF])
        misc = ps("misc", [P, HALF])
        miscbf = misc[:].bitcast(BF16)
        block = ctx.enter_context(nc.Block())
        LOADS = 2 * NPAIR + 1
        MAXT_STEP = 13
        ROUNDS = (NU - 2) // NBUF

        @block.sync
        def _(sp):
            def max_rows(count, buf):
                sp.wait_ge(sem["maxT_ready"], count)
                sp.dma_start(qst[ROW_MAX:ROWS, buf].rearrange("p h (j q) -> p (h j) q", q=P),
                             maxT[:]).then_inc(sem["max_rows"][buf], 16)

            def store_ctx(u, half):
                sp.wait_ge(sem["ctxn_ready"], u * 2 + (1 + half + 1))
                for h in range(HU):
                    sp.dma_start(mem["ctx_dram"][bass.ds(u, 1), h, HALF * half:HALF * half + HALF, :]
                                 .rearrange("u (a p) d -> (u p) a d", p=P),
                                 ctxn[:, half, :, h, :]).then_inc(sem["ctx_stored"][half], 16)

            load_stacks(nc, mem, sem, sp, 1, 1)
            max_rows(1, 0)

            def unit(u, r, more):
                sp.wait_ge(sem["ctxT_ready"], u * 2 + 2)
                if more:
                    load_stacks(nc, mem, sem, sp, u + 2, (r + 2) % NBUF)
                store_ctx(u, 0)
                max_rows(u + 2, (r + 1) % NBUF)
                store_ctx(u, 1)

            rounds = (NU - 1) // NBUF
            with sp.Fori(0, rounds - 1) as it:
                for r in range(NBUF):
                    unit(it * NBUF + r, r, True)
            for r in range(NBUF):
                u = (rounds - 1) * NBUF + r
                unit(u, r, u + 2 < NU)
            store_ctx(NU - 1, 0)
            store_ctx(NU - 1, 1)
            for half in range(2):
                sp.wait_ge(sem["ctx_stored"][half], 64 + 64 * NU)

        @block.gpsimd
        def _(pool):
            xs = mem["xs_dram"].rearrange("(c a p) d -> c p a d", a=4, p=P)
            for c in range(NTILE // 4):
                pool.dma_start(xs[c], mem["zero"]).then_inc(sem["zeroed"], 16)
                pool.wait_ge(sem["zeroed"], 16 * c + 16)
            positions(nc, mem, pool, sem["position_chain"])
            for k in range(TOPK):
                for t in range(NT):
                    pool.indirect_dma_start(mem["xs_dram"], bass.IndirectOffsetOnAxis(
                        ap=mem["pos"][:, k, t:t + 1], axis=0), mem["xn"][:, t, :], None)\
                        .then_inc(sem["scattered"], 16)
            pool.wait_ge(sem["scattered"], 16 * TOPK * NT)
            for e in range(2 * E):
                part = slice(e * KT * GUW // 2, (e + 1) * KT * GUW // 2)
                pool.dma_start(mem["w_gu"][:, part], io["w_gu"][:, part]).then_inc(sem["gu_loaded"], 16)
                pool.wait_ge(sem["gu_loaded"], 16 * e + 16)

        def bank_pair(n):
            return (sm[:, 0:2], sc[:, 0:2], sc[:, 2:4])[n % 3]

        def pe_max(pe, base, n, buf, first=False):
            h, j, half = n // (2 * QT), n // 2 % QT, n % 2
            if first:
                bank = bank_pair(n // 2)[:, half]
                if n >= 6:
                    pe.wait_ge(sem["max_taken"], n // 2 * 2 - 4)
            else:
                bank = sm[:, n % 2]
                pe.wait_ge(sem["max_taken"], base + (n - 1))
            parts = [(g, *near_keys(j, half, g)) for g in range(4)]
            parts = [x for x in parts if x[2] > 0]
            last = nc.tensor.matmul(bank, qst[0:ROW_MAX, buf, h, P * j:P * j + P],
                                    kst[0:ROW_MAX, buf, h, HALF * half:HALF * half + HALF],
                                    start=True, stop=not parts, skip_group_check=True)
            for g, at, width, col in parts:
                last = nc.tensor.matmul(bank[32 * g:32 * g + 32, at:at + width], anti[0:96, :],
                                        near[0:96, g, col:col + width], start=False, stop=True,
                                        skip_group_check=True)
            last.then_inc(sem["max_scores"], 1)

        def pe_maxT(pe, count):
            pe.wait_ge(sem["maxparts_ready"], count)
            nc.tensor.transpose(miscbf[0:3 * HU * QT, 0:P], maxparts[:].rearrange("p c h j -> p (c h j)"),
                                mem["ident_bf"][:]).then_inc(sem["maxT_done"], 1)

        def pe_scores(pe, base, step, buf, h):
            half, i = step // QT, step % QT
            at, width, col = near_queries(i, half)
            if h % 2 == 0:
                pe.wait_ge(sem["probs_ready"], base + (2 + 2 * step + h // 2 - 1))
            last = nc.tensor.matmul(sc[:, h, :], kst[0:ROWS, buf, h, P * i:P * i + P],
                                    qst[0:ROWS, buf, h, HALF * half:HALF * half + HALF],
                                    start=True, stop=width <= 0, skip_group_check=True)
            if width > 0:
                for g in range(4):
                    last = nc.tensor.matmul(sc[32 * g:32 * g + 32, h, at:at + width], anti[0:96, :],
                                            near[0:96, 4 + g, col:col + width], start=False, stop=True,
                                            skip_group_check=True)
            if h % 2:
                last.then_inc(sem["scores_ready"], 1)

        def pe_values(pe, base, u, step, buf):
            half, i = step // QT, step % QT
            pe.wait_ge(sem["probs_ready"], base + (2 + 2 * step + 2))
            if i == 0:
                pe.wait_ge(sem["ctxu_ready"], u * 2 + (1 + half))
            for h in range(HU):
                last = nc.tensor.matmul(pv[32 * h:32 * h + 32, :], vst[:, buf, i, 32 * h:32 * h + 32],
                                        probs[:, step % 2, h, :], start=(i == 0), stop=(i == QT - 1),
                                        skip_group_check=True)
            last.then_inc(sem["values_added"], 1)

        def pe_ctxT(pe, u, half):
            pe.wait_ge(sem["ctxu_ready"], u * 2 + (1 + half + 1))
            if half == 0:
                pe.wait_ge(sem["ctxn_ready"], u * 2 + 1)
            else:
                pe.wait_ge(sem["ctxn_ready"], u * 2 + (1 + 1))
            for a in range(4):
                last = nc.tensor.transpose(misc[:, P * a:P * a + P], ctxu[:, half, P * a:P * a + P], mem["ident"][:])
            last.then_inc(sem["ctxT_ready"], 1)

        @block.tensor
        def _(pe):
            pe.sem_inc(sem["probs_ready"], 2)
            pe.sem_inc(sem["values_added"], 2)
            pe.sem_inc(sem["ctxT_ready"], 2)
            pe.sem_inc(sem["ctxu_ready"], 1)
            pe.sem_inc(sem["ctxn_ready"], 1)
            for half in range(2):
                pe.sem_inc(sem["ctx_stored"][half], 64)

            def ring(it, r, ahead, each):
                return (it + (r + ahead) // NBUF) * each + each

            def extra(step):
                return 2 <= step < 10 and step % 2 == 0

            def step_work(u, step, buf, n, max_base, max_buf, maxT=None):
                base = u * (2 * STEPS)
                for h in range(HU):
                    pe_scores(pe, base, step, buf, h)
                    if n < MAXIMA:
                        pe_max(pe, max_base, n, max_buf)
                        n += 1
                    if h == 1 and maxT is not None:
                        pe_maxT(pe, maxT)
                return n

            def head(u, r, it, more):
                n = 0 if more else MAXIMA
                pe.wait_ge(sem["max_rows"][r % NBUF], ring(it, r, 0, 16))
                if more:
                    pe.wait_ge(sem["stack_loaded"][(r + 1) % NBUF], ring(it, r, 1, 16 * LOADS))
                max_base, max_buf = u * MAXIMA + MAXIMA, (r + 1) % NBUF
                first = isinstance(u, int) and u == 0
                for step in range(2):
                    n = step_work(u, step, r % NBUF, n, max_base, max_buf)
                    if step == 0 and not first:
                        pe_values(pe, (u - 1) * (2 * STEPS), u - 1, STEPS - 1, (r - 1) % NBUF)
                    if step == 1:
                        if not first:
                            pe.wait_ge(sem["maxT_ready"], u + 1)
                            pe_ctxT(pe, u - 1, 1)
                        pe_values(pe, u * (2 * STEPS), u, 0, r % NBUF)
                    if n < MAXIMA:
                        pe_max(pe, max_base, n, max_buf)
                        n += 1

            def rest(u, r, ahead):
                n = 2 * (HU + 1) if ahead else MAXIMA
                max_base, max_buf = u * MAXIMA + MAXIMA, (r + 1) % NBUF
                for step in range(2, STEPS):
                    n = step_work(u, step, r, n, max_base, max_buf, u + 2 if step == MAXT_STEP and ahead else None)
                    pe_values(pe, u * (2 * STEPS), u, step - 1, r)
                    for _ in range(1 + extra(step)):
                        if n < MAXIMA:
                            pe_max(pe, max_base, n, max_buf)
                            n += 1
                    if step == 10:
                        pe_ctxT(pe, u, 0)

            pe.wait_ge(sem["stack_loaded"][0], 16 * LOADS)
            for n in range(MAXIMA):
                pe_max(pe, 0, n, 0, first=True)
            pe_maxT(pe, 1)
            head(0, 0, 0, True)
            with pe.Fori(0, ROUNDS) as it:
                for r in range(NBUF):
                    rest(it * NBUF + r, r, True)
                    head(it * NBUF + (r + 1), r + 1, it, True)
            for u in range(NBUF * ROUNDS, NU):
                rest(u, u % NBUF, u + 1 < NU)
                if u + 1 < NU:
                    head(u + 1, (u + 1) % NBUF, (u + 1) // NBUF, u + 2 < NU)
            pe_values(pe, (NU - 1) * (2 * STEPS), NU - 1, STEPS - 1, (NU - 1) % NBUF)
            pe_ctxT(pe, NU - 1, 1)

        @block.scalar
        def _(act):
            def copy_maxT(count):
                act.wait_ge(sem["maxT_done"], count)
                nc.scalar.activation(maxT[:], miscbf[0:3 * HU * QT, 0:P], ACT.Copy).then_inc(sem["maxT_ready"], 1)

            def copy_ctx(u, half):
                act.wait_ge(sem["values_added"], u * STEPS + (2 + QT * (half + 1)))
                nc.scalar.activation(ctxu[:, half, :], pv[:], ACT.Copy).then_inc(sem["ctxu_ready"], 1)

            def exps(u, step, maxT=None):
                for pair in range(2):
                    act.wait_ge(sem["scores_ready"], u * (2 * STEPS) + (2 * step + pair + 1))
                    if pair == 0:
                        act.wait_ge(sem["values_added"], u * STEPS + (2 + step - 1))
                    nc.scalar.activation(probs[:, step % 2, 2 * pair:2 * pair + 2, :],
                                         sc[:, 2 * pair:2 * pair + 2, :], ACT.Exp, scale=1.0 / SCALE_INV)\
                        .then_inc(sem["probs_ready"], 1)
                    if pair == 0 and maxT is not None:
                        copy_maxT(maxT)

            def rest(u, ahead):
                for step in range(2, STEPS):
                    exps(u, step, u + 2 if step == MAXT_STEP and ahead else None)
                    if step == QT:
                        copy_ctx(u, 0)

            def head(u):
                exps(u, 0)
                copy_ctx(u - 1, 1)
                exps(u, 1)

            copy_maxT(1)
            exps(0, 0)
            exps(0, 1)
            with act.Fori(0, ROUNDS) as it:
                for r in range(NBUF):
                    rest(it * NBUF + r, True)
                    head(it * NBUF + (r + 1))
            for u in range(NBUF * ROUNDS, NU):
                rest(u, u + 1 < NU)
                if u + 1 < NU:
                    head(u + 1)
            copy_ctx(NU - 1, 1)

        @block.vector
        def _(dve):
            def take_max(base, n, slot):
                h, j, half = n // (2 * QT), n // 2 % QT, n % 2
                dve.wait_ge(sem["max_scores"], base + (n + 1))
                nc.vector.tensor_reduce(rowmax[:, slot, h, j, half:half + 1], sm[:, n % 2, :], AX.X, ALU.max)\
                    .then_inc(sem["max_taken"], 1)

            def split_max(base, links):
                dve.wait_ge(sem["max_taken"], base + MAXIMA)
                link, made = linker(dve, sem["max_chain"], links)
                link(nc.vector.tensor_reduce(negmax[:], rowmax[:, 0], AX.X, ALU.max, negate=True))
                split3_last(link)
                return made[0]

            def split3_last(link):
                hi, mid, lo = (maxparts[:, j] for j in range(3))
                link(nc.vector.tensor_copy(hi, negmax[:]))
                link(nc.vector.tensor_tensor(maxrest[:], negmax[:], hi, ALU.subtract))
                link(nc.vector.tensor_copy(mid, maxrest[:]))
                nc.vector.tensor_tensor(lo, maxrest[:], mid, ALU.subtract).then_inc(sem["maxparts_ready"], 1)

            def normalise(u, half):
                dve.wait_ge(sem["ctxT_ready"], u * 2 + (2 + half + 1))
                dve.wait_ge(sem["ctx_stored"][half], u * (16 * 4) + 64)
                m = misc[:].rearrange("p (a h w) -> p a h w", a=4, w=VW)
                nc.vector.reciprocal(recip[:, half], m[:, :, :, HD]).then_inc(sem["recip_ready"], 1)
                dve.wait_ge(sem["recip_ready"], u * 2 + (half + 1))
                nc.vector.tensor_tensor(ctxn[:, half], m[:, :, :, 0:HD],
                                        recip[:, half].unsqueeze(3).to_broadcast([P, 4, HU, HD]),
                                        ALU.mult).then_inc(sem["ctxn_ready"], 1)

            LINKS = 4
            HEAD = 2 * (HU + 1)

            def rest(u, ahead):
                if ahead:
                    for n in range(HEAD, MAXIMA):
                        take_max(u * MAXIMA + MAXIMA, n, 0)
                        if n == 60:
                            normalise(u, 0)
                    made = split_max(u * MAXIMA + MAXIMA, u * LINKS + LINKS)
                    assert made == LINKS
                else:
                    normalise(u, 0)

            def head(u, more):
                if more:
                    for n in range(HEAD):
                        take_max(u * MAXIMA + MAXIMA, n, 0)
                normalise(u - 1, 1)

            for n in range(MAXIMA // 2):
                dve.wait_ge(sem["max_scores"], 2 * n + 2)
                nc.vector.tensor_reduce(rowmax[:, 0, n // QT, n % QT, :], bank_pair(n), AX.X, ALU.max)\
                    .then_inc(sem["max_taken"], 2)
            split_max(0, 0)
            for n in range(HEAD):
                take_max(MAXIMA, n, 0)
            with dve.Fori(0, ROUNDS) as it:
                for r in range(NBUF):
                    rest(it * NBUF + r, True)
                    head(it * NBUF + (r + 1), True)
            for u in range(NBUF * ROUNDS, NU):
                rest(u, u + 1 < NU)
                if u + 1 < NU:
                    head(u + 1, u + 2 < NU)
            normalise(NU - 1, 1)


def phase_experts(nc, io, mem, sem):
    with ExitStack() as ctx:
        sb = lambda n, s, d: ctx.enter_context(nc.sbuf_tensor(n, s, d))
        ps = lambda n, s, d=FP32: ctx.enter_context(nc.psum_tensor(n, s, d))
        w_gu = mem["w_gu"]
        w_dn = sb("w_dn", [P, E * NI * D], FP32)
        xs = sb("xs", [P, 2, D], FP32)
        xsT = sb("xsT", [P, 2, KT, P], FP32)
        silu = sb("silu", [P, 2, IC], FP32)
        hid = sb("hid", [P, 2, I], FP32)
        hidT = sb("hidT", [P, NI, P], FP32)
        ys = sb("ys", [P, 2, D], FP32)
        gu = ps("gu", [P, 4, HALF])
        xt = ps("xt", [P, HALF])
        ht = ps("ht", [P, 8, P])
        yp = ps("yp", [P, HALF])
        block = ctx.enter_context(nc.Block())
        PAIRS = (NTILE - 2) // 2
        REM = I - (NI - 1) * P

        @block.sync
        def _(sp):
            dn = w_dn[:].rearrange("p (e i d) -> p e i d", e=E, i=NI)
            sp.dma_start(dn[0:REM, :, NI - 1, :], io["w_dn"][:, (NI - 1) * P:I, :].rearrange("e p d -> p e d"))\
                .then_inc(sem["dn_loaded"], 16)
            for i in range(NI - 1):
                sp.dma_start(dn[:, :, i, :], io["w_dn"][:, i * P:i * P + P, :].rearrange("e p d -> p e d"))\
                    .then_inc(sem["dn_loaded"], 16)

            def load(t, s):
                sp.dma_start(xs[:, s, :], mem["xs_dram"][bass.ds(t * P, P), :]).then_inc(sem["xs_loaded"][s], 16)

            def store(t, s):
                sp.wait_ge(sem["y_ready"], t + 1)
                sp.dma_start(mem["y_dram"][bass.ds(t * P, P), :], ys[:, s, :]).then_inc(sem["y_stored"][s], 16)

            load(0, 0)
            load(1, 1)
            sp.wait_ge(sem["xT_done"], 1)
            load(2, 0)
            with sp.Fori(0, PAIRS - 1) as it:
                for r in range(2):
                    t = it * 2 + (r + 1)
                    sp.wait_ge(sem["xT_done"], t + 1)
                    load(t + 2, (r + 1) % 2)
                    store(t - 1, r)
            for t in range(NTILE - 3, NTILE + 1):
                if t + 2 < NTILE:
                    sp.wait_ge(sem["xT_done"], t + 1)
                    load(t + 2, t % 2)
                store(t - 1, (t - 1) % 2)
            for s in range(2):
                sp.wait_ge(sem["y_stored"][s], 16 + 16 * NTILE // 2)

        @block.tensor
        def _(pe):
            def x_T(s, loaded):
                pe.wait_ge(sem["xs_loaded"][s], loaded)
                for k in range(KT):
                    last = nc.tensor.transpose(xt[:, P * k:P * k + P], xs[:, s, P * k:P * k + P], mem["ident"][:])
                last.then_inc(sem["xT_done"], 1)

            def expert(t):
                return pe.value_load(mem["tile_expert"][0:1, bass.ds(t, 1)], min_val=0, max_val=E - 1)

            def gate_up(t, s, e, first=False):
                pe.wait_ge(sem["xsT_ready"], t + 1)
                for j in range(2):
                    if not first:
                        pe.wait_ge(sem["hid_ready"], t * 2 + (j - 1))
                    for which in range(2):
                        for k in range(KT):
                            last = nc.tensor.matmul(
                                gu[:, 2 * j + which, 0:IC], xsT[:, s, k, :],
                                w_gu[:, bass.ds(e * (KT * GUW) + (k * GUW + which * I + j * IC), IC)],
                                start=(k == 0), stop=(k == KT - 1))
                    last.then_inc(sem["gate_up"], 1)

            def h_T(t, s):
                pe.wait_ge(sem["hid_ready"], t * 2 + 2)
                for i in range(NI):
                    w = min(P, I - P * i)
                    last = nc.tensor.transpose(ht[0:w, i, :], hid[:, s, P * i:P * i + w], mem["ident"][:])
                last.then_inc(sem["hT_done"], 1)

            def down(t, e, first=False):
                pe.wait_ge(sem["hidT_lo"], t + 1)
                pe.wait_ge(sem["hidT_hi"], t + 1)
                if not first:
                    pe.wait_ge(sem["y_ready"], t)
                for i in range(NI):
                    w = min(P, I - P * i)
                    last = nc.tensor.matmul(yp[:, 0:D], hidT[0:w, i, :],
                                            w_dn[0:w, bass.ds(e * (NI * D) + i * D, D)],
                                            start=(i == 0), stop=(i == NI - 1))
                last.then_inc(sem["y_done"], 1)

            for s in range(2):
                pe.sem_inc(sem["y_stored"][s], 16)
            x_T(0, 16)
            gate_up(0, 0, expert(0), first=True)
            x_T(1, 16)
            pe.wait_ge(sem["dn_loaded"], 16 * NI)
            with pe.Fori(0, PAIRS) as it:
                for r in range(2):
                    t = it * 2 + (r + 1)
                    s = (r + 1) % 2
                    h_T(t - 1, r)
                    gate_up(t, s, expert(t))
                    x_T(r, it * 16 + (32 if r == 0 else 32))
                    down(t - 1, expert(t - 1))
            t = NTILE - 1
            h_T(t - 1, 0)
            gate_up(t, 1, expert(t))
            down(t - 1, expert(t - 1))
            h_T(t, 1)
            down(t, expert(t))

        @block.scalar
        def _(act):
            def copy_xT(t, s):
                act.wait_ge(sem["xT_done"], t + 1)
                nc.scalar.activation(xsT[:, s], xt[:, 0:KT * P].rearrange("p (k t) -> p k t", k=KT), ACT.Copy)\
                    .then_inc(sem["xsT_ready"], 1)

            def gate(t, first=False):
                for j in range(2):
                    act.wait_ge(sem["gate_up"], t * 2 + (j + 1))
                    if not first:
                        act.wait_ge(sem["hid_ready"], t * 2 + (j - 1))
                    nc.scalar.activation(silu[:, j, :], gu[:, 2 * j, 0:IC], ACT.Silu).then_inc(sem["silu_ready"], 1)

            def copy_hT(t):
                act.wait_ge(sem["hT_done"], t + 1)
                nc.scalar.activation(hidT[:, 4, :], ht[:, 4, :], ACT.Copy)
                nc.scalar.activation(hidT[0:REM, 5, :], ht[0:REM, 5, :], ACT.Copy).then_inc(sem["hidT_hi"], 1)

            def copy_y(t, s, stored):
                act.wait_ge(sem["y_done"], t + 1)
                act.wait_ge(sem["y_stored"][s], stored)
                nc.scalar.activation(ys[:, s, :], yp[:, 0:D], ACT.Copy).then_inc(sem["y_ready"], 1)

            copy_xT(0, 0)
            gate(0, first=True)
            copy_xT(1, 1)
            with act.Fori(0, PAIRS) as it:
                for r in range(2):
                    t = it * 2 + (r + 1)
                    copy_hT(t - 1)
                    gate(t)
                    copy_xT(t + 1, r)
                    copy_y(t - 1, r, it * 16 + 16)
            t = NTILE - 1
            copy_hT(t - 1)
            gate(t)
            copy_y(t - 1, 0, 16 + 16 * (t - 1) // 2)
            copy_hT(t)
            copy_y(t, 1, 16 + 16 * (t - 1) // 2)

        @block.vector
        def _(dve):
            def copy_hT(t):
                dve.wait_ge(sem["hT_done"], t + 1)
                nc.vector.tensor_copy(hidT[:, 0:4, :], ht[:, 0:4, :]).then_inc(sem["hidT_lo"], 1)

            def hidden(t, s):
                for j in range(2):
                    dve.wait_ge(sem["silu_ready"], t * 2 + (j + 1))
                    nc.vector.tensor_tensor(hid[:, s, j * IC:j * IC + IC], silu[:, j, :], gu[:, 2 * j + 1, 0:IC],
                                            ALU.mult).then_inc(sem["hid_ready"], 1)

            hidden(0, 0)
            with dve.Fori(0, PAIRS) as it:
                for r in range(2):
                    t = it * 2 + (r + 1)
                    copy_hT(t - 1)
                    hidden(t, (r + 1) % 2)
            copy_hT(NTILE - 2)
            hidden(NTILE - 1, 1)
            copy_hT(NTILE - 1)


def phase_combine(nc, io, mem, sem, out):
    with ExitStack() as ctx:
        sb = lambda n, s, d: ctx.enter_context(nc.sbuf_tensor(n, s, d))
        ps = lambda n, s, d=FP32: ctx.enter_context(nc.psum_tensor(n, s, d))
        PAIRS = QT // 2
        wo = sb("wo", [P, KT, D], FP32)
        wo_hi = sb("wo_hi", [P, KT, D], FP32R)
        wo_lo = sb("wo_lo", [P, KT, D], FP32R)
        bo = sb("bo", [P, D], FP32)
        xin = sb("xin", [P, QT, D], FP32)
        cin = sb("cin", [P, QT, D], FP32)
        yin = sb("yin", [P, QT, TOPK, D], FP32)
        chi = sb("chi", [P, 2, KT, P], FP32R)
        clo = sb("clo", [P, 2, KT, P], FP32R)
        acc = sb("acc", [P, 2, 3, D], FP32)
        res = sb("res", [P, QT, D], FP32)
        ct = ps("ct", [P, 2, HALF])
        op = ps("op", [P, 4, HALF])
        x_rows = io["x"].rearrange("(n p) d -> p n d", p=P)
        out_rows = out.rearrange("(n p) d -> p n d", p=P)
        ctx_rows = mem["ctx_dram"].rearrange("(s b g) h (r q) d -> g b h s r (q d)", s=2, b=2, q=HD)
        block = ctx.enter_context(nc.Block())

        @block.sync
        def _(sp):
            sp.dma_start(wo[:], io["w_o"]).then_inc(sem["wo_loaded"], 16)

            def load(g, j):
                pair = slice(2 * j, 2 * j + 2)
                for b in range(2):
                    sp.dma_start(cin[64 * b:64 * b + 64, pair, :],
                                 ctx_rows[bass.ds(g, 1), b, j].rearrange("u s r c -> r (u s) c"))\
                        .then_inc(sem["in_loaded"][j], 16)
                sp.dma_start(xin[:, pair, :], x_rows[:, bass.ds(g * QT + 2 * j, 2), :])\
                    .then_inc(sem["in_loaded"][j], 16)

            def store(g, j):
                sp.wait_ge(sem["res_ready"], g * QT + (2 * j + 2))
                sp.dma_start(out_rows[:, bass.ds(g * QT + 2 * j, 2), :], res[:, 2 * j:2 * j + 2, :])\
                    .then_inc(sem["out_stored"][j], 16)

            for j in range(PAIRS):
                load(0, j)
            with sp.Fori(0, GU - 1) as g:
                for j in range(PAIRS):
                    store(g, j)
                    load(g + 1, j)
            for j in range(PAIRS):
                store(GU - 1, j)
            for j in range(PAIRS):
                sp.wait_ge(sem["out_stored"][j], 16 + 16 * GU)

        @block.gpsimd
        def _(pool):
            for t in range(NT):
                if t >= QT:
                    pool.wait_ge(sem["res_ready"], t - QT + 1)
                for k in range(TOPK):
                    pool.indirect_dma_start(yin[:, t % QT, k, :], None, mem["y_dram"], bass.IndirectOffsetOnAxis(
                        ap=mem["pos"][:, k, t:t + 1], axis=0)).then_inc(sem["y_gathered"][t % QT], 16)

        @block.tensor
        def _(pe):
            pe.sem_inc(sem["proj_used"], 4)
            pe.sem_inc(sem["proj_done"], 2)
            for j in range(PAIRS):
                pe.sem_inc(sem["out_stored"][j], 16)

            def transposes(g, tt):
                pe.wait_ge(sem["in_loaded"][tt // 2], g * 48 + 48)
                for k in range(KT):
                    last = nc.tensor.transpose(ct[:, tt % 2, P * k:P * k + P], cin[:, tt, P * k:P * k + P],
                                               mem["ident"][:])
                last.then_inc(sem["ct_done"], 1)

            def product(g, tt):
                t = g * QT + tt
                pe.wait_ge(sem["proj_used"], t + 1)
                pe.wait_ge(sem["clo_ready"], t + 1)
                i = 0
                for k in range(KT):
                    for c, w in ((chi, wo_hi), (clo, wo_hi), (chi, wo_lo)):
                        last = nc.tensor.matmul(op[:, tt % 4, 0:D], c[:, tt % 2, k, :], w[:, k, :],
                                                start=(i == 0), stop=(i == 3 * KT - 1))
                        i += 1
                last.then_inc(sem["proj_done"], 1)

            transposes(0, 0)
            pe.wait_ge(sem["wo_split"], 2)
            with pe.Fori(0, GU - 1) as g:
                for tt in range(QT):
                    if tt < QT - 1:
                        transposes(g, tt + 1)
                    else:
                        transposes(g + 1, 0)
                    product(g, tt)
            for tt in range(QT):
                if tt < QT - 1:
                    transposes(GU - 1, tt + 1)
                product(GU - 1, tt)

        @block.scalar
        def _(act):
            act.dma_start(bo[:], io["b_o"].partition_broadcast(P)).then_inc(sem["bo_loaded"], 16)
            act.wait_ge(sem["wo_loaded"], 16)
            nc.scalar.activation(wo_hi[:], wo[:], ACT.Copy).then_inc(sem["wo_split"], 1)

            with act.Fori(0, GU) as g:
                for tt in range(QT):
                    t = g * QT + tt
                    act.wait_ge(sem["proj_done"], t + 1)
                    act.wait_ge(sem["ct_done"], t + 1)
                    nc.scalar.activation(chi[:, tt % 2], ct[:, tt % 2, 0:KT * P].rearrange("p (k t) -> p k t", k=KT),
                                         ACT.Copy).then_inc(sem["chi_ready"], 1)

        @block.vector
        def _(dve):
            def split(g, tt):
                t = g * QT + tt
                dve.wait_ge(sem["chi_ready"], t + 1)
                nc.vector.tensor_tensor(clo[:, tt % 2], ct[:, tt % 2, 0:KT * P].rearrange("p (k t) -> p k t", k=KT),
                                        chi[:, tt % 2], ALU.subtract).then_inc(sem["clo_ready"], 1)

            def sums(g, tt):
                t, s, j = g * QT + tt, tt % 2, tt // 2
                dve.wait_ge(sem["in_loaded"][j], g * 48 + 48)
                nc.vector.tensor_tensor(acc[:, s, 0], xin[:, tt, :], bo[:], ALU.add).then_inc(sem["x_added"], 1)
                dve.wait_ge(sem["x_added"], t + 1)
                dve.wait_ge(sem["proj_done"], t + (2 + 1))
                nc.vector.tensor_tensor(acc[:, s, 1], acc[:, s, 0], op[:, tt % 4, 0:D], ALU.add)\
                    .then_inc(sem["proj_used"], 1)
                dve.wait_ge(sem["proj_used"], t + (4 + 1))
                dve.wait_ge(sem["y_gathered"][tt], g * 32 + 32)
                nc.vector.scalar_tensor_tensor(out=acc[:, s, 2], in0=yin[:, tt, 0, :],
                                               scalar=mem["gate_w"][:, 0, bass.ds(t, 1)],
                                               in1=acc[:, s, 1], op0=ALU.mult, op1=ALU.add)\
                    .then_inc(sem["y_added"], 1)
                dve.wait_ge(sem["y_added"], t + 1)
                dve.wait_ge(sem["out_stored"][j], g * 16 + 16)
                nc.vector.scalar_tensor_tensor(out=res[:, tt, :], in0=yin[:, tt, 1, :],
                                               scalar=mem["gate_w"][:, 1, bass.ds(t, 1)],
                                               in1=acc[:, s, 2], op0=ALU.mult, op1=ALU.add)\
                    .then_inc(sem["res_ready"], 1)

            dve.wait_ge(sem["wo_split"], 1)
            nc.vector.tensor_tensor(wo_lo[:], wo[:], wo_hi[:], ALU.subtract).then_inc(sem["wo_split"], 1)
            dve.wait_ge(sem["bo_loaded"], 16)
            split(0, 0)
            with dve.Fori(0, GU - 1) as g:
                for tt in range(QT):
                    if tt < QT - 1:
                        split(g, tt + 1)
                    else:
                        split(g + 1, 0)
                    sums(g, tt)
            for tt in range(QT):
                if tt < QT - 1:
                    split(GU - 1, tt + 1)
                sums(GU - 1, tt)


SEMS = """weights w_hi w_lo ones_ready xn_ready rest_ready lo_ready q32_ready vr_used var_ready std_ready
tr_ready xhi_ready xlo_ready qk_ready hi_ready mid_ready vr_ready stats_chain root_chain
gates_loaded bias_loaded bias_chain bias_stored sig_ready
tables rows_set far_ready far_begun far_chain zeroed ex_ready exp_ready onehot_ready counts_ready sums_copied route_chain position_chain
scattered gu_loaded max_scores max_taken maxparts_ready maxT_done maxT_ready scores_ready probs_ready values_added
ctxu_ready ctxT_ready ctxn_ready recip_ready max_chain
dn_loaded xT_done xsT_ready gate_up silu_ready hid_ready hT_done hidT_lo hidT_hi y_done y_ready
wo_loaded bo_loaded wo_split ct_done chi_ready clo_ready proj_done proj_used x_added y_added res_ready""".split()
SEM_RINGS = {"x_loaded": 2, "xn_stored": 2, "parts_stored": 4, "v_stored": 2, "stack_loaded": NBUF, "max_rows": NBUF,
             "ctx_stored": 2, "xs_loaded": 2, "y_stored": 2, "in_loaded": 4, "y_gathered": QT, "out_stored": 4}


def build(nc, io, out):
    with ExitStack() as ctx:
        sb = lambda n, s, d: ctx.enter_context(nc.sbuf_tensor(n, s, d))
        dram = lambda n, s, d: nc.dram_tensor(n, s, d, kind="Internal").ap()
        sem = {n: ctx.enter_context(nc.semaphore(n)) for n in SEMS}
        for n, k in SEM_RINGS.items():
            sem[n] = [ctx.enter_context(nc.semaphore(f"{n}{i}")) for i in range(k)]
        mem = {
            "qk_dram": dram("qk_dram", (NU, 2, 3, HU * HD, T), BF16),
            "v_dram": dram("v_dram", (NU, P, QT, P), FP32),
            "ctx_dram": dram("ctx_dram", (NU, HU, T, HD), FP32),
            "xs_dram": dram("xs_dram", (NPOS, D), FP32),
            "bias_dram": dram("bias_dram", (3, 2, TBLEN), BF16),
            "y_dram": dram("y_dram", (NPOS, D), FP32),
            "ident": sb("ident", [P, P], FP32),
            "pos": sb("pos", [P, TOPK, NT], I32),
            "gate_w": sb("gate_w", [P, TOPK, NT], FP32),
            "tile_expert": sb("tile_expert", [1, NTILE], I32),
            "logits": sb("logits", [P, NT, E], FP32),
            "w_gu": sb("w_gu", [P, E * KT * GUW], FP32),
        }
        mem["xn"] = mem["w_gu"][:, 0:NT * D].rearrange("p (t d) -> p t d", d=D)
        mem["zero"] = mem["w_gu"][:, NT * D:(NT + 4) * D].rearrange("p (a d) -> p a d", d=D)
        with ExitStack() as shared:
            def keep(tensors):
                for n, s, d in tensors:
                    mem[n] = shared.enter_context(nc.sbuf_tensor(n, s, d))

            keep([("near", [96, 8, 256], BF16), ("near_mask", [96, 2, 256], BF16), ("anti", [96, 32], BF16),
                  ("ident_bf", [P, P], BF16), ("tri", [P, P], BF16), ("sides", [P, 2, T], BF16),
                  ("ends", [P, 2], BF16), ("iota8", [P, E], FP32), ("steps", [P, NT], FP32),
                  ("tile_after", [1, NTILE], FP32)])
            phase_project(nc, io, mem, sem)
            keep([("qst", [P, NBUF, HU, T], BF16), ("kst", [P, NBUF, HU, T], BF16), ("vst", [P, NBUF, QT, P], FP32),
                  ("onehot", [P, TOPK, NT, E], FP32), ("in_tile", [P, NT, E], FP32), ("tile_sum", [P, NT, E], FP32),
                  ("tot", [P, 2, NT, E], FP32), ("excl", [P, NT, E], FP32), ("count", [P, E], FP32),
                  ("ge", [P, E, NT], FP32), ("ntile", [P, 2, E], FP32), ("tile0", [P, E], FP32),
                  ("past", [1, NTILE, E], FP32)])
            phase_route(nc, io, mem, sem)
            phase_attention(nc, io, mem, sem)
        phase_experts(nc, io, mem, sem)
        phase_combine(nc, io, mem, sem, out)


def constants():
    def bf16_bits(ones):
        return np.where(ones != 0, 0x3F80, 0).astype(np.uint16)

    c = {}
    c["ident"] = np.eye(P, dtype=np.float32)
    c["ident_bf"] = bf16_bits(np.eye(P))
    c["anti"] = bf16_bits(np.tile(np.eye(32)[::-1], (3, 1)))
    c["tri"] = bf16_bits(np.triu(np.ones((P, P)), 1))
    c["iota8"] = np.tile(np.arange(E, dtype=np.float32), (P, 1))
    c["steps"] = np.tile(np.arange(NT, dtype=np.float32) * P, (P, 1))
    c["tile_after"] = np.arange(1, NTILE + 1, dtype=np.float32)[None]
    t = np.arange(T)
    rows = np.zeros((ROWS - ROW_FAR, T), np.float32)
    sides = np.zeros((3 * QT, 2, T), np.float32)
    for p in range(3):
        for i in range(QT):
            rows[QT * p + i] = (t // P == i)
            sides[QT * p + i, 0] = t < P * i - REACH
            sides[QT * p + i, 1] = t >= P * i + P + REACH
    rows[3 * QT:] = 1
    c["key_rows"] = bf16_bits(rows)
    c["sides"] = bf16_bits(sides)
    mask = np.ones((3, 32, 2, 256), np.float32)
    mask[:, 0:2, 0, 0:P] = 0
    mask[:, 30:32, 1, P:] = 0
    c["near_mask"] = bf16_bits(mask.reshape(96, 2, 256))
    return c


def kernel(L0_attn_x, L0_attn_Wq, L0_attn_bq, L0_attn_Wk, L0_attn_bk, L0_attn_Wv, L0_attn_bv, L0_attn_Wo,
           L0_attn_bo, L0_attn_et_gate, L0_attn_is_gate, L0_attn_time_bias, L0_ffn_w_router, L0_ffn_w_gate,
           L0_ffn_w_up, L0_ffn_w_down):
    import concourse.bacc as bacc
    from concourse.bass_utils import run_bass_kernel_spmd

    a = np.asarray
    tiles = lambda w: np.ascontiguousarray(w.reshape(KT, P, -1).transpose(1, 0, 2))
    tb = a(L0_attn_time_bias).reshape(TB)
    arrays = dict(constants())
    arrays["x"] = np.ascontiguousarray(a(L0_attn_x).reshape(NTOK, D))
    arrays["w_qk"] = tiles(np.concatenate([a(L0_attn_Wq).T, a(L0_attn_Wk).T], axis=1))
    arrays["w_vr"] = tiles(np.concatenate([a(L0_attn_Wv).T, a(L0_ffn_w_router).T], axis=1))
    arrays["w_o"] = tiles(a(L0_attn_Wo).T)
    arrays["b_qk"] = np.ascontiguousarray(np.concatenate([a(L0_attn_bq), a(L0_attn_bk)]).reshape(4, P).T)
    arrays["b_v"] = a(L0_attn_bv).reshape(1, D)
    arrays["b_o"] = a(L0_attn_bo).reshape(1, D)
    arrays["et_gate"] = a(L0_attn_et_gate).reshape(1, 1)
    arrays["is_gate"] = a(L0_attn_is_gate).reshape(1, 1)
    arrays["time_bias"] = np.stack([np.pad(tb, (129, TBLEN - 129 - TB), mode="edge"),
                                    np.pad(tb[::-1], (127, TBLEN - 127 - TB), mode="edge")])
    gu = np.concatenate([a(L0_ffn_w_gate), a(L0_ffn_w_up)], axis=1).transpose(0, 2, 1)
    arrays["w_gu"] = np.ascontiguousarray(gu.reshape(E, KT, P, GUW).transpose(2, 0, 1, 3).reshape(P, -1))
    arrays["w_dn"] = np.ascontiguousarray(a(L0_ffn_w_down).transpose(0, 2, 1))

    nc = bacc.Bacc("TRN2", target_bir_lowering=False, num_devices=1)
    io = {n: nc.dram_tensor(n + "_in", v.shape, mybir.dt.from_np(v.dtype), kind="ExternalInput").ap()
          for n, v in arrays.items()}
    for n, v in arrays.items():
        if v.dtype == np.uint16:
            io[n] = io[n].bitcast(BF16)
    out = nc.dram_tensor("out", (NTOK, D), FP32, kind="ExternalOutput").ap()
    build(nc, io, out)
    r = run_bass_kernel_spmd(nc, [{n + "_in": v for n, v in arrays.items()}], core_ids=[0])
    return r.results[0]["out"].reshape(B, T, D)
```

```python
from contextlib import ExitStack

import numpy as np
import concourse.bass as bass
import concourse.mybir as mybir

FP32 = mybir.dt.float32
FP32R = mybir.dt.float32r
BF16 = mybir.dt.bfloat16
I32 = mybir.dt.int32
U32 = mybir.dt.uint32
ALU = mybir.AluOpType
ACT = mybir.ActivationFunctionType
AX = mybir.AxisListType

P = 128
B, T, D = 4, 1024, 256
H, HD = 16, 16
NTOK = B * T
NT = NTOK // P
E, I, TOPK = 8, 704, 2
TB = 125
REACH = TB // 2
KT = D // P
EPS = 1e-5

HU = 4
GU = H // HU
NU = B * GU
QT = T // P
HALF = 512
VW = 32
NPAIR = 6
QPART = [0, 0, 0, 1, 1, 2]
KPART = [0, 1, 2, 0, 1, 0]
ROW_FAR = NPAIR * HD
ROW_MAX = ROW_FAR + 3 * QT
ROWS = ROW_MAX + 3
NBUF = 3
MAXIMA = HU * QT * 2
STEPS = 2 * QT
SCALE_INV = 4.0

NTILE = NT * TOPK + E - 1
NPOS = (NTILE + 1) * P
IC = 352
NI = (I + P - 1) // P
REM = I - (NI - 1) * P
GUW = 2 * I
TBLEN = 384
CONSTS = ["near_mask", "anti", "ident_bf", "tri", "iota8", "steps", "tile_after", "token_rows"]


def linker(engine, done, base=0):
    count = [0]

    def link(ins):
        count[0] += 1
        ins.then_inc(done, 1)
        engine.wait_ge(done, base + count[0])

    return link, count


def phase_project(nc, io, mem, sem):
    with ExitStack() as ctx:
        sb = lambda n, s, d: ctx.enter_context(nc.sbuf_tensor(n, s, d))
        ps = lambda n, s, d=FP32: ctx.enter_context(nc.psum_tensor(n, s, d))
        xbuf = sb("xbuf", [P, 2, 4, D], FP32)
        xns = sb("xns", [P, 2, 4, D], FP32)
        stats = sb("stats", [P, 2, 4, 6], FP32)
        both = sb("both_stats", [P, 2, 4, 2], FP32)
        diff = sb("diff", [P, 2, 4], FP32)
        diff2 = sb("diff2", [P, 2, 4], FP32)
        mean = sb("mean", [P, 2, 4], FP32)
        var = sb("var", [P, 2, 4], FP32)
        vareps = sb("vareps", [P, 2, 4], FP32)
        std = sb("std", [P, 2, 4], FP32)
        rstd = sb("rstd", [P, 2, 4], FP32)
        xhi = sb("xhi", [P, 2, KT, HALF], FP32R)
        xlo = sb("xlo", [P, 2, KT, HALF], FP32R)
        wqk = sb("wqk", [P, KT, 2 * D], FP32)
        wqk_hi = sb("wqk_hi", [P, KT, 2 * D], FP32R)
        wqk_lo = sb("wqk_lo", [P, KT, 2 * D], FP32R)
        wvr = sb("wvr", [P, KT, D + E], FP32)
        wvr_hi = sb("wvr_hi", [P, KT, D + E], FP32R)
        wvr_lo = sb("wvr_lo", [P, KT, D + E], FP32R)
        bqk = sb("bqk", [P, 4], FP32)
        bv = sb("bv", [P, D], FP32)
        q32 = sb("q32", [P, 4, HALF], FP32)
        rest = sb("rest", [P, 4, HALF], FP32)
        parts = sb("parts", [P, 4, 3, HALF], BF16)
        vpad = sb("vpad", [P, 2, 4, H, VW], FP32)
        bias = sb("bias", [2, TBLEN], FP32)
        bias_rest = sb("bias_rest", [2, TBLEN], FP32)
        bias_parts = sb("bias_parts", [2, 3, TBLEN], BF16)
        gates = sb("gates", [2, 2], FP32)
        sig = sb("sig", [2, 3], FP32)
        tr = ps("tr", [P, KT, HALF])
        qk = ps("qk", [P, 2, HALF])
        vr = ps("vr", [P, 2, HALF])
        block = ctx.enter_context(nc.Block())
        NC = NTOK // HALF

        @block.sync
        def _(sp):
            x4 = io["x"].rearrange("(c a p) d -> c p a d", a=4, p=P)

            def load(c, s):
                sp.dma_start(xbuf[:, s], x4[bass.ds(c, 1)].rearrange("c p a d -> (c p) a d"))\
                    .then_inc(sem["x_loaded"][s], 16)

            def store(it, s, more, tables=()):
                c = it * 2 + s
                sp.wait_ge(sem["xn_ready"], c + (2 + 1))
                sp.dma_start(mem["xn"][:, bass.ds(c * 4, 4), :], xns[:, s]).then_inc(sem["xn_stored"][s], 16)
                for m in range(4):
                    sp.wait_ge(sem["lo_ready"], it * 8 + (4 + 4 * s + m + 1))
                    sp.dma_start(mem["qk_dram"][m // 2, :, bass.ds(it * D + P * (m % 2), P), HALF * s:HALF * s + HALF]
                                 .rearrange("c r t -> r c t"), parts[:, m]).then_inc(sem["parts_stored"][m], 16)
                    if m == 0 and more:
                        sp.wait_ge(sem["xn_ready"], c + (2 + 2))
                        load(it * 2 + (3 + s), 1 - s)
                    for dst, src in tables[m::4]:
                        sp.dma_start(dst, src).then_inc(sem["tables"], 16)
                sp.wait_ge(sem["vr_used"], it * 8 + (2 + 4 * s + 4))
                sp.dma_start(mem["v_dram"][:, 4 * s:4 * s + 4, bass.ds(it * GU, GU), :]
                             .rearrange("p a u w -> p a (u w)"),
                             vpad[:, s].rearrange("p a h w -> p a (h w)")).then_inc(sem["v_stored"][s], 16)

            load(0, 0)
            sp.dma_start(mem["ident"][:], io["ident"]).then_inc(sem["ident_loaded"], 16)
            sp.dma_start(wqk[:], io["w_qk"]).then_inc(sem["weights"], 16)
            sp.dma_start(wvr[:], io["w_vr"]).then_inc(sem["weights"], 16)
            sp.dma_start(bqk[:], io["b_qk"]).then_inc(sem["weights"], 16)
            sp.dma_start(bv[:], io["b_v"].partition_broadcast(P)).then_inc(sem["weights"], 16)
            load(1, 1)
            consts = [(mem[n][:], io[n]) for n in CONSTS] + [(mem["sides"][ROW_FAR:ROW_MAX], io["sides"])]
            for dst, src in consts:
                sp.dma_start(dst, src).then_inc(sem["tables"], 16)
            sp.wait_ge(sem["xn_ready"], 2 + 1)
            load(2, 0)
            with sp.Fori(0, NC // 2 - 2) as it:
                for s in range(2):
                    store(it, s, True)
            for s in range(2):
                store(NC // 2 - 2, s, s == 0)
            sp.wait_ge(sem["bias_stored"], 16)
            tables = bias_tables(mem)
            store(NC // 2 - 1, 0, False, tables)
            store(NC // 2 - 1, 1, False)
            sp.wait_ge(sem["tables"], 16 * (len(tables) + len(consts)))
            for s in range(2):
                sp.wait_ge(sem["xn_stored"][s], 16 + 16 * NC // 2)
                sp.wait_ge(sem["v_stored"][s], 16 + 16 * NC // 2)
            for m in range(4):
                sp.wait_ge(sem["parts_stored"][m], 16 + 16 * NC)

        @block.gpsimd
        def _(pool):
            pool.dma_start(gates[:, 0:1], io["et_gate"].partition_broadcast(2)).then_inc(sem["gates_loaded"], 16)
            pool.dma_start(gates[:, 1:2], io["is_gate"].partition_broadcast(2)).then_inc(sem["gates_loaded"], 16)
            pool.dma_start(bias[:], io["time_bias"]).then_inc(sem["bias_loaded"], 16)
            nc.gpsimd.memset(vpad[:], 1.0).then_inc(sem["ones_ready"], 1)
            link, _ = linker(pool, sem["bias_chain"])
            pool.wait_ge(sem["bias_loaded"], 16)
            pool.wait_ge(sem["gates_loaded"], 32)
            pool.wait_ge(sem["sig_ready"], 3)
            link(nc.gpsimd.tensor_scalar(bias[:], bias[:], sig[:, 2:3], gates[:, 1:2], ALU.mult, ALU.add))
            link(nc.gpsimd.tensor_scalar(bias[:], bias[:], SCALE_INV, None, ALU.mult))
            link(nc.gpsimd.tensor_copy(bias_parts[:, 0], bias[:]))
            link(nc.gpsimd.tensor_tensor(bias_rest[:], bias[:], bias_parts[:, 0], ALU.subtract))
            link(nc.gpsimd.tensor_copy(bias_parts[:, 1], bias_rest[:]))
            link(nc.gpsimd.tensor_tensor(bias_parts[:, 2], bias_rest[:], bias_parts[:, 1], ALU.subtract))
            pool.dma_start(mem["bias_dram"].rearrange("c s t -> s c t"), bias_parts[:]).then_inc(sem["bias_stored"], 16)
            with pool.Fori(0, NC // 2) as it:
                for s in range(2):
                    for m in range(4):
                        n = it * 8 + (4 * s + m)
                        pool.wait_ge(sem["mid_ready"], n + 1)
                        nc.gpsimd.tensor_tensor(parts[:, m, 2, :], rest[:, m, :], parts[:, m, 1, :],
                                                ALU.subtract).then_inc(sem["lo_ready"], 1)

        @block.scalar
        def _(act):
            def root(c, s):
                act.wait_ge(sem["var_ready"], c + 1)
                nc.scalar.activation(std[:, s], vareps[:, s], ACT.Sqrt).then_inc(sem["std_ready"], 1)

            def x_hi(c, s):
                act.wait_ge(sem["tr_ready"], c + 1)
                nc.scalar.activation(xhi[:, s], tr[:], ACT.Copy).then_inc(sem["xhi_ready"], 1)

            def chunk(it, s, next1=True, next2=True):
                c = it * 2 + s

                def middle(m):
                    act.wait_ge(sem["rest_ready"], it * 8 + (4 + 4 * s + m + 1))
                    nc.scalar.activation(parts[:, m, 1, :], rest[:, m, :], ACT.Copy)\
                        .then_inc(sem["mid_ready"], 1)

                for m in range(4):
                    n = it * 8 + (4 * s + m)
                    act.wait_ge(sem["qk_ready"], n + 1)
                    act.wait_ge(sem["rest_ready"], n + (4 - 3))
                    act.wait_ge(sem["parts_stored"][m], it * 32 + (16 + 16 * s))
                    nc.scalar.activation(q32[:, m, :], qk[:, m % 2, :], ACT.Identity,
                                         bias=bqk[:, m:m + 1]).then_inc(sem["q32_ready"], 1)
                    act.wait_ge(sem["q32_ready"], n + (2 + 1))
                    nc.scalar.activation(parts[:, m, 0, :], q32[:, m, :], ACT.Copy)\
                        .then_inc(sem["hi_ready"], 1)
                    if m:
                        middle(m - 1)
                    if m == 1 and next1:
                        x_hi(c + 1, 1 - s)
                middle(3)
                if next2:
                    root(c + 2, s)

            root(0, 0)
            act.wait_ge(sem["weights"], 64)
            nc.scalar.activation(wqk_hi[:], wqk[:], ACT.Copy).then_inc(sem["w_hi"], 1)
            nc.scalar.activation(wvr_hi[:], wvr[:], ACT.Copy).then_inc(sem["w_hi"], 1)
            x_hi(0, 0)
            act.wait_ge(sem["gates_loaded"], 32)
            nc.scalar.activation(sig[:, 0:1], gates[:, 0:1], ACT.Exp, scale=-1.0).then_inc(sem["sig_ready"], 1)
            root(1, 1)
            with act.Fori(0, NC // 2 - 1) as it:
                for s in range(2):
                    chunk(it, s)
            chunk(NC // 2 - 1, 0, next2=False)
            chunk(NC // 2 - 1, 1, next1=False, next2=False)

        @block.vector
        def _(dve):
            LINKS = 3

            def raw_stats(c, s, loaded):
                dve.wait_ge(sem["x_loaded"][s], loaded)
                for a in range(4):
                    last = nc.vector.bn_stats(stats[:, s, a], xbuf[:, s, a])
                last.then_inc(sem["stats_chain"], 1)

            def statistics(c, s):
                dve.wait_ge(sem["stats_chain"], c * LINKS + 1)
                link, _ = linker(dve, sem["stats_chain"], c * LINKS + 1)
                even, odd = stats[:, s, :, 1:3], stats[:, s, :, 4:6]
                nc.vector.tensor_tensor(both[:, s], even, odd, ALU.add)
                link(nc.vector.tensor_tensor(diff[:, s], even[:, :, 0], odd[:, :, 0], ALU.subtract))
                nc.vector.tensor_scalar(mean[:, s], both[:, s, :, 0], 0.5, None, ALU.mult)
                nc.vector.tensor_scalar(var[:, s], both[:, s, :, 1], 1.0 / D, EPS, ALU.mult, ALU.add)
                link(nc.vector.scalar_tensor_tensor(out=diff2[:, s], in0=diff[:, s], scalar=0.25,
                                                    in1=diff[:, s], op0=ALU.mult, op1=ALU.mult))
                nc.vector.tensor_tensor(vareps[:, s], var[:, s], diff2[:, s], ALU.add)\
                    .then_inc(sem["var_ready"], 1)

            def normalise(c, s, stored):
                link, _ = linker(dve, sem["root_chain"], c)
                dve.wait_ge(sem["std_ready"], c + 1)
                link(nc.vector.reciprocal(rstd[:, s], std[:, s]))
                dve.wait_ge(sem["xn_stored"][s], stored)
                for a in range(4):
                    last = nc.vector.tensor_scalar(xns[:, s, a], xbuf[:, s, a], mean[:, s, a:a + 1],
                                                   rstd[:, s, a:a + 1], ALU.subtract, ALU.mult)
                last.then_inc(sem["xn_ready"], 1)

            def x_lo(c, s):
                dve.wait_ge(sem["xhi_ready"], c + 1)
                nc.vector.tensor_tensor(xlo[:, s], tr[:], xhi[:, s], ALU.subtract)\
                    .then_inc(sem["xlo_ready"], 1)

            def take_rest(it, s, m):
                n = it * 8 + (4 * s + m)
                dve.wait_ge(sem["hi_ready"], n + 1)
                dve.wait_ge(sem["lo_ready"], n + (4 - 3))
                nc.vector.tensor_tensor(rest[:, m, :], q32[:, m, :], parts[:, m, 0, :],
                                        ALU.subtract).then_inc(sem["rest_ready"], 1)

            def values(it, s, a):
                n = it * 8 + (4 * s + a)
                dve.wait_ge(sem["vr_ready"], n + 1)
                if a == 0:
                    dve.wait_ge(sem["v_stored"][s], it * 16 + 16)
                nc.vector.tensor_tensor(vpad[:, s, a, :, 0:HD],
                                        vr[:, a % 2, 0:D].rearrange("p (h d) -> p h d", h=H),
                                        bv[:].rearrange("p (h d) -> p h d", h=H), ALU.add)
                nc.vector.tensor_scalar(mem["logits"][:, bass.ds(it * 8 + (4 * s + a), 1), :],
                                        vr[:, a % 2:a % 2 + 1, D:D + E], 1.0, None, ALU.mult)\
                    .then_inc(sem["vr_used"], 1)

            def chunk(it, s, next1=True, next2=True):
                c = it * 2 + s
                if next1:
                    normalise(c + 1, 1 - s, it * 16 + 16 * (s + 1))
                take_rest(it, s, 0)
                if next2:
                    raw_stats(c + 2, s, it * 16 + 32)
                take_rest(it, s, 1)
                if next1:
                    x_lo(c + 1, 1 - s)
                if next2:
                    statistics(c + 2, s)
                take_rest(it, s, 2)
                values(it, s, 0)
                take_rest(it, s, 3)
                for a in range(1, 4):
                    values(it, s, a)

            raw_stats(0, 0, 16)
            statistics(0, 0)
            normalise(0, 0, 16)
            dve.wait_ge(sem["w_hi"], 2)
            nc.vector.tensor_tensor(wqk_lo[:], wqk[:], wqk_hi[:], ALU.subtract).then_inc(sem["w_lo"], 1)
            nc.vector.tensor_tensor(wvr_lo[:], wvr[:], wvr_hi[:], ALU.subtract).then_inc(sem["w_lo"], 1)
            x_lo(0, 0)
            raw_stats(1, 1, 16)
            statistics(1, 1)
            dve.wait_ge(sem["sig_ready"], 1)
            nc.vector.tensor_scalar(sig[:, 1:2], sig[:, 0:1], 1.0, None, ALU.add).then_inc(sem["sig_ready"], 1)
            dve.wait_ge(sem["sig_ready"], 2)
            nc.vector.reciprocal(sig[:, 2:3], sig[:, 1:2]).then_inc(sem["sig_ready"], 1)
            dve.wait_ge(sem["ones_ready"], 1)
            with dve.Fori(0, NC // 2 - 1) as it:
                for s in range(2):
                    chunk(it, s)
            chunk(NC // 2 - 1, 0, next2=False)
            chunk(NC // 2 - 1, 1, next1=False, next2=False)

        @block.tensor
        def _(pe):
            for s in range(2):
                pe.sem_inc(sem["xn_stored"][s], 16)
                pe.sem_inc(sem["v_stored"][s], 16)
            pe.sem_inc(sem["xn_ready"], 2)
            for m in range(4):
                pe.sem_inc(sem["parts_stored"][m], 16)
            pe.sem_inc(sem["rest_ready"], 4)
            pe.sem_inc(sem["lo_ready"], 4)
            pe.sem_inc(sem["q32_ready"], 2)
            pe.sem_inc(sem["vr_used"], 2)
            pe.wait_ge(sem["ident_loaded"], 16)

            def x_T(c, s):
                pe.wait_ge(sem["xn_ready"], c + (2 + 1))
                for a in range(4):
                    for k in range(KT):
                        last = nc.tensor.transpose(tr[:, k, P * a:P * a + P],
                                                   xns[:, s, a, P * k:P * k + P], mem["ident"][:])
                last.then_inc(sem["tr_ready"], 1)

            def chunk(it, s, ahead):
                c = it * 2 + s
                pe.wait_ge(sem["xlo_ready"], c + 1)
                for m in range(4):
                    pe.wait_ge(sem["q32_ready"], it * 8 + (4 * s + m) + (2 - 1))
                    i = 0
                    for k in range(KT):
                        for w, x in ((wqk_hi, xhi), (wqk_hi, xlo), (wqk_lo, xhi)):
                            last = nc.tensor.matmul(qk[:, m % 2, :], w[:, k, P * m:P * m + P], x[:, s, k, :],
                                                    start=(i == 0), stop=(i == 3 * KT - 1))
                            i += 1
                    last.then_inc(sem["qk_ready"], 1)
                    if m == 1 and ahead:
                        x_T(c + 1, 1 - s)
                for a in range(4):
                    pe.wait_ge(sem["vr_used"], it * 8 + (4 * s + a) + (2 - 1))
                    i = 0
                    for k in range(KT):
                        for w, x in ((wvr_hi, xhi), (wvr_hi, xlo), (wvr_lo, xhi)):
                            last = nc.tensor.matmul(vr[:, a % 2, 0:D + E], x[:, s, k, P * a:P * a + P],
                                                    w[:, k, :], start=(i == 0), stop=(i == 3 * KT - 1))
                            i += 1
                    last.then_inc(sem["vr_ready"], 1)

            x_T(0, 0)
            pe.wait_ge(sem["w_lo"], 2)
            with pe.Fori(0, NC // 2 - 1) as it:
                for s in range(2):
                    chunk(it, s, True)
            chunk(NC // 2 - 1, 0, True)
            chunk(NC // 2 - 1, 1, False)


def bias_tables(mem):
    parts = mem["bias_dram"]
    loads = []
    for j in range(3):
        rows = slice(32 * j, 32 * j + 32)
        rise, fall = parts.offset + 2 * j * TBLEN, parts.offset + (2 * j + 1) * TBLEN
        for side, at in enumerate((rise, fall)):
            loads.append((mem["near"][rows, 4 * side:4 * side + 4, :],
                          bass.AP(parts.tensor, at + 96, [[1, 32], [-32, 4], [1, 256]])))
        for side, at in enumerate((TBLEN - 1, 0)):
            loads.append((mem["ends"][ROW_FAR + QT * j:ROW_FAR + QT * j + QT, side:side + 1],
                          bass.AP(parts.tensor, rise + at, [[0, QT], [1, 1]])))
    return loads


def load_stacks(nc, mem, sem, queue, u, buf):
    for stack, which, order in ((mem["qst"], 0, QPART), (mem["kst"], 1, KPART)):
        for g, part in enumerate(order):
            queue.dma_start(stack[HD * g:HD * g + HD, buf],
                            mem["qk_dram"][which, part, bass.ds(u * (HU * HD), HU * HD)]
                            .rearrange("(h d) t -> d h t", d=HD))\
                .then_inc(sem["stack_loaded"][buf], 16)
    queue.dma_start(mem["vst"][:, buf], mem["v_dram"][:, :, bass.ds(u, 1), :].rearrange("p a u w -> p a (u w)"))\
        .then_inc(sem["stack_loaded"][buf], 16)


def phase_route(nc, io, mem, sem):
    with ExitStack() as ctx:
        sb = lambda n, s, d: ctx.enter_context(nc.sbuf_tensor(n, s, d))
        ps = lambda n, s, d=FP32: ctx.enter_context(nc.psum_tensor(n, s, d))
        ends32 = sb("ends32", [P, 2], FP32)
        far = sb("far", [P, 2, T], FP32)
        far_bf = sb("far_bf", [P, T], BF16)
        lmax = sb("lmax", [P, NT], FP32)
        ex = sb("ex", [P, NT, E], FP32)
        ex2 = sb("ex2", [P, NT, E], FP32)
        ssum = sb("ssum", [P, NT], FP32)
        wsum = sb("wsum", [P, NT], FP32)
        best = sb("best", [P, NT, 8], FP32)
        besti = sb("besti", [P, NT, 8], U32)
        bestf = sb("bestf", [P, NT, 2], FP32)
        both = sb("both", [P, NT, E], BF16)
        ones = sb("ones", [P, P], BF16)
        psum_ex = ps("psum_ex", [P, 512])
        psum_tot = ps("psum_tot", [P, 512])
        block = ctx.enter_context(nc.Block())
        far_rows = slice(ROW_FAR, ROW_MAX)
        onehot = mem["onehot"]

        @block.sync
        def _(sp):
            for b in range(NBUF):
                sp.dma_start(mem["kst"][ROW_FAR:ROWS, b],
                             io["key_rows"].unsqueeze(1).to_broadcast([ROWS - ROW_FAR, HU, T]))\
                    .then_inc(sem["rows_set"], 16)
            sp.wait_ge(sem["far_ready"], 1)
            for b in range(NBUF):
                sp.dma_start(mem["qst"][far_rows, b], far_bf[far_rows].unsqueeze(1).to_broadcast([3 * QT, HU, T]))\
                    .then_inc(sem["rows_set"], 16)
            sp.wait_ge(sem["rows_set"], 16 * 2 * NBUF)

        @block.gpsimd
        def _(pool):
            pool.wait_ge(sem["far_begun"], 3)
            nc.gpsimd.tensor_tensor(far_bf[far_rows], far[far_rows, 0], far[far_rows, 1], ALU.add)\
                .then_inc(sem["far_ready"], 1)
            link, _ = linker(pool, sem["far_chain"])
            for i, slot in enumerate((0, 3)):
                link(nc.gpsimd.tensor_tensor(mem["near"][:, slot], mem["near"][:, slot], mem["near_mask"][:, i],
                                             ALU.mult))
            link(nc.gpsimd.memset(mem["zero"], 0.0))

        @block.scalar
        def _(act):
            act.wait_ge(sem["ex_ready"], 1)
            nc.scalar.activation(ex2[:], ex[:], ACT.Exp).then_inc(sem["exp_ready"], 1)
            nc.scalar.activation(ends32[far_rows], mem["ends"][far_rows], ACT.Copy).then_inc(sem["far_begun"], 1)
            act.wait_ge(sem["far_begun"], 1)
            for side in range(2):
                nc.scalar.activation(far[far_rows, side], mem["sides"][far_rows, side], ACT.Copy,
                                     scale=ends32[far_rows, side:side + 1]).then_inc(sem["far_begun"], 1)
            load_stacks(nc, mem, sem, act, 0, 0)
            act.wait_ge(sem["counts_ready"], 1)
            nc.scalar.activation(mem["in_tile"].rearrange("p t e -> p (t e)"), psum_ex[:, 0:NT * E], ACT.Copy)
            nc.scalar.activation(mem["tile_sum"].rearrange("p t e -> p (t e)"), psum_tot[:, 0:NT * E], ACT.Copy)\
                .then_inc(sem["sums_copied"], 1)
            act.wait_ge(sem["sums_copied"], 1)

        @block.tensor
        def _(pe):
            pe.wait_ge(sem["onehot_ready"], 1)
            pairs = both[:].rearrange("p t e -> p (t e)")
            nc.tensor.matmul(psum_ex[:, 0:NT * E], mem["tri"][:], pairs, start=True, stop=True)
            nc.tensor.matmul(psum_tot[:, 0:NT * E], ones[:], pairs, start=True, stop=True)\
                .then_inc(sem["counts_ready"], 1)

        @block.vector
        def _(dve):
            link, _ = linker(dve, sem["route_chain"])
            logits = mem["logits"]
            link(nc.vector.tensor_reduce(lmax[:], logits[:], AX.X, ALU.max))
            nc.vector.tensor_tensor(ex[:], logits[:], lmax[:].unsqueeze(2).to_broadcast([P, NT, E]), ALU.subtract)\
                .then_inc(sem["ex_ready"], 1)
            link(nc.vector.memset(ones[:], 1.0))
            dve.wait_ge(sem["exp_ready"], 1)
            link(nc.vector.tensor_reduce(ssum[:], ex2[:], AX.X, ALU.add))
            link(nc.vector.reciprocal(wsum[:], ssum[:]))
            link(nc.vector.tensor_tensor(ex[:], ex2[:], wsum[:].unsqueeze(2).to_broadcast([P, NT, E]), ALU.mult))
            for t in range(NT):
                last = nc.vector.max(best[:, t], ex[:, t])
            link(last)
            for t in range(NT):
                last = nc.vector.max_index(besti[:, t], best[:, t], ex[:, t])
            link(last)
            link(nc.vector.tensor_copy(bestf[:], besti[:, :, 0:2]))
            for k in range(TOPK):
                link(nc.vector.tensor_tensor(onehot[:, k], bestf[:, :, k:k + 1].to_broadcast([P, NT, E]),
                                             mem["iota8"][:].unsqueeze(1).to_broadcast([P, NT, E]), ALU.is_equal))
            nc.vector.tensor_tensor(both[:], onehot[:, 0], onehot[:, 1], ALU.add).then_inc(sem["onehot_ready"], 1)
            link(nc.vector.tensor_tensor(ssum[:], best[:, :, 0], best[:, :, 1], ALU.add))
            link(nc.vector.reciprocal(wsum[:], ssum[:]))
            for k in range(TOPK):
                link(nc.vector.tensor_tensor(mem["gate_w"][:, k, :], best[:, :, k], wsum[:], ALU.mult))


def positions(nc, mem, pool, chain):
    link, _ = linker(pool, chain)
    eng = nc.gpsimd
    tot, excl, count, ge, ntile = (mem[n] for n in ("tot", "excl", "count", "ge", "ntile"))
    src, a, d = mem["tile_sum"], 0, 1
    while d < NT:
        dst = tot[:, a]
        link(eng.tensor_copy(dst[:, 0:d], src[:, 0:d]))
        link(eng.tensor_tensor(dst[:, d:NT], src[:, d:NT], src[:, 0:NT - d], ALU.add))
        src, a, d = dst, 1 - a, 2 * d
    link(eng.tensor_copy(count[:], src[:, NT - 1]))
    link(eng.tensor_tensor(excl[:], src, mem["tile_sum"][:], ALU.subtract))
    link(eng.tensor_tensor(ge[:], count[:].unsqueeze(2).to_broadcast([P, E, NT]),
                           mem["steps"][:].unsqueeze(1).to_broadcast([P, E, NT]), ALU.subtract))
    link(eng.tensor_scalar(ge[:], ge[:], 0.0, 1.0, ALU.max, ALU.min))
    w = NT
    while w > 1:
        w //= 2
        link(eng.tensor_tensor(ge[:, :, 0:w], ge[:, :, 0:w], ge[:, :, w:2 * w], ALU.add))
    link(eng.tensor_copy(ntile[:, 0], ge[:, :, 0]))
    a, d = 0, 1
    while d < E:
        link(eng.tensor_copy(ntile[:, 1 - a, 0:d], ntile[:, a, 0:d]))
        link(eng.tensor_tensor(ntile[:, 1 - a, d:E], ntile[:, a, d:E], ntile[:, a, 0:E - d], ALU.add))
        a, d = 1 - a, 2 * d
    tile0 = mem["tile0"]
    link(eng.tensor_tensor(tile0[:], ntile[:, a], ge[:, :, 0], ALU.subtract))
    link(eng.tensor_scalar(tile0[:], tile0[:], float(P), None, ALU.mult))
    link(eng.tensor_tensor(excl[:], excl[:], mem["in_tile"][:], ALU.add))
    link(eng.tensor_tensor(excl[:], excl[:], tile0[:].unsqueeze(1).to_broadcast([P, NT, E]), ALU.add))
    for k in range(TOPK):
        own = mem["onehot"][:, k]
        link(eng.tensor_tensor(own, own, excl[:], ALU.mult))
        w = E
        while w > 1:
            w //= 2
            link(eng.tensor_tensor(own[:, :, 0:w], own[:, :, 0:w], own[:, :, w:2 * w], ALU.add))
        link(eng.tensor_copy(mem["pos"][:, k, :], own[:, :, 0]))
    past = mem["past"]
    link(eng.tensor_tensor(past[:], mem["tile_after"][:].unsqueeze(2).to_broadcast([1, NTILE, E]),
                           ntile[0:1, a, :].unsqueeze(1).to_broadcast([1, NTILE, E]), ALU.subtract))
    link(eng.tensor_scalar(past[:], past[:], 0.0, 1.0, ALU.max, ALU.min))
    w = E
    while w > 1:
        w //= 2
        link(eng.tensor_tensor(past[:, :, 0:w], past[:, :, 0:w], past[:, :, w:2 * w], ALU.add))
    link(eng.tensor_scalar(past[:, :, 0], past[:, :, 0], float(E - 1), None, ALU.min))
    link(eng.tensor_copy(mem["tile_expert"][:], past[:, :, 0]))


def near_queries(i, half):
    lo, hi = max(P * i - REACH, HALF * half), min(P * i + P + REACH, HALF * half + HALF)
    return lo - HALF * half, hi - lo, lo - (P * i - REACH)


def near_keys(j, half, group):
    start = P * (j - 1) if group < 2 else P * j
    lo, hi = max(start, HALF * half), min(start + 2 * P, HALF * half + HALF)
    return lo - HALF * half, hi - lo, lo - start


def load_tile(mem, sem, queue, t, s):
    queue.dma_start(mem["xs"][:, s, :], mem["xs_dram"][bass.ds(t * P, P), :]).then_inc(sem["xs_loaded"][s], 16)


def load_down(nc, io, mem, sem, queue):
    dn = mem["w_dn"].rearrange("p (e i d) -> p e i d", e=E, i=NI)
    queue.dma_start(dn[0:REM, :, NI - 1, :], io["w_dn"][:, (NI - 1) * P:I, :].rearrange("e p d -> p e d"))\
        .then_inc(sem["dn_loaded"], 16)
    for i in range(NI - 1):
        queue.dma_start(dn[:, :, i, :], io["w_dn"][:, i * P:i * P + P, :].rearrange("e p d -> p e d"))\
            .then_inc(sem["dn_loaded"], 16)


def phase_attention(nc, io, mem, sem):
    with ExitStack() as ctx:
        sb = lambda n, s, d: ctx.enter_context(nc.sbuf_tensor(n, s, d))
        ps = lambda n, s, d=FP32: ctx.enter_context(nc.psum_tensor(n, s, d))
        qst, kst, vst, near, anti = (mem[n] for n in ("qst", "kst", "vst", "near", "anti"))
        probs = sb("probs", [P, 2, HU, HALF], FP32)
        rowmax = sb("rowmax", [P, HU, QT, 2], FP32)
        negmax = sb("negmax", [P, HU, QT], FP32)
        maxrest = sb("maxrest", [P, HU, QT], FP32)
        maxparts = sb("maxparts", [P, 3, HU, QT], BF16)
        maxT = sb("maxT", [3 * HU * QT, P], BF16)
        ctxu = sb("ctxu", [P, 2, HALF], FP32)
        recip = sb("recip", [P, 2, 4, HU], FP32)
        ctxn = sb("ctxn", [P, 2, 4, HU, HD], FP32)
        sc = ps("sc", [P, 4, HALF])
        sm = ps("sm", [P, 2, HALF])
        pv = ps("pv", [P, HALF])
        misc = ps("misc", [P, HALF])
        miscbf = misc[:].bitcast(BF16)
        block = ctx.enter_context(nc.Block())
        LOADS = 2 * NPAIR + 1
        MAXT_STEP = 13
        ROUNDS = (NU - 2) // NBUF

        @block.sync
        def _(sp):
            def max_rows(count, buf):
                sp.wait_ge(sem["maxT_ready"], count)
                sp.dma_start(qst[ROW_MAX:ROWS, buf].rearrange("p h (j q) -> p (h j) q", q=P),
                             maxT[:]).then_inc(sem["max_rows"][buf], 16)

            def store_ctx(u, half):
                sp.wait_ge(sem["ctxn_ready"], u * 2 + (1 + half + 1))
                for h in range(HU):
                    sp.dma_start(mem["ctx_dram"][bass.ds(u, 1), h, HALF * half:HALF * half + HALF, :]
                                 .rearrange("u (a p) d -> (u p) a d", p=P),
                                 ctxn[:, half, :, h, :]).then_inc(sem["ctx_stored"][half], 16)

            load_stacks(nc, mem, sem, sp, 1, 1)
            max_rows(1, 0)

            def unit(u, r, more):
                sp.wait_ge(sem["ctxT_ready"], u * 2 + 2)
                if more:
                    load_stacks(nc, mem, sem, sp, u + 2, (r + 2) % NBUF)
                store_ctx(u, 0)
                max_rows(u + 2, (r + 1) % NBUF)
                store_ctx(u, 1)

            with sp.Fori(0, ROUNDS) as it:
                for r in range(NBUF):
                    unit(it * NBUF + r, r, True)
            for u in range(NBUF * ROUNDS, NU - 1):
                unit(u, u % NBUF, u + 2 < NU)
            sp.wait_ge(sem["ctxT_ready"], 2 * (NU - 1) + 2)
            load_down(nc, io, mem, sem, sp)
            sp.wait_ge(sem["scattered"], 16 * TOPK * NT)
            for s in range(2):
                load_tile(mem, sem, sp, s, s)
            store_ctx(NU - 1, 0)
            store_ctx(NU - 1, 1)
            sp.wait_ge(sem["dn_loaded"], 16 * NI)
            for s in range(2):
                sp.wait_ge(sem["xs_loaded"][s], 16)
            for half in range(2):
                sp.wait_ge(sem["ctx_stored"][half], 64 + 64 * NU)

        @block.gpsimd
        def _(pool):
            xs = mem["xs_dram"].rearrange("(c a p) d -> c p a d", a=4, p=P)
            for c in range(NPOS // (4 * P)):
                pool.dma_start(xs[c], mem["zero"]).then_inc(sem["zeroed"], 16)
                pool.wait_ge(sem["zeroed"], 16 * c + 16)
            pool.dma_start(mem["ids_dram"], io["spare_rows"]).then_inc(sem["ids_set"], 16)
            positions(nc, mem, pool, sem["position_chain"])
            pool.wait_ge(sem["ids_set"], 16)
            for k in range(TOPK):
                for t in range(NT):
                    pool.indirect_dma_start(mem["xs_dram"], bass.IndirectOffsetOnAxis(
                        ap=mem["pos"][:, k, t:t + 1], axis=0), mem["xn"][:, t, :], None)\
                        .then_inc(sem["scattered"], 16)
                    pool.indirect_dma_start(mem["ids_dram"], bass.IndirectOffsetOnAxis(
                        ap=mem["pos"][:, k, t:t + 1], axis=0), mem["token_rows"][:, k, t:t + 1], None)\
                        .then_inc(sem["ids_scattered"], 16)
            pool.wait_ge(sem["scattered"], 16 * TOPK * NT)
            pool.wait_ge(sem["ids_scattered"], 16 * TOPK * NT)
            pool.dma_start(mem["row_of"][:], mem["ids_dram"][0:NTILE * P].rearrange("(t p) o -> p (t o)", p=P),
                           allow_slow_non_contiguous=True)\
                .then_inc(sem["rows_loaded"], 16)
            for e in range(2 * E):
                part = slice(e * KT * GUW // 2, (e + 1) * KT * GUW // 2)
                pool.dma_start(mem["w_gu"][:, part], io["w_gu"][:, part]).then_inc(sem["gu_loaded"], 16)
                pool.wait_ge(sem["gu_loaded"], 16 * e + 16)
            pool.wait_ge(sem["rows_loaded"], 16)

        def bank_pair(n):
            return (sm[:, 0:2], sc[:, 0:2], sc[:, 2:4])[n % 3]

        def pe_max(pe, base, n, buf, first=False):
            h, j, half = n // (2 * QT), n // 2 % QT, n % 2
            if first:
                bank = bank_pair(n // 2)[:, half]
                if n >= 6:
                    pe.wait_ge(sem["max_taken"], n // 2 * 2 - 4)
            else:
                bank = sm[:, n % 2]
                pe.wait_ge(sem["max_taken"], base + (n - 1))
            parts = [(g, *near_keys(j, half, g)) for g in range(4)]
            parts = [x for x in parts if x[2] > 0]
            last = nc.tensor.matmul(bank, qst[0:ROW_MAX, buf, h, P * j:P * j + P],
                                    kst[0:ROW_MAX, buf, h, HALF * half:HALF * half + HALF],
                                    start=True, stop=not parts, skip_group_check=True)
            for g, at, width, col in parts:
                last = nc.tensor.matmul(bank[32 * g:32 * g + 32, at:at + width], anti[0:96, :],
                                        near[0:96, (g + 2) % 4, col:col + width], start=False, stop=True,
                                        skip_group_check=True)
            last.then_inc(sem["max_scores"], 1)

        def pe_maxT(pe, count):
            pe.wait_ge(sem["maxparts_ready"], count)
            nc.tensor.transpose(miscbf[0:3 * HU * QT, 0:P], maxparts[:].rearrange("p c h j -> p (c h j)"),
                                mem["ident_bf"][:]).then_inc(sem["maxT_done"], 1)

        def pe_scores(pe, base, step, buf, h):
            half, i = step // QT, step % QT
            at, width, col = near_queries(i, half)
            if h % 2 == 0:
                pe.wait_ge(sem["probs_ready"], base + (2 + 2 * step + h // 2 - 1))
            last = nc.tensor.matmul(sc[:, h, :], kst[0:ROWS, buf, h, P * i:P * i + P],
                                    qst[0:ROWS, buf, h, HALF * half:HALF * half + HALF],
                                    start=True, stop=width <= 0, skip_group_check=True)
            if width > 0:
                for g in range(4):
                    last = nc.tensor.matmul(sc[32 * g:32 * g + 32, h, at:at + width], anti[0:96, :],
                                            near[0:96, 4 + g, col:col + width], start=False, stop=True,
                                            skip_group_check=True)
            if h % 2:
                last.then_inc(sem["scores_ready"], 1)

        def pe_values(pe, base, u, step, buf):
            half, i = step // QT, step % QT
            pe.wait_ge(sem["probs_ready"], base + (2 + 2 * step + 2))
            if i == 0:
                pe.wait_ge(sem["ctxu_ready"], u * 2 + (1 + half))
            for h in range(HU):
                last = nc.tensor.matmul(pv[32 * h:32 * h + 32, :], vst[:, buf, i, 32 * h:32 * h + 32],
                                        probs[:, step % 2, h, :], start=(i == 0), stop=(i == QT - 1),
                                        skip_group_check=True)
            last.then_inc(sem["values_added"], 1)

        def pe_ctxT(pe, u, half):
            pe.wait_ge(sem["ctxu_ready"], u * 2 + (1 + half + 1))
            if half == 0:
                pe.wait_ge(sem["ctxn_ready"], u * 2 + 1)
            else:
                pe.wait_ge(sem["ctxn_ready"], u * 2 + (1 + 1))
            for a in range(4):
                last = nc.tensor.transpose(misc[:, P * a:P * a + P], ctxu[:, half, P * a:P * a + P], mem["ident"][:])
            last.then_inc(sem["ctxT_ready"], 1)

        @block.tensor
        def _(pe):
            pe.sem_inc(sem["probs_ready"], 2)
            pe.sem_inc(sem["values_added"], 2)
            pe.sem_inc(sem["ctxT_ready"], 2)
            pe.sem_inc(sem["ctxu_ready"], 1)
            pe.sem_inc(sem["ctxn_ready"], 1)
            for half in range(2):
                pe.sem_inc(sem["ctx_stored"][half], 64)

            def ring(it, r, ahead, each):
                return (it + (r + ahead) // NBUF) * each + each

            def step_work(u, step, buf, n, max_base, max_buf, maxT=None):
                base = u * (2 * STEPS)
                for h in range(HU):
                    pe_scores(pe, base, step, buf, h)
                    if n < MAXIMA:
                        pe_max(pe, max_base, n, max_buf)
                        n += 1
                    if h == 3 and maxT is not None:
                        pe_maxT(pe, maxT)
                return n

            def head(u, r, it, more):
                first = isinstance(u, int) and u == 0
                n = 0 if more and not first else MAXIMA
                pe.wait_ge(sem["max_rows"][r % NBUF], ring(it, r, 0, 16))
                if more:
                    pe.wait_ge(sem["stack_loaded"][(r + 1) % NBUF], ring(it, r, 1, 16 * LOADS))
                max_base, max_buf = u * MAXIMA + MAXIMA, (r + 1) % NBUF
                for step in range(2):
                    n = step_work(u, step, r % NBUF, n, max_base, max_buf)
                    if step == 0 and not first:
                        pe_values(pe, (u - 1) * (2 * STEPS), u - 1, STEPS - 1, (r - 1) % NBUF)
                    if step == 1:
                        if not first:
                            pe.wait_ge(sem["maxT_ready"], u + 1)
                            pe_ctxT(pe, u - 1, 1)
                        pe_values(pe, u * (2 * STEPS), u, 0, r % NBUF)
                    if n < MAXIMA:
                        pe_max(pe, max_base, n, max_buf)
                        n += 1

            def rest(u, r, ahead):
                n = 2 * (HU + 1) if ahead else MAXIMA
                max_base, max_buf = u * MAXIMA + MAXIMA, (r + 1) % NBUF
                for step in range(2, STEPS):
                    n = step_work(u, step, r, n, max_base, max_buf, u + 2 if step == MAXT_STEP and ahead else None)
                    pe_values(pe, u * (2 * STEPS), u, step - 1, r)
                    if n < MAXIMA:
                        pe_max(pe, max_base, n, max_buf)
                        n += 1
                    if step == 10:
                        pe_ctxT(pe, u, 0)

            pe.wait_ge(sem["stack_loaded"][0], 16 * LOADS)
            for n in range(MAXIMA):
                pe_max(pe, 0, n, 0, first=True)
            pe.wait_ge(sem["stack_loaded"][1], 16 * LOADS)
            for n in range(2 * (HU + 1)):
                pe_max(pe, MAXIMA, n, 1)
                if n == 1:
                    pe_maxT(pe, 1)
            head(0, 0, 0, True)
            with pe.Fori(0, ROUNDS) as it:
                for r in range(NBUF):
                    rest(it * NBUF + r, r, True)
                    head(it * NBUF + (r + 1), r + 1, it, True)
            for u in range(NBUF * ROUNDS, NU):
                rest(u, u % NBUF, u + 1 < NU)
                if u + 1 < NU:
                    head(u + 1, (u + 1) % NBUF, (u + 1) // NBUF, u + 2 < NU)
            pe_values(pe, (NU - 1) * (2 * STEPS), NU - 1, STEPS - 1, (NU - 1) % NBUF)
            pe_ctxT(pe, NU - 1, 1)

        @block.scalar
        def _(act):
            def copy_maxT(count):
                act.wait_ge(sem["maxT_done"], count)
                nc.scalar.activation(maxT[:], miscbf[0:3 * HU * QT, 0:P], ACT.Copy).then_inc(sem["maxT_ready"], 1)

            def copy_ctx(u, half):
                act.wait_ge(sem["values_added"], u * STEPS + (2 + QT * (half + 1)))
                nc.scalar.activation(ctxu[:, half, :], pv[:], ACT.Copy).then_inc(sem["ctxu_ready"], 1)

            def exps(u, step, maxT=None):
                for pair in range(2):
                    act.wait_ge(sem["scores_ready"], u * (2 * STEPS) + (2 * step + pair + 1))
                    if pair == 0:
                        act.wait_ge(sem["values_added"], u * STEPS + (2 + step - 1))
                    nc.scalar.activation(probs[:, step % 2, 2 * pair:2 * pair + 2, :],
                                         sc[:, 2 * pair:2 * pair + 2, :], ACT.Exp, scale=1.0 / SCALE_INV)\
                        .then_inc(sem["probs_ready"], 1)
                    if pair == 1 and maxT is not None:
                        copy_maxT(maxT)

            def rest(u, ahead):
                for step in range(2, STEPS):
                    exps(u, step, u + 2 if step == MAXT_STEP and ahead else None)
                    if step == QT:
                        copy_ctx(u, 0)

            def head(u):
                exps(u, 0)
                copy_ctx(u - 1, 1)
                exps(u, 1)

            copy_maxT(1)
            exps(0, 0)
            exps(0, 1)
            with act.Fori(0, ROUNDS) as it:
                for r in range(NBUF):
                    rest(it * NBUF + r, True)
                    head(it * NBUF + (r + 1))
            for u in range(NBUF * ROUNDS, NU):
                rest(u, u + 1 < NU)
                if u + 1 < NU:
                    head(u + 1)
            copy_ctx(NU - 1, 1)

        @block.vector
        def _(dve):
            def take_max(base, n):
                h, j, half = n // (2 * QT), n // 2 % QT, n % 2
                dve.wait_ge(sem["max_scores"], base + (n + 1))
                nc.vector.tensor_reduce(rowmax[:, h, j, half:half + 1], sm[:, n % 2, :], AX.X, ALU.max)\
                    .then_inc(sem["max_taken"], 1)

            def split_max(base, links):
                dve.wait_ge(sem["max_taken"], base + MAXIMA)
                link, made = linker(dve, sem["max_chain"], links)
                link(nc.vector.tensor_reduce(negmax[:], rowmax[:], AX.X, ALU.max, negate=True))
                split3_last(link)
                return made[0]

            def split3_last(link):
                hi, mid, lo = (maxparts[:, j] for j in range(3))
                link(nc.vector.tensor_copy(hi, negmax[:]))
                link(nc.vector.tensor_tensor(maxrest[:], negmax[:], hi, ALU.subtract))
                link(nc.vector.tensor_copy(mid, maxrest[:]))
                nc.vector.tensor_tensor(lo, maxrest[:], mid, ALU.subtract).then_inc(sem["maxparts_ready"], 1)

            def normalise(u, half):
                dve.wait_ge(sem["ctxT_ready"], u * 2 + (2 + half + 1))
                dve.wait_ge(sem["ctx_stored"][half], u * (16 * 4) + 64)
                m = misc[:].rearrange("p (a h w) -> p a h w", a=4, w=VW)
                nc.vector.reciprocal(recip[:, half], m[:, :, :, HD]).then_inc(sem["recip_ready"], 1)
                dve.wait_ge(sem["recip_ready"], u * 2 + (half + 1))
                nc.vector.tensor_tensor(ctxn[:, half], m[:, :, :, 0:HD],
                                        recip[:, half].unsqueeze(3).to_broadcast([P, 4, HU, HD]),
                                        ALU.mult).then_inc(sem["ctxn_ready"], 1)

            LINKS = 4
            HEAD = 2 * (HU + 1)

            def rest(u, ahead):
                if ahead:
                    for n in range(HEAD, MAXIMA):
                        take_max(u * MAXIMA + MAXIMA, n)
                        if n == 60:
                            normalise(u, 0)
                    made = split_max(u * MAXIMA + MAXIMA, u * LINKS + LINKS)
                    assert made == LINKS
                else:
                    normalise(u, 0)

            def head(u, more):
                if more:
                    for n in range(HEAD):
                        take_max(u * MAXIMA + MAXIMA, n)
                normalise(u - 1, 1)

            for n in range(MAXIMA // 2):
                dve.wait_ge(sem["max_scores"], 2 * n + 2)
                nc.vector.tensor_reduce(rowmax[:, n // QT, n % QT, :], bank_pair(n), AX.X, ALU.max)\
                    .then_inc(sem["max_taken"], 2)
            split_max(0, 0)
            for n in range(HEAD):
                take_max(MAXIMA, n)
            with dve.Fori(0, ROUNDS) as it:
                for r in range(NBUF):
                    rest(it * NBUF + r, True)
                    head(it * NBUF + (r + 1), True)
            for u in range(NBUF * ROUNDS, NU):
                rest(u, u + 1 < NU)
                if u + 1 < NU:
                    head(u + 1, u + 2 < NU)
            normalise(NU - 1, 1)


def phase_experts(nc, io, mem, sem):
    with ExitStack() as ctx:
        sb = lambda n, s, d: ctx.enter_context(nc.sbuf_tensor(n, s, d))
        ps = lambda n, s, d=FP32: ctx.enter_context(nc.psum_tensor(n, s, d))
        w_gu, w_dn = mem["w_gu"], mem["w_dn"]
        xs = mem["xs"]
        xsT = sb("xsT", [P, 2, KT, P], FP32)
        silu = sb("silu", [P, 2, IC], FP32)
        hid = sb("hid", [P, 2, I], FP32)
        hidT = sb("hidT", [P, NI, P], FP32)
        ys = sb("ys", [P, 2, D], FP32)
        gu = ps("gu", [P, 4, HALF])
        xt = ps("xt", [P, HALF])
        ht = ps("ht", [P, 8, P])
        yp = ps("yp", [P, HALF])
        block = ctx.enter_context(nc.Block())
        PAIRS = (NTILE - 2) // 2

        @block.sync
        def _(sp):
            def load(t, s):
                load_tile(mem, sem, sp, t, s)

            sp.wait_ge(sem["xT_done"], 1)
            load(2, 0)
            with sp.Fori(0, PAIRS - 1) as it:
                for r in range(2):
                    t = it * 2 + (r + 1)
                    sp.wait_ge(sem["xT_done"], t + 1)
                    load(t + 2, (r + 1) % 2)
            for t in range(2 * PAIRS - 1, NTILE + 1):
                if t + 2 < NTILE:
                    sp.wait_ge(sem["xT_done"], t + 1)
                    load(t + 2, t % 2)

        @block.gpsimd
        def _(pool):
            for t in range(NTILE):
                pool.wait_ge(sem["y_ready"], t + 1)
                pool.indirect_dma_start(mem["y_dram"], bass.IndirectOffsetOnAxis(
                    ap=mem["row_of"][:, t:t + 1], axis=0), ys[:, t % 2, :], None).then_inc(sem["y_stored"], 16)
                pool.wait_ge(sem["y_stored"], 16 * t + 16)
                pool.sem_inc(sem["ys_free"], 1)

        @block.tensor
        def _(pe):
            def x_T(s, loaded):
                pe.wait_ge(sem["xs_loaded"][s], loaded)
                for k in range(KT):
                    last = nc.tensor.transpose(xt[:, P * k:P * k + P], xs[:, s, P * k:P * k + P], mem["ident"][:])
                last.then_inc(sem["xT_done"], 1)

            def expert(t):
                return pe.value_load(mem["tile_expert"][0:1, bass.ds(t, 1)], min_val=0, max_val=E - 1)

            def gate_up(t, s, e, first=False):
                pe.wait_ge(sem["xsT_ready"], t + 1)
                for j in range(2):
                    if not first:
                        pe.wait_ge(sem["hid_ready"], t * 2 + (j - 1))
                    for which in range(2):
                        for k in range(KT):
                            last = nc.tensor.matmul(
                                gu[:, 2 * j + which, 0:IC], xsT[:, s, k, :],
                                w_gu[:, bass.ds(e * (KT * GUW) + (k * GUW + which * I + j * IC), IC)],
                                start=(k == 0), stop=(k == KT - 1))
                    last.then_inc(sem["gate_up"], 1)

            def h_T(t, s):
                pe.wait_ge(sem["hid_ready"], t * 2 + 2)
                for i in range(NI):
                    w = min(P, I - P * i)
                    last = nc.tensor.transpose(ht[0:w, i, :], hid[:, s, P * i:P * i + w], mem["ident"][:])
                last.then_inc(sem["hT_done"], 1)

            def down(t, e, first=False):
                pe.wait_ge(sem["hidT_lo"], t + 1)
                pe.wait_ge(sem["hidT_hi"], t + 1)
                if not first:
                    pe.wait_ge(sem["y_ready"], t)
                for i in range(NI):
                    w = min(P, I - P * i)
                    last = nc.tensor.matmul(yp[:, 0:D], hidT[0:w, i, :],
                                            w_dn[0:w, bass.ds(e * (NI * D) + i * D, D)],
                                            start=(i == 0), stop=(i == NI - 1))
                last.then_inc(sem["y_done"], 1)

            pe.sem_inc(sem["ys_free"], 2)
            x_T(0, 16)
            gate_up(0, 0, expert(0), first=True)
            x_T(1, 16)
            with pe.Fori(0, PAIRS) as it:
                for r in range(2):
                    t = it * 2 + (r + 1)
                    s = (r + 1) % 2
                    h_T(t - 1, r)
                    gate_up(t, s, expert(t))
                    x_T(r, it * 16 + 32)
                    down(t - 1, expert(t - 1))
            for t in range(2 * PAIRS + 1, NTILE):
                h_T(t - 1, (t - 1) % 2)
                gate_up(t, t % 2, expert(t))
                if t + 1 < NTILE:
                    x_T((t + 1) % 2, 16 * ((t + 1) // 2 + 1))
                down(t - 1, expert(t - 1))
            h_T(NTILE - 1, (NTILE - 1) % 2)
            down(NTILE - 1, expert(NTILE - 1))

        @block.scalar
        def _(act):
            def copy_xT(t, s):
                act.wait_ge(sem["xT_done"], t + 1)
                nc.scalar.activation(xsT[:, s], xt[:, 0:KT * P].rearrange("p (k t) -> p k t", k=KT), ACT.Copy)\
                    .then_inc(sem["xsT_ready"], 1)

            def gate(t, first=False):
                for j in range(2):
                    act.wait_ge(sem["gate_up"], t * 2 + (j + 1))
                    if not first:
                        act.wait_ge(sem["hid_ready"], t * 2 + (j - 1))
                    nc.scalar.activation(silu[:, j, :], gu[:, 2 * j, 0:IC], ACT.Silu).then_inc(sem["silu_ready"], 1)

            def copy_hT(t):
                act.wait_ge(sem["hT_done"], t + 1)
                nc.scalar.activation(hidT[:, 4, :], ht[:, 4, :], ACT.Copy)
                nc.scalar.activation(hidT[0:REM, 5, :], ht[0:REM, 5, :], ACT.Copy).then_inc(sem["hidT_hi"], 1)

            def copy_y(t, s):
                act.wait_ge(sem["y_done"], t + 1)
                act.wait_ge(sem["ys_free"], t + 1)
                nc.scalar.activation(ys[:, s, :], yp[:, 0:D], ACT.Copy).then_inc(sem["y_ready"], 1)

            copy_xT(0, 0)
            gate(0, first=True)
            copy_xT(1, 1)
            with act.Fori(0, PAIRS) as it:
                for r in range(2):
                    t = it * 2 + (r + 1)
                    copy_hT(t - 1)
                    gate(t)
                    copy_xT(t + 1, r)
                    copy_y(t - 1, r)
            for t in range(2 * PAIRS + 1, NTILE):
                copy_hT(t - 1)
                gate(t)
                if t + 1 < NTILE:
                    copy_xT(t + 1, (t + 1) % 2)
                copy_y(t - 1, (t - 1) % 2)
            copy_hT(NTILE - 1)
            copy_y(NTILE - 1, (NTILE - 1) % 2)

        @block.vector
        def _(dve):
            def copy_hT(t):
                dve.wait_ge(sem["hT_done"], t + 1)
                nc.vector.tensor_copy(hidT[:, 0:4, :], ht[:, 0:4, :]).then_inc(sem["hidT_lo"], 1)

            def hidden(t, s):
                for j in range(2):
                    dve.wait_ge(sem["silu_ready"], t * 2 + (j + 1))
                    nc.vector.tensor_tensor(hid[:, s, j * IC:j * IC + IC], silu[:, j, :], gu[:, 2 * j + 1, 0:IC],
                                            ALU.mult).then_inc(sem["hid_ready"], 1)

            hidden(0, 0)
            with dve.Fori(0, PAIRS) as it:
                for r in range(2):
                    t = it * 2 + (r + 1)
                    copy_hT(t - 1)
                    hidden(t, (r + 1) % 2)
            for t in range(2 * PAIRS + 1, NTILE):
                copy_hT(t - 1)
                hidden(t, t % 2)
            copy_hT(NTILE - 1)


def phase_combine(nc, io, mem, sem, out):
    with ExitStack() as ctx:
        sb = lambda n, s, d: ctx.enter_context(nc.sbuf_tensor(n, s, d))
        ps = lambda n, s, d=FP32: ctx.enter_context(nc.psum_tensor(n, s, d))
        PAIRS = QT // 2
        wo = sb("wo", [P, KT, D], FP32)
        wo_hi = sb("wo_hi", [P, KT, D], FP32R)
        wo_lo = sb("wo_lo", [P, KT, D], FP32R)
        bo = sb("bo", [P, D], FP32)
        xin = sb("xin", [P, QT, D], FP32)
        cin = sb("cin", [P, QT, D], FP32)
        yin = sb("yin", [P, QT, TOPK, D], FP32)
        chi = sb("chi", [P, 2, KT, P], FP32R)
        clo = sb("clo", [P, 2, KT, P], FP32R)
        xb = sb("xb", [P, QT, D], FP32)
        acc = sb("acc", [P, 2, 2, 2, D], FP32)
        res = sb("res", [P, QT, D], FP32)
        ct = ps("ct", [P, 2, HALF])
        op = ps("op", [P, 4, HALF])
        x_rows = io["x"].rearrange("(n p) d -> p n d", p=P)
        y_rows = mem["y_dram"][0:TOPK * NTOK].rearrange("(n p) d -> p n d", p=P)
        out_rows = out.rearrange("(n p) d -> p n d", p=P)
        ctx_rows = mem["ctx_dram"].rearrange("(s b g) h (r q) d -> g b h s r (q d)", s=2, b=2, q=HD)
        block = ctx.enter_context(nc.Block())

        @block.sync
        def _(sp):
            sp.dma_start(wo[:], io["w_o"]).then_inc(sem["wo_loaded"], 16)

            def load(g, j):
                pair = slice(2 * j, 2 * j + 2)
                for b in range(2):
                    sp.dma_start(cin[64 * b:64 * b + 64, pair, :],
                                 ctx_rows[bass.ds(g, 1), b, j].rearrange("u s r c -> r (u s) c"))\
                        .then_inc(sem["in_loaded"][j], 16)
                sp.dma_start(xin[:, pair, :], x_rows[:, bass.ds(g * QT + 2 * j, 2), :])\
                    .then_inc(sem["in_loaded"][j], 16)

            def store(g, j):
                sp.wait_ge(sem["res_ready"], g * QT + (2 * j + 2))
                sp.dma_start(out_rows[:, bass.ds(g * QT + 2 * j, 2), :], res[:, 2 * j:2 * j + 2, :])\
                    .then_inc(sem["out_stored"][j], 16)

            for j in range(PAIRS):
                load(0, j)
            with sp.Fori(0, GU - 1) as g:
                for j in range(PAIRS):
                    store(g, j)
                    load(g + 1, j)
            for j in range(PAIRS):
                store(GU - 1, j)
            for j in range(PAIRS):
                sp.wait_ge(sem["out_stored"][j], 16 + 16 * GU)

        @block.gpsimd
        def _(pool):
            def load(pair):
                j = pair % PAIRS
                if pair >= PAIRS:
                    pool.wait_ge(sem["res_ready"], 2 * (pair - PAIRS) + 2)
                for k in range(TOPK):
                    pool.dma_start(yin[:, 2 * j:2 * j + 2, k, :],
                                   y_rows[:, k * NT + 2 * pair:k * NT + 2 * pair + 2, :])\
                        .then_inc(sem["y_loaded"][j], 16)

            for pair in range(PAIRS - 1):
                load(pair)
            pool.wait_ge(sem["bo_loaded"], 16)
            for pair in range(NT // 2):
                j = pair % PAIRS
                pool.wait_ge(sem["in_loaded"][j], 48 * (pair // PAIRS) + 48)
                nc.gpsimd.tensor_tensor(xb[:, 2 * j:2 * j + 2, :], xin[:, 2 * j:2 * j + 2, :],
                                        bo[:].unsqueeze(1).to_broadcast([P, 2, D]), ALU.add)\
                    .then_inc(sem["x_added"], 1)
                if pair + PAIRS - 1 < NT // 2:
                    load(pair + PAIRS - 1)

        @block.tensor
        def _(pe):
            pe.sem_inc(sem["proj_used"], 4)
            pe.sem_inc(sem["proj_done"], 2)
            for j in range(PAIRS):
                pe.sem_inc(sem["out_stored"][j], 16)

            def transposes(g, tt):
                pe.wait_ge(sem["in_loaded"][tt // 2], g * 48 + 48)
                for k in range(KT):
                    last = nc.tensor.transpose(ct[:, tt % 2, P * k:P * k + P], cin[:, tt, P * k:P * k + P],
                                               mem["ident"][:])
                last.then_inc(sem["ct_done"], 1)

            def product(g, tt):
                t = g * QT + tt
                pe.wait_ge(sem["proj_used"], t + 1)
                pe.wait_ge(sem["clo_ready"], t + 1)
                i = 0
                for k in range(KT):
                    for c, w in ((chi, wo_hi), (clo, wo_hi), (chi, wo_lo)):
                        last = nc.tensor.matmul(op[:, tt % 4, 0:D], c[:, tt % 2, k, :], w[:, k, :],
                                                start=(i == 0), stop=(i == 3 * KT - 1))
                        i += 1
                last.then_inc(sem["proj_done"], 1)

            transposes(0, 0)
            pe.wait_ge(sem["wo_split"], 2)
            with pe.Fori(0, GU - 1) as g:
                for tt in range(QT):
                    if tt < QT - 1:
                        transposes(g, tt + 1)
                    else:
                        transposes(g + 1, 0)
                    product(g, tt)
            for tt in range(QT):
                if tt < QT - 1:
                    transposes(GU - 1, tt + 1)
                product(GU - 1, tt)

        @block.scalar
        def _(act):
            act.dma_start(bo[:], io["b_o"].partition_broadcast(P)).then_inc(sem["bo_loaded"], 16)
            act.wait_ge(sem["wo_loaded"], 16)
            nc.scalar.activation(wo_hi[:], wo[:], ACT.Copy).then_inc(sem["wo_split"], 1)

            with act.Fori(0, GU) as g:
                for tt in range(QT):
                    t = g * QT + tt
                    act.wait_ge(sem["proj_done"], t + 1)
                    act.wait_ge(sem["ct_done"], t + 1)
                    nc.scalar.activation(chi[:, tt % 2], ct[:, tt % 2, 0:KT * P].rearrange("p (k t) -> p k t", k=KT),
                                         ACT.Copy).then_inc(sem["chi_ready"], 1)

        @block.vector
        def _(dve):
            def split(g, tt):
                t = g * QT + tt
                dve.wait_ge(sem["chi_ready"], t + 1)
                nc.vector.tensor_tensor(clo[:, tt % 2], ct[:, tt % 2, 0:KT * P].rearrange("p (k t) -> p k t", k=KT),
                                        chi[:, tt % 2], ALU.subtract).then_inc(sem["clo_ready"], 1)

            def sums(g, j):
                t, s = g * QT + 2 * j, j % 2
                pair = g * PAIRS + j
                dve.wait_ge(sem["x_added"], pair + 1)
                dve.wait_ge(sem["proj_done"], t + (2 + 2))
                nc.vector.tensor_tensor(acc[:, s, 0], xb[:, 2 * j:2 * j + 2, :],
                                        op[:, 2 * j % 4:2 * j % 4 + 2, 0:D], ALU.add).then_inc(sem["proj_used"], 2)
                dve.wait_ge(sem["proj_used"], t + (4 + 2))
                dve.wait_ge(sem["y_loaded"][j], g * 32 + 32)
                for i in range(2):
                    nc.vector.scalar_tensor_tensor(out=acc[:, s, 1, i], in0=yin[:, 2 * j + i, 0, :],
                                                   scalar=mem["gate_w"][:, 0, bass.ds(t + i, 1)],
                                                   in1=acc[:, s, 0, i], op0=ALU.mult, op1=ALU.add)\
                        .then_inc(sem["y_added"], 1)
                dve.wait_ge(sem["out_stored"][j], g * 16 + 16)
                for i in range(2):
                    dve.wait_ge(sem["y_added"], t + (i + 1))
                    nc.vector.scalar_tensor_tensor(out=res[:, 2 * j + i, :], in0=yin[:, 2 * j + i, 1, :],
                                                   scalar=mem["gate_w"][:, 1, bass.ds(t + i, 1)],
                                                   in1=acc[:, s, 1, i], op0=ALU.mult, op1=ALU.add)\
                        .then_inc(sem["res_ready"], 1)

            dve.wait_ge(sem["wo_split"], 1)
            nc.vector.tensor_tensor(wo_lo[:], wo[:], wo_hi[:], ALU.subtract).then_inc(sem["wo_split"], 1)
            for tt in range(2):
                split(0, tt)
            with dve.Fori(0, GU - 1) as g:
                for j in range(PAIRS):
                    for tt in range(2 * j + 2, 2 * j + 4):
                        split(g + tt // QT, tt % QT)
                    sums(g, j)
            for j in range(PAIRS):
                for tt in range(2 * j + 2, 2 * j + 4):
                    if tt < QT:
                        split(GU - 1, tt)
                sums(GU - 1, j)


SEMS = """ident_loaded weights w_hi w_lo ones_ready xn_ready rest_ready lo_ready q32_ready vr_used var_ready std_ready
tr_ready xhi_ready xlo_ready qk_ready hi_ready mid_ready vr_ready stats_chain root_chain gates_loaded
bias_loaded bias_chain bias_stored sig_ready tables rows_set ids_set ids_scattered rows_loaded far_ready
far_begun far_chain zeroed ex_ready exp_ready onehot_ready counts_ready sums_copied route_chain
position_chain scattered gu_loaded max_scores max_taken maxparts_ready maxT_done maxT_ready scores_ready
probs_ready values_added ctxu_ready ctxT_ready ctxn_ready recip_ready max_chain dn_loaded xT_done xsT_ready
gate_up silu_ready hid_ready hT_done hidT_lo hidT_hi y_done y_ready y_stored ys_free wo_loaded bo_loaded
wo_split ct_done chi_ready clo_ready proj_done proj_used x_added y_added res_ready""".split()
SEM_RINGS = {"x_loaded": 2, "xn_stored": 2, "parts_stored": 4, "v_stored": 2, "stack_loaded": NBUF, "max_rows": NBUF,
             "ctx_stored": 2, "xs_loaded": 2, "in_loaded": 4, "y_loaded": QT // 2, "out_stored": 4}


def build(nc, io, out):
    with ExitStack() as ctx:
        sb = lambda n, s, d: ctx.enter_context(nc.sbuf_tensor(n, s, d))
        dram = lambda n, s, d: nc.dram_tensor(n, s, d, kind="Internal").ap()
        sem = {n: ctx.enter_context(nc.semaphore(n)) for n in SEMS}
        for n, k in SEM_RINGS.items():
            sem[n] = [ctx.enter_context(nc.semaphore(f"{n}{i}")) for i in range(k)]
        mem = {
            "qk_dram": dram("qk_dram", (2, 3, NU * HU * HD, T), BF16),
            "v_dram": dram("v_dram", (P, QT, NU, P), FP32),
            "ctx_dram": dram("ctx_dram", (NU, HU, T, HD), FP32),
            "xs_dram": dram("xs_dram", (NPOS, D), FP32),
            "bias_dram": dram("bias_dram", (3, 2, TBLEN), BF16),
            "ids_dram": dram("ids_dram", (NPOS, 1), I32),
            "y_dram": dram("y_dram", (TOPK * NTOK + NPOS, D), FP32),
            "ident": sb("ident", [P, P], FP32),
            "pos": sb("pos", [P, TOPK, NT], I32),
            "gate_w": sb("gate_w", [P, TOPK, NT], FP32),
            "xs": sb("xs", [P, 2, D], FP32),
            "row_of": sb("row_of", [P, NTILE], I32),
            "tile_expert": sb("tile_expert", [1, NTILE], I32),
            "logits": sb("logits", [P, NT, E], FP32),
            "w_gu": sb("w_gu", [P, E * KT * GUW], FP32),
        }
        at = 0
        for n, shape, letters in (("xn", [NT, D], "a b"), ("zero", [4, D], "a b"), ("onehot", [TOPK, NT, E], "a b c"),
                                  ("in_tile", [NT, E], "a b"), ("tile_sum", [NT, E], "a b"),
                                  ("tot", [2, NT, E], "a b c"), ("excl", [NT, E], "a b"), ("ge", [E, NT], "a b")):
            size = int(np.prod(shape))
            mem[n] = mem["w_gu"][:, at:at + size].rearrange(f"p ({letters}) -> p {letters}",
                                                            **dict(zip(letters.split()[1:], shape[1:])))
            at += size
        mem["token_rows"] = mem["w_gu"][:, at:at + TOPK * NT].bitcast(I32).rearrange("p (k t) -> p k t", k=TOPK)
        with ExitStack() as shared:
            def keep(tensors):
                for n, s, d in tensors:
                    mem[n] = shared.enter_context(nc.sbuf_tensor(n, s, d))

            keep([("near", [96, 8, 256], BF16), ("near_mask", [96, 2, 256], BF16), ("anti", [96, 32], BF16),
                  ("ident_bf", [P, P], BF16), ("tri", [P, P], BF16), ("sides", [P, 2, T], BF16),
                  ("ends", [P, 2], BF16), ("iota8", [P, E], FP32), ("steps", [P, NT], FP32),
                  ("tile_after", [1, NTILE], FP32)])
            phase_project(nc, io, mem, sem)
            keep([("vst", [P, NBUF, QT, P], FP32),
                  ("count", [P, E], FP32), ("ntile", [P, 2, E], FP32), ("tile0", [P, E], FP32),
                  ("past", [1, NTILE, E], FP32), ("stacks", [P, 2 * (HU * T + E * NI * D)], BF16)])
            stacks = mem["stacks"][:, 0:NBUF * 2 * HU * T].rearrange("p (b w h t) -> p b w h t", b=NBUF, w=2, h=HU)
            mem["qst"], mem["kst"] = stacks[:, :, 0], stacks[:, :, 1]
            mem["w_dn"] = mem["stacks"][:, 2 * HU * T:].bitcast(FP32)
            phase_route(nc, io, mem, sem)
            phase_attention(nc, io, mem, sem)
            phase_experts(nc, io, mem, sem)
        phase_combine(nc, io, mem, sem, out)


def constants():
    def bf16_bits(ones):
        return np.where(ones != 0, 0x3F80, 0).astype(np.uint16)

    c = {}
    c["ident"] = np.eye(P, dtype=np.float32)
    c["ident_bf"] = bf16_bits(np.eye(P))
    c["anti"] = bf16_bits(np.tile(np.eye(32)[::-1], (3, 1)))
    c["tri"] = bf16_bits(np.triu(np.ones((P, P)), 1))
    c["iota8"] = np.tile(np.arange(E, dtype=np.float32), (P, 1))
    c["steps"] = np.tile(np.arange(NT, dtype=np.float32) * P, (P, 1))
    c["tile_after"] = np.arange(1, NTILE + 1, dtype=np.float32)[None]
    c["token_rows"] = np.arange(TOPK * NTOK, dtype=np.int32).reshape(TOPK, NT, P).transpose(2, 0, 1).copy()
    c["spare_rows"] = np.arange(TOPK * NTOK, TOPK * NTOK + NPOS, dtype=np.int32)[:, None]
    t = np.arange(T)
    rows = np.zeros((ROWS - ROW_FAR, T), np.float32)
    sides = np.zeros((3 * QT, 2, T), np.float32)
    for p in range(3):
        for i in range(QT):
            rows[QT * p + i] = (t // P == i)
            sides[QT * p + i, 0] = t < P * i - REACH
            sides[QT * p + i, 1] = t >= P * i + P + REACH
    rows[3 * QT:] = 1
    c["key_rows"] = bf16_bits(rows)
    c["sides"] = bf16_bits(sides)
    mask = np.ones((3, 32, 2, 256), np.float32)
    mask[:, 30:32, 0, P:] = 0
    mask[:, 0:2, 1, 0:P] = 0
    c["near_mask"] = bf16_bits(mask.reshape(96, 2, 256))
    return c


def kernel(L0_attn_x, L0_attn_Wq, L0_attn_bq, L0_attn_Wk, L0_attn_bk, L0_attn_Wv, L0_attn_bv, L0_attn_Wo,
           L0_attn_bo, L0_attn_et_gate, L0_attn_is_gate, L0_attn_time_bias, L0_ffn_w_router, L0_ffn_w_gate,
           L0_ffn_w_up, L0_ffn_w_down):
    import concourse.bacc as bacc
    from concourse.bass_utils import run_bass_kernel_spmd

    a = np.asarray
    tiles = lambda w: np.ascontiguousarray(w.reshape(KT, P, -1).transpose(1, 0, 2))
    tb = a(L0_attn_time_bias).reshape(TB)
    arrays = dict(constants())
    arrays["x"] = np.ascontiguousarray(a(L0_attn_x).reshape(NTOK, D))
    arrays["w_qk"] = tiles(np.concatenate([a(L0_attn_Wq).T, a(L0_attn_Wk).T], axis=1))
    arrays["w_vr"] = tiles(np.concatenate([a(L0_attn_Wv).T, a(L0_ffn_w_router).T], axis=1))
    arrays["w_o"] = tiles(a(L0_attn_Wo).T)
    arrays["b_qk"] = np.ascontiguousarray(np.concatenate([a(L0_attn_bq), a(L0_attn_bk)]).reshape(4, P).T)
    arrays["b_v"] = a(L0_attn_bv).reshape(1, D)
    arrays["b_o"] = a(L0_attn_bo).reshape(1, D)
    arrays["et_gate"] = a(L0_attn_et_gate).reshape(1, 1)
    arrays["is_gate"] = a(L0_attn_is_gate).reshape(1, 1)
    arrays["time_bias"] = np.stack([np.pad(tb, (129, TBLEN - 129 - TB), mode="edge"),
                                    np.pad(tb[::-1], (127, TBLEN - 127 - TB), mode="edge")])
    gu = np.concatenate([a(L0_ffn_w_gate), a(L0_ffn_w_up)], axis=1).transpose(0, 2, 1)
    arrays["w_gu"] = np.ascontiguousarray(gu.reshape(E, KT, P, GUW).transpose(2, 0, 1, 3).reshape(P, -1))
    arrays["w_dn"] = np.ascontiguousarray(a(L0_ffn_w_down).transpose(0, 2, 1))

    nc = bacc.Bacc("TRN2", target_bir_lowering=False, num_devices=1)
    io = {n: nc.dram_tensor(n + "_in", v.shape, mybir.dt.from_np(v.dtype), kind="ExternalInput").ap()
          for n, v in arrays.items()}
    for n, v in arrays.items():
        if v.dtype == np.uint16:
            io[n] = io[n].bitcast(BF16)
    out = nc.dram_tensor("out", (NTOK, D), FP32, kind="ExternalOutput").ap()
    build(nc, io, out)
    r = run_bass_kernel_spmd(nc, [{n + "_in": v for n, v in arrays.items()}], core_ids=[0])
    return r.results[0]["out"].reshape(B, T, D)
```
